# Optimizing a Trainium2 kernel written in Bass

```python
import numpy as np
import jax
import jax.numpy as jnp

def _softmax(x, axis=-1):
    return jax.nn.softmax(x, axis=axis)

def _gelu(x):
    return jax.nn.gelu(x, approximate=True)

def _silu(x):
    return jax.nn.silu(x)

def _sigmoid(x):
    return jax.nn.sigmoid(x)

def _layernorm(x, axis=-1, eps=1e-05):
    m = jnp.mean(x, axis=axis, keepdims=True)
    v = jnp.var(x, axis=axis, keepdims=True)
    return (x - m) / jnp.sqrt(v + eps)

def _scatter_add(tgt, idx, src, axis=0):
    return tgt.at[idx].add(src)

def _segment_sum(src, seg, n):
    return jax.ops.segment_sum(src, seg, n)
kernel_name = 'mk_gnn_resnorm_d4_gnn_r32_529ff7'

def setup_inputs(seed: int=0):
    np.random.seed(seed)
    _w = jnp.asarray

    def _rec_inputs():
        import jax
        import jax.numpy as jnp
        _gk = jax.random.key(seed)
        x = -0.0002117 + 1 * jax.random.normal(jax.random.fold_in(_gk, 1), (3125, 256), jnp.float32)
        src = jax.random.randint(jax.random.fold_in(_gk, 2), (50000,), 0, 3125, jnp.int32)
        dst = jnp.minimum((3125 * jax.random.uniform(jax.random.fold_in(_gk, 3), (50000,)) ** 2.0).astype(jnp.int32), 99999)
        _o = jnp.argsort(dst, stable=True)
        src = src[_o]
        dst = dst[_o]
        edge_type_16 = jax.random.randint(jax.random.fold_in(_gk, 13), (50000,), 0, 16, jnp.int32)
        edge_weight1 = jax.random.uniform(jax.random.fold_in(_gk, 14), (50000, 1), jnp.float32, 0.0, 0.999998)
        return (x, src, dst, edge_type_16, edge_weight1)
    x, src, dst, edge_type_16, edge_weight1 = _rec_inputs()

    def _L0_gnn_setup():
        import jax, jax.numpy as jnp
        import numpy as np
        N_NODES = 3125
        N_EDGES = 100000
        D_FEAT = 256
        LEAKY_ALPHA = 0.2
        key = jax.random.key(seed)
        k1, k2, k3 = jax.random.split(key, 3)
        x = jax.random.normal(k1, (N_NODES, D_FEAT), dtype=jnp.float32)
        edge_index = jax.random.randint(k2, (2, N_EDGES), 0, N_NODES, dtype=jnp.int32)
        W = jax.random.normal(k3, (D_FEAT, D_FEAT), dtype=jnp.float32) * (1.0 / np.sqrt(D_FEAT))
        b = jnp.zeros((D_FEAT,), dtype=jnp.float32)
        return {'x': x, 'edge_index': edge_index, 'W': W, 'b': b}
    _L0_gnn_all = _L0_gnn_setup()
    _L0_gnn_in = {k: v for k, v in _L0_gnn_all.items() if k in ('W', 'b')}
    del _L0_gnn_all

    def _L1_gnn_setup():
        import jax, jax.numpy as jnp
        import numpy as np
        N_NODES = 50000
        N_EDGES = 25000
        IN_DIM = 256
        OUT_DIM = 32
        NUM_HEADS = 8
        key = jax.random.key(seed)
        ks = jax.random.split(key, 9)
        h = jax.random.normal(ks[0], (N_NODES, IN_DIM), dtype=jnp.float32)
        src = jax.random.randint(ks[1], (N_EDGES,), 0, N_NODES, dtype=jnp.int32)
        dst = jax.random.randint(ks[2], (N_EDGES,), 0, N_NODES, dtype=jnp.int32)
        s = 1.0 / np.sqrt(IN_DIM)
        W_lin = jax.random.uniform(ks[3], (IN_DIM, IN_DIM), jnp.float32, -s, s)
        b_lin = jax.random.uniform(ks[4], (IN_DIM,), jnp.float32, -s, s)
        W_gat = jax.random.normal(ks[5], (IN_DIM, NUM_HEADS * OUT_DIM), dtype=jnp.float32) * s
        attn_l = jax.random.normal(ks[6], (NUM_HEADS, OUT_DIM), dtype=jnp.float32) * 0.1
        attn_r = jax.random.normal(ks[7], (NUM_HEADS, OUT_DIM), dtype=jnp.float32) * 0.1
        gat_bias = jnp.zeros((NUM_HEADS * OUT_DIM,), dtype=jnp.float32)
        return {'h': h, 'src': src, 'dst': dst, 'W_lin': W_lin, 'b_lin': b_lin, 'W_gat': W_gat, 'attn_l': attn_l, 'attn_r': attn_r, 'gat_bias': gat_bias}
    _L1_gnn_all = _L1_gnn_setup()
    _L1_gnn_in = {k: v for k, v in _L1_gnn_all.items() if k in ('W_lin', 'b_lin', 'W_gat', 'attn_l', 'attn_r', 'gat_bias')}
    del _L1_gnn_all

    def _L2_gnn_setup():
        import jax, jax.numpy as jnp
        import numpy as np
        N_NODES = 10000
        N_EDGES = 10000
        D = 256
        L = 3
        BN_EPS = 1e-05

        def _segment_softmax(logits, seg, num_segments):
            m = jax.ops.segment_max(logits, seg, num_segments=num_segments)
            e = jnp.exp(logits - m[seg])
            s = jax.ops.segment_sum(e, seg, num_segments=num_segments)
            return e / s[seg]
        key = jax.random.key(seed)
        ks = jax.random.split(key, 20)
        scale = 1.0 / np.sqrt(D)
        inp = {'x': jax.random.normal(ks[0], (N_NODES, D), dtype=jnp.float32), 'edge_index': jax.random.randint(ks[1], (2, N_EDGES), 0, N_NODES, dtype=jnp.int64), 'Wq': jax.random.normal(ks[2], (D, D), jnp.float32) * scale, 'bq': jnp.zeros((D,), jnp.float32), 'Wk': jax.random.normal(ks[3], (D, D), jnp.float32) * scale, 'bk': jnp.zeros((D,), jnp.float32), 'Wv': jax.random.normal(ks[4], (D, D), jnp.float32) * scale, 'bv': jnp.zeros((D,), jnp.float32), 'Ws': jax.random.normal(ks[5], (D, D), jnp.float32) * scale, 'bs': jnp.zeros((D,), jnp.float32), 'Wl': jax.random.normal(ks[6], (L, D, D), jnp.float32) * scale, 'bl': jnp.zeros((L, D), jnp.float32), 'Wr': jax.random.normal(ks[7], (L, D, D), jnp.float32) * scale, 'gamma': jnp.ones((L, D), jnp.float32) + 0.1 * jax.random.normal(ks[8], (L, D), jnp.float32), 'beta': 0.1 * jax.random.normal(ks[9], (L, D), jnp.float32), 'alpha_res': jnp.asarray(0.5, jnp.float32)}
        return inp
    _L2_gnn_all = _L2_gnn_setup()
    _L2_gnn_in = {k: v for k, v in _L2_gnn_all.items() if k in ('Wq', 'bq', 'Wk', 'bk', 'Wv', 'bv', 'Ws', 'bs', 'Wl', 'bl', 'Wr', 'gamma', 'beta', 'alpha_res')}
    del _L2_gnn_all

    def _L3_gnn_setup():
        import jax, jax.numpy as jnp
        import numpy as np
        N_NODES = 625
        N_EDGES = 10000
        NUM_RELS = 16
        IN_FEAT = 256
        OUT_FEAT = 256
        key = jax.random.key(seed)
        k_h, k_w, k_n, k_s, k_d, k_r = jax.random.split(key, 6)
        h = jax.random.normal(k_h, (N_NODES, IN_FEAT), dtype=jnp.float32)
        weight = jax.random.normal(k_w, (NUM_RELS, IN_FEAT, OUT_FEAT), dtype=jnp.float32)
        norm = jax.random.uniform(k_n, (N_EDGES, 1), dtype=jnp.float32)
        src = jax.random.randint(k_s, (N_EDGES,), 0, N_NODES, dtype=jnp.int32)
        dst = jax.random.randint(k_d, (N_EDGES,), 0, N_NODES, dtype=jnp.int32)
        rel_type = jax.random.randint(k_r, (N_EDGES,), 0, NUM_RELS, dtype=jnp.int32)
        return {'h': h, 'weight': weight, 'norm': norm, 'src': src, 'dst': dst, 'rel_type': rel_type}
    _L3_gnn_all = _L3_gnn_setup()
    _L3_gnn_in = {k: v for k, v in _L3_gnn_all.items() if k in ('weight',)}
    del _L3_gnn_all
    return {'x': x, 'src': src, 'dst': dst, 'edge_type_16': edge_type_16, 'edge_weight1': edge_weight1, 'L0_gnn_W': _L0_gnn_in['W'], 'L0_gnn_b': _L0_gnn_in['b'], 'L1_gnn_W_lin': _L1_gnn_in['W_lin'], 'L1_gnn_b_lin': _L1_gnn_in['b_lin'], 'L1_gnn_W_gat': _L1_gnn_in['W_gat'], 'L1_gnn_attn_l': _L1_gnn_in['attn_l'], 'L1_gnn_attn_r': _L1_gnn_in['attn_r'], 'L1_gnn_gat_bias': _L1_gnn_in['gat_bias'], 'L2_gnn_Wq': _L2_gnn_in['Wq'], 'L2_gnn_bq': _L2_gnn_in['bq'], 'L2_gnn_Wk': _L2_gnn_in['Wk'], 'L2_gnn_bk': _L2_gnn_in['bk'], 'L2_gnn_Wv': _L2_gnn_in['Wv'], 'L2_gnn_bv': _L2_gnn_in['bv'], 'L2_gnn_Ws': _L2_gnn_in['Ws'], 'L2_gnn_bs': _L2_gnn_in['bs'], 'L2_gnn_Wl': _L2_gnn_in['Wl'], 'L2_gnn_bl': _L2_gnn_in['bl'], 'L2_gnn_Wr': _L2_gnn_in['Wr'], 'L2_gnn_gamma': _L2_gnn_in['gamma'], 'L2_gnn_beta': _L2_gnn_in['beta'], 'L2_gnn_alpha_res': _L2_gnn_in['alpha_res'], 'L3_gnn_weight': _L3_gnn_in['weight']}

def reference(x, src, dst, edge_type_16, edge_weight1, L0_gnn_W, L0_gnn_b, L1_gnn_W_lin, L1_gnn_b_lin, L1_gnn_W_gat, L1_gnn_attn_l, L1_gnn_attn_r, L1_gnn_gat_bias, L2_gnn_Wq, L2_gnn_bq, L2_gnn_Wk, L2_gnn_bk, L2_gnn_Wv, L2_gnn_bv, L2_gnn_Ws, L2_gnn_bs, L2_gnn_Wl, L2_gnn_bl, L2_gnn_Wr, L2_gnn_gamma, L2_gnn_beta, L2_gnn_alpha_res, L3_gnn_weight):
    import jax
    import jax.numpy as jnp

    def _L0_gnn_ref(x, edge_index, W, b):
        import jax, jax.numpy as jnp
        import numpy as np
        N_NODES = 3125
        N_EDGES = 100000
        D_FEAT = 256
        LEAKY_ALPHA = 0.2
        N = x.shape[0]
        row = edge_index[0]
        col = edge_index[1]
        ones = jnp.ones(row.shape[0], dtype=x.dtype)
        deg = jax.ops.segment_sum(ones, row, num_segments=N)
        deg_safe = jnp.where(deg > 0, deg, 1.0)
        dinv_sqrt = jnp.where(deg > 0, jax.lax.rsqrt(deg_safe), 0.0)
        w = dinv_sqrt[row] * dinv_sqrt[col]
        h = jax.ops.segment_sum(w[:, None] * x[col], row, num_segments=N)
        h = h @ W + b
        return jnp.where(h >= 0, h, LEAKY_ALPHA * h)

    def _L1_gnn_ref(h, src, dst, W_lin, b_lin, W_gat, attn_l, attn_r, gat_bias):
        import jax, jax.numpy as jnp
        import numpy as np
        N_NODES = 50000
        N_EDGES = 25000
        IN_DIM = 256
        OUT_DIM = 32
        NUM_HEADS = 8
        N = h.shape[0]
        h = h @ W_lin + b_lin
        h_in = h
        feat = (h @ W_gat).reshape(N, NUM_HEADS, OUT_DIM)
        el = jnp.sum(feat * attn_l, axis=-1)
        er = jnp.sum(feat * attn_r, axis=-1)
        e = jax.nn.leaky_relu(el[src] + er[dst], 0.2)
        m = jax.ops.segment_max(e, dst, num_segments=N)
        m = jnp.where(jnp.isfinite(m), m, 0.0)
        e = jnp.exp(e - m[dst])
        s = jax.ops.segment_sum(e, dst, num_segments=N)
        a = e / s[dst]
        msg = feat[src] * a[:, :, None]
        out = jax.ops.segment_sum(msg, dst, num_segments=N)
        out = out.reshape(N, NUM_HEADS * OUT_DIM) + gat_bias
        out = jax.nn.leaky_relu(out, 0.01)
        return h_in + out

    def _L2_gnn_ref(x, edge_index, Wq, bq, Wk, bk, Wv, bv, Ws, bs, Wl, bl, Wr, gamma, beta, alpha_res):
        import jax, jax.numpy as jnp
        import numpy as np
        N_NODES = 10000
        N_EDGES = 10000
        D = 256
        L = 3
        BN_EPS = 1e-05

        def _segment_softmax(logits, seg, num_segments):
            m = jax.ops.segment_max(logits, seg, num_segments=num_segments)
            e = jnp.exp(logits - m[seg])
            s = jax.ops.segment_sum(e, seg, num_segments=num_segments)
            return e / s[seg]
        src, dst = (edge_index[0], edge_index[1])
        n, d = x.shape
        q = x @ Wq + bq
        k = x @ Wk + bk
        v = x @ Wv + bv
        logits = jnp.sum(q[dst] * k[src], axis=-1) / jnp.sqrt(jnp.asarray(d, x.dtype))
        attn = _segment_softmax(logits, dst, n)
        agg = jax.ops.segment_sum(attn[:, None] * v[src], dst, num_segments=n)
        h = agg + x @ Ws + bs
        h = jax.nn.relu(h)
        deg = jax.ops.segment_sum(jnp.ones((src.shape[0],), x.dtype), dst, num_segments=n)
        deg = jnp.maximum(deg, 1.0)[:, None]
        prev = h
        bn_scale = 1.0 / jnp.sqrt(1.0 + BN_EPS)
        al = jax.nn.sigmoid(alpha_res)
        for i in range(Wl.shape[0]):
            mean_nb = jax.ops.segment_sum(h[src], dst, num_segments=n) / deg
            z = mean_nb @ Wl[i] + bl[i] + h @ Wr[i]
            z = z * bn_scale * gamma[i] + beta[i]
            z = al * z + (1.0 - al) * prev
            h = jax.nn.relu(z)
            prev = h
        return h

    def _L3_gnn_ref(h, weight, norm, src, dst, rel_type):
        import jax, jax.numpy as jnp
        import numpy as np
        N_NODES = 625
        N_EDGES = 10000
        NUM_RELS = 16
        IN_FEAT = 256
        OUT_FEAT = 256
        transformed = jnp.einsum('ni,rio->rno', h, weight)
        msg = transformed[rel_type, src] * norm
        out = jax.ops.segment_sum(msg, dst, num_segments=h.shape[0])
        return out
    edge_index = jnp.stack([src, dst])
    x = _layernorm(x + _L0_gnn_ref(x, edge_index, L0_gnn_W, L0_gnn_b), axis=-1)
    x = _layernorm(x + _L1_gnn_ref(x, src, dst, L1_gnn_W_lin, L1_gnn_b_lin, L1_gnn_W_gat, L1_gnn_attn_l, L1_gnn_attn_r, L1_gnn_gat_bias), axis=-1)
    x = _layernorm(x + _L2_gnn_ref(x, edge_index, L2_gnn_Wq, L2_gnn_bq, L2_gnn_Wk, L2_gnn_bk, L2_gnn_Wv, L2_gnn_bv, L2_gnn_Ws, L2_gnn_bs, L2_gnn_Wl, L2_gnn_bl, L2_gnn_Wr, L2_gnn_gamma, L2_gnn_beta, L2_gnn_alpha_res), axis=-1)
    x = _layernorm(x + _L3_gnn_ref(x, L3_gnn_weight, edge_weight1, src, dst, edge_type_16), axis=-1)
    return x

_drawn_inputs = setup_inputs


def setup_inputs(seed=0):
    import zlib

    import numpy as np

    out = dict(_drawn_inputs(seed))
    spreads = {'L0_gnn_b': (0.0, 0.1),
     'L1_gnn_gat_bias': (0.0, 0.1),
     'L2_gnn_bq': (0.0, 0.8),
     'L2_gnn_bk': (0.0, 0.8),
     'L2_gnn_bv': (0.0, 0.329),
     'L2_gnn_bs': (0.0, 0.327),
     'L2_gnn_bl': (0.0, 0.1)}
    factors = {'L1_gnn_attn_r': 5.949}
    for name, (base, spread) in spreads.items():
        noise = np.random.default_rng([zlib.crc32(name.encode()), seed]).standard_normal(out[name].shape)
        drawn = base * np.exp(spread * noise) if base else spread * noise
        out[name] = jnp.asarray(drawn.astype(out[name].dtype))
    for name, factor in factors.items():
        out[name] = (out[name] * factor).astype(out[name].dtype)
    return out
```

```python
from contextlib import ExitStack

import numpy as np
import concourse.bass as bass
from concourse import mybir

F32 = mybir.dt.float32
BF16 = mybir.dt.bfloat16
I32 = mybir.dt.int32
ALU = mybir.AluOpType
ACT = mybir.ActivationFunctionType
AX = mybir.AxisListType

P = 128
N = 3125
D = 256
E = 50000
H = 8
HD = D // H
R = 16
T = (N + P - 1) // P
NP = T * P
NLAST = N - (T - 1) * P
EP = 125
EC = E // EP
U = 16
IT = -(-(E // P + T) // U)
S = IT * U
SE = S * P
SG = 4
SQ = S // SG
RING = 8
G4 = 4
CH = 4
NTRASH = NP
BIG = 1.0e30
PAD_DST = float(1 << 20)
LN_EPS = 1e-5
BN_SCALE = 1.0 / float(np.sqrt(1.0 + 1e-5))


class Bag:
    pass


class Order:

    def __init__(self, eng, sem, base=0):
        self.eng, self.sem, self.n = eng, sem, base

    def __call__(self, ins):
        ins.then_inc(self.sem, 1)
        self.n = self.n + 1
        self.eng.wait_ge(self.sem, self.n)


def cols(ap, start, count):
    return ap[:, bass.ds(start, count)]


def tile_of(ap, t):
    return ap[:, bass.ds(t, 1), :].rearrange("p a f -> p (a f)")


def over_tiles(eng, body):
    with eng.Fori(0, T // 2) as i:
        body(2 * i, 0)
        body(2 * i + 1, 1)
    body(T - 1, 0)


def over_tiles_after_two(eng, body):
    body(0, 0)
    body(1, 1)
    with eng.Fori(1, T // 2) as i:
        body(2 * i, 0)
        body(2 * i + 1, 1)
    body(T - 1, 0)


def reused(t):
    return not isinstance(t, int) or t >= 2


def spread(ap, p=P):
    return bass.AP(ap.tensor, ap.offset, [[0, p]] + [list(x) for x in ap.ap])



def prepare(nc, k, x, src, dst):
    with ExitStack() as c:
        c.enter_context(nc.cleanup_on_exit())
        sb = lambda n, s, d=F32: c.enter_context(nc.sbuf_tensor("p_" + n, s, d))
        sem = lambda n: nc.alloc_semaphore("p_" + n)
        dn = sb("dn", [EP, EC], I32)
        nxt = sb("nxt", [EP, 1], I32)
        sn = sb("sn", [EP, EC], I32)
        bits = sb("bits", [EP, EC], I32)
        dtile = sb("dtile", [EP, EC])
        slo = sb("slo", [EP, EC])
        shi = sb("shi", [EP, EC])
        junk = sb("junk", [EP, EC])
        junk2 = sb("junk2", [EP, EC])
        per = sb("per", [EP, T + 2])
        lob = sb("lob", [EP, 8, P], BF16)
        hib = sb("hib", [EP, 8, T], BF16)
        zed = sb("zed", [EP, P], BF16)
        iob = sb("iob", [P, P], BF16)
        row = sb("row", [1, 8, T + 2])
        rowi = sb("rowi", [1, 2, T + 2], I32)
        ends = sb("ends", [T, 1])
        ioj = sb("ioj", [T, S + 1])
        cmpj = sb("cmpj", [T, S + 1])
        ends_all = sb("ends_all", [T, T])
        dg = sb("dg", [T, T])
        hist = c.enter_context(nc.psum_tensor("hist", [P, 512], F32))
        small = c.enter_context(nc.psum_tensor("small", [P, 512], F32))
        mapp = c.enter_context(nc.psum_tensor("mapp", [P, 512], F32))
        x_in, e_in, zeroed = sem("x_in"), sem("e_in"), sem("zeroed")
        made, vstep, pstep = sem("made"), sem("vstep"), sem("pstep")
        hot, used, counted, cleared = sem("hot"), sem("used"), sem("counted"), sem("cleared")
        sums, rowed, mapped = sem("sums"), sem("rowed"), sem("mapped")
        block = c.enter_context(nc.Block())

        @block.sync
        def _(sp):
            sp.dma_start(sn[:], src.rearrange("(p c) -> p c", c=EC)).then_inc(e_in, 16)
            sp.dma_start(dn[:], dst.rearrange("(p c) -> p c", c=EC)).then_inc(e_in, 16)
            sp.wait_ge(zeroed, 1)
            sp.dma_start(nxt[0:EP - 1, :], dst.rearrange("(p c) -> p c", c=EC)[1:EP, 0:1],
                         allow_slow_non_contiguous=True).then_inc(e_in, 16)
            sp.dma_start(k.X[:, 0:T - 1, :], x[0:(T - 1) * P, :].rearrange("(t p) f -> p t f", p=P)).then_inc(x_in, 16)
            sp.wait_ge(zeroed, 2)
            sp.dma_start(k.X[0:NLAST, T - 1, :], x[(T - 1) * P:N, :]).then_inc(x_in, 16)
            sp.wait_ge(x_in, 32)

        @block.gpsimd
        def _(pool):
            step = Order(pool, pstep)
            pool.memset(nxt[:], NP).then_inc(zeroed, 1)
            pool.memset(k.X[:, T - 1, :], 0.0).then_inc(zeroed, 1)
            pool.iota(k.iota[:], [[1, P]], base=0, channel_multiplier=0,
                      allow_small_or_imprecise_dtypes=True).then_inc(made, 1)
            pool.iota(iob[:], [[1, P]], base=0, channel_multiplier=0,
                      allow_small_or_imprecise_dtypes=True).then_inc(made, 1)
            pool.iota(k.pcol[:], [[1, 1]], base=0, channel_multiplier=1,
                      allow_small_or_imprecise_dtypes=True).then_inc(made, 1)
            pool.iota(ioj[:], [[1, S + 1]], base=-1, channel_multiplier=0,
                      allow_small_or_imprecise_dtypes=True).then_inc(made, 1)
            pool.memset(k.ones[:], 1.0).then_inc(made, 1)
            pool.memset(zed[:], 0.0).then_inc(made, 1)
            pool.memset(k.zero[:], 0.0).then_inc(made, 1)
            step(pool.memset(k.ident[:], 0.0))
            pool.affine_select(out=k.ident[:], in_=k.ident[:], compare_op=ALU.not_equal, fill=1.0, base=0,
                               pattern=[[-1, P]], channel_multiplier=1).then_inc(made, 1)

        @block.vector
        def _(dve):
            step = Order(dve, vstep)
            dve.wait_ge(made, 8)
            dve.tensor_scalar(k.low[:], k.iota[:], k.pcol[:, 0:1], None, ALU.is_lt).then_inc(vstep, 1)
            dve.memset(per[:], 0.0).then_inc(vstep, 1)
            step.n = 2
            dve.wait_ge(vstep, 2)
            dve.wait_ge(e_in, 48)
            step(dve.tensor_single_scalar(bits[:], sn[:], P - 1, ALU.bitwise_and))
            step(dve.tensor_copy(slo[:], bits[:]))
            step(dve.tensor_single_scalar(bits[:], sn[:], 7, ALU.arith_shift_right))
            step(dve.tensor_copy(shi[:], bits[:]))
            dve.sem_inc(used, 1)
            with dve.Fori(0, EC // 8) as i:
                dve.wait_ge(used, i + 1)
                for u in range(8):
                    dve.tensor_scalar(lob[:, u, :], iob[0:EP, :], cols(slo, i * 8 + u, 1), None,
                                      ALU.is_equal).then_inc(hot, 1)
                    dve.tensor_scalar(hib[:, u, :], iob[0:EP, 0:T], cols(shi, i * 8 + u, 1), None,
                                      ALU.is_equal).then_inc(hot, 1)
            step(dve.tensor_single_scalar(bits[:], dn[:], 7, ALU.arith_shift_right))
            step(dve.tensor_copy(dtile[:], bits[:]))
            for t in range(T):
                step(dve.tensor_scalar(junk[:], dtile[:], float(t), 0.0, ALU.is_equal, ALU.add,
                                       accum_out=per[:, t:t + 1]))
            step(dve.tensor_tensor(junk2[:, 0:EC - 1], dn[:, 1:EC], dn[:, 0:EC - 1], ALU.is_lt))
            step(dve.tensor_tensor(junk2[:, EC - 1:EC], nxt[:], dn[:, EC - 1:EC], ALU.is_lt))
            step(dve.tensor_reduce(per[:, T:T + 1], junk2[:], AX.X, ALU.add))
            dve.sem_inc(sums, 1)
            dve.wait_ge(counted, 1)
            step(dve.tensor_copy(row[0:1, 0, :], small[0:1, 0:T + 2]))
            step(dve.tensor_scalar(row[0:1, 1, :], row[0:1, 0, :], float(P - 1), None, ALU.add))
            step(dve.tensor_copy(rowi[0:1, 0, :], row[0:1, 1, :]))
            step(dve.tensor_single_scalar(rowi[0:1, 1, :], rowi[0:1, 0, :], 7, ALU.arith_shift_right))
            step(dve.tensor_copy(row[0:1, 2, :], rowi[0:1, 1, :]))
            step(dve.tensor_tensor_scan(row[0:1, 3, 0:T], k.zero[0:1, 0:T], row[0:1, 0, 0:T], 0.0, ALU.add, ALU.add))
            step(dve.tensor_tensor_scan(row[0:1, 4, 0:T], k.zero[0:1, 0:T], row[0:1, 2, 0:T], 0.0, ALU.add, ALU.add))
            step(dve.tensor_tensor(row[0:1, 5, 0:T], row[0:1, 3, 0:T], row[0:1, 0, 0:T], ALU.subtract))
            step(dve.tensor_tensor(row[0:1, 6, 0:T], row[0:1, 4, 0:T], row[0:1, 2, 0:T], ALU.subtract))
            step(dve.tensor_scalar(row[0:1, 6, 0:T], row[0:1, 6, 0:T], float(P), None, ALU.mult))
            step(dve.tensor_copy(k.starts[0:1, 0:T], row[0:1, 5, 0:T]))
            step(dve.tensor_copy(k.starts[0:1, T:2 * T], row[0:1, 6, 0:T]))
            step(dve.tensor_scalar(row[0:1, 7, 0:1], row[0:1, 0, T:T + 1], 1.0, None, ALU.min))
            step(dve.tensor_copy(k.starts[0:1, 2 * T:2 * T + 1], row[0:1, 7, 0:1]))
            dve.sem_inc(rowed, 1)
            dve.wait_ge(counted, 2)
            step(dve.tensor_copy(ends[:], small[0:T, 64:65]))
            step(dve.tensor_scalar(cmpj[:], ioj[:], ends[:, 0:1], None, ALU.is_ge))
            dve.sem_inc(mapped, 1)
            dve.wait_ge(counted, 3)
            step(dve.tensor_scalar(k.slot_tile[:], mapp[:, 0:S + 1], float(T - 1), None, ALU.min))
            step(dve.tensor_copy(k.slot_tile_i[0:1, :], k.slot_tile[0:1, :]))
            dve.wait_ge(cleared, 1)
            step(dve.tensor_copy(k.deg_src[:], hist[:, 0:T]))

        @block.tensor
        def _(pe):
            pe.wait_ge(made, 8)
            pe.matmul(hist[:, 0:T], zed[:, 0:P], zed[:, 0:T], start=True, stop=False)
            with pe.Fori(0, EC // 8) as i:
                for u in range(8):
                    pe.wait_ge(hot, i * 16 + 2 * u + 2)
                    last = pe.matmul(hist[:, 0:T], lob[:, u, :], hib[:, u, :], start=False, stop=False)
                last.then_inc(used, 1)
            pe.matmul(hist[:, 0:T], zed[:, 0:P], zed[:, 0:T], start=False, stop=True).then_inc(cleared, 1)
            pe.wait_ge(sums, 1)
            pe.matmul(small[0:1, 0:T + 2], k.ones[0:EP, 0:1], per[:], start=True, stop=True).then_inc(counted, 1)
            pe.wait_ge(rowed, 1)
            pe.matmul(small[0:T, 64:65], row[0:1, 4, 0:T], k.ones[0:1, 0:1], start=True, stop=True).then_inc(counted, 1)
            pe.wait_ge(mapped, 1)
            pe.matmul(mapp[:, 0:S + 1], k.ones[0:T, :], cmpj[:], start=True, stop=True).then_inc(counted, 1)


def order_edges(nc, k, fields, dst):
    with ExitStack() as c:
        c.enter_context(nc.cleanup_on_exit())
        sb = lambda n, s, d=F32: c.enter_context(nc.sbuf_tensor("o_" + n, s, d))
        sem = lambda n: nc.alloc_semaphore("o_" + n)
        padi = sb("padi", [P, SE // P], I32)
        padz = sb("padz", [P, SE // P], I32)
        dni = sb("dni", [EP, EC], I32)
        dnf = sb("dnf", [EP, EC])
        en = sb("en", [EP, EC])
        BK = EP * 25
        NB = E // BK
        keys = sb("keys", [EP, BK], I32)
        keyf = sb("keyf", [EP, BK])
        place = sb("place", [EP, BK])
        before = sb("before", [EP, BK])
        hit = sb("hit", [EP, BK])
        two = sb("two", [EP, 2])
        rank = sb("rank", [EP, EC])
        ranki = sb("ranki", [EP, EC], I32)
        rk1 = sb("rk1", [EP, 1], I32)
        fl = [sb(f"fl{n}", [EP, EC], I32) for n in range(4)]
        f1 = sb("f1", [EP, 4], I32)
        padded, pads, copied = sem("padded"), sem("pads"), sem("copied")
        iot, keyed, vstep, ranked, put = sem("iot"), sem("keyed"), sem("vstep"), sem("ranked"), sem("put")
        bl, fields_in, pstep = sem("bl"), sem("fields_in"), sem("pstep")
        block = c.enter_context(nc.Block())

        @block.sync
        def _(sp):
            unordered = sp.value_load(k.starts[0:1, 2 * T:2 * T + 1], min_val=0, max_val=1)
            sp.wait_ge(padded, 2)
            for f in range(4):
                sp.dma_start(k.ordered[f][E:E + SE].rearrange("(p c) -> p c", p=P),
                             (padi if f == 1 else padz)[:]).then_inc(pads, 16)
            with sp.If(unordered == 0):
                for f in range(4):
                    sp.dma_start(k.ordered[f][0:E].rearrange("(a b) -> a b", a=16),
                                 fields[f].rearrange("(a b) -> a b", a=16)).then_inc(copied, 16)
                sp.wait_ge(copied, 64)
            with sp.If(unordered != 0):
                sp.dma_start(dni[:], dst.rearrange("(p c) -> p c", c=EC)).then_inc(fields_in, 16)
                for f in range(4):
                    sp.dma_start(fl[f][:], fields[f].rearrange("(p c) -> p c", c=EC)).then_inc(fields_in, 16)
                with sp.Fori(0, NB) as b:
                    sp.wait_ge(bl, b + 1)
                    sp.dma_start(keys[:],
                                 bass.AP(dst.tensor, 0, [[0, EP], [1, E]])[:, bass.ds(b * BK, BK)]).then_inc(keyed, 16)
                sp.wait_ge(bl, NB + 1)
            sp.wait_ge(pads, 64)

        @block.gpsimd
        def _(pool):
            unordered = pool.value_load(k.starts[0:1, 2 * T:2 * T + 1], min_val=0, max_val=1)
            step = Order(pool, pstep)
            pool.memset(padi[:], int(PAD_DST)).then_inc(padded, 1)
            pool.memset(padz[:], 0).then_inc(padded, 1)
            with pool.If(unordered != 0):
                pool.iota(en[:], [[1, EC]], base=0, channel_multiplier=EC,
                          allow_small_or_imprecise_dtypes=True).then_inc(iot, 1)
                pool.iota(place[:], [[1, BK]], base=0, channel_multiplier=0,
                          allow_small_or_imprecise_dtypes=True).then_inc(iot, 1)
                pool.wait_ge(ranked, 1)
                pool.wait_ge(fields_in, 80)
                with pool.Fori(0, EC) as i:
                    step.n = i * 5
                    step(pool.tensor_copy(rk1[:], cols(ranki, i, 1)))
                    for f in range(4):
                        step(pool.tensor_copy(f1[:, f:f + 1], cols(fl[f], i, 1)))
                    for f in range(4):
                        pool.sem_inc(k.passed, 1)
                        pool.indirect_dma_start(k.ordered[f].rearrange("(e a) -> e a", a=1),
                                                bass.IndirectOffsetOnAxis(ap=rk1[:, 0:1], axis=0),
                                                f1[:, f:f + 1], None).then_inc(put, 16)
                    pool.wait_ge(put, i * 64 + 64)
                    pool.sem_inc(k.passed, 1)

        @block.vector
        def _(dve):
            unordered = dve.value_load(k.starts[0:1, 2 * T:2 * T + 1], min_val=0, max_val=1)
            with dve.If(unordered != 0):
                step = Order(dve, vstep)
                dve.sem_inc(bl, 1)
                dve.wait_ge(fields_in, 80)
                dve.wait_ge(iot, 2)
                step(dve.tensor_copy(dnf[:], dni[:]))
                step(dve.memset(rank[:], 0.0))
                with dve.Fori(0, NB) as b:
                    step.n = 2 + b * (2 + EC * 5)
                    dve.wait_ge(keyed, b * 16 + 16)
                    step(dve.tensor_copy(keyf[:], keys[:]))
                    dve.sem_inc(k.passed, 1)
                    with dve.Fori(0, EC) as i:
                        step.n = 3 + b * (2 + EC * 5) + i * 5
                        step(dve.tensor_scalar(hit[:], keyf[:], cols(dnf, i, 1), 0.0, ALU.is_lt, ALU.add,
                                               accum_out=two[:, 0:1]))
                        step(dve.tensor_scalar(before[:], place[:], cols(en, i, 1), None, ALU.is_lt))
                        step(dve.scalar_tensor_tensor(hit[:], keyf[:], cols(dnf, i, 1), before[:], ALU.is_equal,
                                                      ALU.mult, accum_out=two[:, 1:2]))
                        step(dve.tensor_tensor(cols(rank, i, 1), cols(rank, i, 1), two[:, 0:1], ALU.add))
                        step(dve.tensor_tensor(cols(rank, i, 1), cols(rank, i, 1), two[:, 1:2], ALU.add))
                        dve.sem_inc(k.passed, 1)
                    step.n = 3 + b * (2 + EC * 5) + EC * 5
                    step(dve.tensor_scalar(en[:], en[:], float(-BK), None, ALU.add))
                    dve.sem_inc(bl, 1)
                dve.tensor_copy(ranki[:], rank[:]).then_inc(ranked, 1)


def fill_slots(nc, k):
    with ExitStack() as c:
        c.enter_context(nc.cleanup_on_exit())
        sb = lambda n, s, d=F32: c.enter_context(nc.sbuf_tensor("f_" + n, s, d))
        sem = lambda n: nc.alloc_semaphore("f_" + n)
        rows_i = sb("rows_i", [SQ, 2, SG, P], I32)
        rows_t = sb("rows_t", [SQ, SG, P], I32)
        rows_f = sb("rows_f", [SQ, 2, SG, P])
        rows_p = sb("rows_p", [SQ, SG, P], I32)
        rows_n = sb("rows_n", [SQ, SG, P], I32)
        shifted = sb("shifted", [SQ, SG, P])
        flips = c.enter_context(nc.psum_tensor("flips", [P, 4, 512], F32))
        laid, rows, vstep, turned, flipped, kept = (sem("laid"), sem("rows"), sem("vstep"), sem("turned"),
                                                    sem("flipped"), sem("kept"))
        ends_in, pstep = sem("ends_in"), sem("pstep")
        block = c.enter_context(nc.Block())

        @block.sync
        def _(sp):
            sp.wait_ge(ends_in, 32)
            for t in range(T):
                first = sp.value_load(k.starts[0:1, t:t + 1], min_val=0, max_val=E)
                place = sp.value_load(k.starts[0:1, T + t:T + t + 1], min_val=0, max_val=SE)
                for f in range(4):
                    sp.dma_start(k.slots[f][bass.ds(place + P, SE)].rearrange("(a b) -> a b", a=16),
                                 k.ordered[f][bass.ds(first, SE)].rearrange("(a b) -> a b", a=16)).then_inc(laid, 16)
                sp.wait_ge(laid, 64 * (t + 1))
            flat = lambda f, o: k.slots[f][o:o + SE].rearrange("(g q p) -> q g p", q=SQ, p=P)
            sp.dma_start(rows_i[:, 0, :, :], flat(0, P)).then_inc(rows, 16)
            sp.dma_start(rows_i[:, 1, :, :], flat(1, P)).then_inc(rows, 16)
            sp.dma_start(rows_t[:], flat(2, P)).then_inc(rows, 16)
            sp.dma_start(k.rows_w[:], k.slots[3][P:P + SE].bitcast(F32).rearrange("(g q p) -> q g p", q=SQ, p=P)).then_inc(rows, 16)
            sp.dma_start(rows_p[:], flat(1, P - 1)).then_inc(rows, 16)
            sp.dma_start(rows_n[:], flat(1, P + 1)).then_inc(rows, 16)
            sp.wait_ge(rows, 96)

        @block.gpsimd
        def _(pool):
            pool.memset(k.edge_pad[:], -1).then_inc(pstep, 1)
            pool.wait_ge(pstep, 1)
            for at in (0, P + SE):
                pool.dma_start(k.slots[1][at:at + P].rearrange("(a b) -> a b", a=1), k.edge_pad[:]).then_inc(ends_in, 16)
            pool.wait_ge(ends_in, 32)

        @block.vector
        def _(dve):
            step = Order(dve, vstep)
            dve.wait_ge(rows, 96)
            step(dve.tensor_copy(rows_f[:, 0, :, :], rows_i[:, 0, :, :]))
            step(dve.tensor_copy(k.rows_dst[:], rows_i[:, 1, :, :]))
            step(dve.tensor_copy(rows_f[:, 1, :, :], rows_t[:]))
            dve.sem_inc(turned, 1)
            for links, whole in ((rows_p, k.pen_prev), (rows_n, k.pen_next)):
                step(dve.tensor_copy(shifted[:], links[:]))
                step(dve.tensor_tensor(whole[:], k.rows_dst[:], shifted[:], ALU.is_equal))
                step(dve.tensor_scalar(whole[:], whole[:], -1.0, BIG, ALU.add, ALU.mult))
            for f, to in enumerate((k.src, k.dst, k.rel, k.weight)):
                dve.wait_ge(flipped, f + 1)
                step(dve.tensor_copy(to[:, 0:S].rearrange("p (g q) -> p g q", g=SG),
                                     flips[:, f, 0:S].rearrange("p (g q) -> p g q", g=SG)))
            step(dve.tensor_scalar(k.node[:], k.slot_tile[:, 1:S + 1], float(P), k.pcol[:, 0:1], ALU.mult, ALU.add))
            step(dve.tensor_scalar(k.dloc[:], k.node[:], -1.0, k.pcol[:, 0:1], ALU.mult, ALU.add))
            step(dve.tensor_tensor(k.dloc[:], k.dloc[:], k.dst[:], ALU.add))
            step(dve.tensor_copy(k.src_i[:], k.src[:]))
            step(dve.tensor_scalar(k.rel[:], k.rel[:], float(NP), None, ALU.mult))
            step(dve.tensor_tensor(k.rel[:], k.rel[:], k.src[:], ALU.add))
            step(dve.tensor_copy(k.rel_i[:], k.rel[:]))

        @block.tensor
        def _(pe):
            pe.wait_ge(turned, 1)
            for f in range(4):
                for g in range(SG):
                    rows_of = (rows_f[:, 0, g, :], k.rows_dst[:, g, :], rows_f[:, 1, g, :], k.rows_w[:, g, :])[f]
                    last = pe.transpose(flips[:, f, g * SQ:(g + 1) * SQ], rows_of, k.ident[0:SQ, 0:SQ])
                last.then_inc(flipped, 1)



def sum_by_source(nc, k, y):
    with ExitStack() as c:
        c.enter_context(nc.cleanup_on_exit())
        sb = lambda n, s, d=F32: c.enter_context(nc.sbuf_tensor("s_" + n, s, d))
        pb = lambda n, s: c.enter_context(nc.psum_tensor(n, s, F32))
        sem = lambda n: nc.alloc_semaphore("s_" + n)
        zrow = sb("zrow", [P, (T + 1) // (RING // CH), D])
        dcol = sb("dcol", [P, U])
        scol = sb("scol", [P, U])
        pick = sb("pick", [P, 2, G4, P])
        same = sb("same", [P, 2, G4, P])
        earlier = sb("earlier", [P, G4, P])
        count = sb("count", [P, G4])
        delta = sb("delta", [P, G4])
        trash = sb("trash", [P, 1])
        to = sb("to", [P, U], I32)
        rows = sb("rows", [P, G4, D])
        merged = sb("merged", [P, RING, D])
        wide = pb("wide", [P, 2, 512])
        wide2 = pb("wide2", [P, 2, 512])
        expand = pb("expand", [P, 2, 512])
        merge = pb("merge", [P, 2, 512])
        zin, vstep = sem("zin"), sem("vstep")
        copied, turned, picked, indexed = sem("copied"), sem("turned"), sem("picked"), sem("indexed")
        expanded, kept, joined, ready = sem("expanded"), sem("kept"), sem("joined"), sem("ready")
        added = [sem(f"added{n}") for n in range(RING)]
        NG = U // G4
        block = c.enter_context(nc.Block())

        @block.gpsimd
        def _(pool):
            pool.memset(zrow[:], 0.0).then_inc(zin, 1)
            pool.wait_ge(zin, 1)
            for n in range(RING):
                part = k.sums[n % CH].rearrange("(a t p) f -> a p t f", a=RING // CH, p=P)[n // CH]
                pool.dma_start(part, zrow[:]).then_inc(added[n], 16)
            for n in range(RING):
                pool.wait_ge(added[n], 16)
            with pool.Fori(0, IT) as i:
                for u in range(U):
                    pool.wait_ge(indexed, i * NG + u // G4 + 2)
                    pool.wait_ge(ready, i * U + u + 3)
                    pool.wait_ge(added[(u - CH) % RING], i * 32 + 16 * ((u - CH) // RING) + 32)
                    pool.sem_inc(k.passed, 1)
                    pool.indirect_dma_start(k.sums[u % CH], bass.IndirectOffsetOnAxis(ap=to[:, u:u + 1], axis=0),
                                            merged[:, u % RING, :], None,
                                            compute_op=ALU.add).then_inc(added[u % RING], 16)
            for n in range(RING):
                pool.wait_ge(added[n], 16 + 16 * (S // RING))

        @block.vector
        def _(dve):
            step = Order(dve, vstep)
            step(dve.tensor_scalar(trash[:], k.pcol[:], float(NTRASH), None, ALU.add))
            dve.sem_inc(picked, 4)
            dve.sem_inc(indexed, 1)
            with dve.Fori(0, IT) as i:
                for g in range(NG):
                    n = i * NG + g
                    step.n = 1 + n * 5
                    dve.wait_ge(indexed, n + 1)
                    if g == 0:
                        dve.wait_ge(turned, n + 4)
                        dve.tensor_copy(dcol[:], cols(k.dst, i * U, U)).then_inc(copied, 1)
                        dve.tensor_copy(scol[:], cols(k.src, i * U, U)).then_inc(copied, 1)
                        dve.wait_ge(copied, i * 2 + 2)
                    dve.wait_ge(turned, n + 5)
                    dve.wait_ge(joined, n * G4 + 4)
                    dve.tensor_tensor(pick[:, g % 2, :, :], wide[:, g % 2, :].rearrange("p (s q) -> p s q", s=G4),
                                      cols(k.node, i * U + g * G4, G4).unsqueeze(2).broadcast_to([P, G4, P]),
                                      ALU.is_equal).then_inc(picked, 1)
                    dve.tensor_tensor(same[:, g % 2, :, :], wide2[:, g % 2, :].rearrange("p (s q) -> p s q", s=G4),
                                      scol[:, g * G4:(g + 1) * G4].unsqueeze(2).broadcast_to([P, G4, P]),
                                      ALU.is_equal).then_inc(picked, 1)
                    dve.wait_ge(picked, n * 2 + 6)
                    step(dve.tensor_tensor(earlier[:], same[:, g % 2, :, :],
                                           k.low[:].unsqueeze(1).broadcast_to([P, G4, P]), ALU.mult))
                    step(dve.tensor_reduce(count[:], earlier[:], AX.X, ALU.max))
                    step(dve.tensor_scalar(delta[:], scol[:, g * G4:(g + 1) * G4], -1.0, trash[:, 0:1],
                                           ALU.mult, ALU.add))
                    step(dve.tensor_tensor(delta[:], delta[:], count[:], ALU.mult))
                    step(dve.tensor_tensor(delta[:], delta[:], scol[:, g * G4:(g + 1) * G4], ALU.add))
                    for u in range(g * G4, (g + 1) * G4):
                        dve.wait_ge(added[u % RING], i * 32 + 16)
                    dve.tensor_copy(to[:, g * G4:(g + 1) * G4], delta[:]).then_inc(indexed, 1)

        @block.tensor
        def _(pe):
            pe.sem_inc(joined, 8)
            pe.sem_inc(turned, 4)
            with pe.Fori(0, IT) as i:
                def turn(g):
                    n = i * NG + g
                    pe.wait_ge(picked, n * 2 + 2)
                    for s in range(G4):
                        u = g * G4 + s
                        pe.transpose(wide[:, g % 2, s * P:(s + 1) * P], dcol[:, u:u + 1].broadcast_to([P, P]),
                                     k.ident[:])
                        last = pe.transpose(wide2[:, g % 2, s * P:(s + 1) * P],
                                            scol[:, u:u + 1].broadcast_to([P, P]), k.ident[:])
                    last.then_inc(turned, 1)

                def expand_slot(u):
                    t = pe.value_load(k.slot_tile_i[0:1, bass.ds(i * U + u + 1, 1)], min_val=0, max_val=T - 1)
                    pe.wait_ge(kept, i * U + u + 1)
                    pe.matmul(expand[:, u % 2, 0:D], pick[:, (u // G4) % 2, u % G4, :], tile_of(y, t),
                              start=True, stop=True).then_inc(expanded, 1)

                def merge_slot(u):
                    pe.wait_ge(kept, i * U + u + 3)
                    pe.wait_ge(ready, i * U + u + 1)
                    pe.matmul(merge[:, u % 2, 0:D], same[:, (u // G4) % 2, u % G4, :], rows[:, u % G4, :],
                              start=True, stop=True).then_inc(joined, 1)

                pe.wait_ge(copied, i * 2 + 2)
                turn(0)
                for g in range(NG):
                    if g + 1 < NG:
                        turn(g + 1)
                    pe.wait_ge(picked, (i * NG + g) * 2 + 6)
                    for s in range(G4 + 1):
                        if s < G4:
                            expand_slot(g * G4 + s)
                        if s > 0:
                            merge_slot(g * G4 + s - 1)

        @block.scalar
        def _(act):
            act.sem_inc(kept, 2)
            act.sem_inc(ready, 2)
            with act.Fori(0, IT) as i:
                for g in range(NG):
                    for s in range(G4 + 1):
                        if s < G4:
                            u = g * G4 + s
                            act.wait_ge(expanded, i * U + u + 1)
                            act.wait_ge(joined, i * U + u + 5)
                            act.copy(rows[:, u % G4, :], expand[:, u % 2, 0:D]).then_inc(kept, 1)
                        if s > 0:
                            u = g * G4 + s - 1
                            act.wait_ge(joined, i * U + u + 9)
                            act.wait_ge(added[u % RING], i * 32 + 16 * (u // RING) + 16)
                            act.copy(merged[:, u % RING, :], merge[:, u % 2, 0:D]).then_inc(ready, 1)


def score_by_edge(nc, k, name, table, width, node_rows, out_src, out_dst):
    dot = out_dst is None
    with ExitStack() as c:
        c.enter_context(nc.cleanup_on_exit())
        sb = lambda n, s, d=F32: c.enter_context(nc.sbuf_tensor(name + n, s, d))
        pb = lambda n, s: c.enter_context(nc.psum_tensor(name + n, s, F32))
        sem = lambda n: nc.alloc_semaphore(name + n)
        dcol = sb("dcol", [P, U])
        pick = sb("pick", [P, 2, G4, P])
        idx = sb("idx", [P, 2, 8], I32)
        ring = RING if dot else U
        got = sb("got", [P, ring, width])
        prod = sb("prod", [P, width])
        score = sb("score", [P, U])
        wide = pb("wide", [P, 2, 512])
        expand = pb("expand", [P, 4, 512])
        copied, turned, picked = sem("copied"), sem("turned"), sem("picked")
        expanded, used, kept, istep = sem("expanded"), sem("used"), sem("kept"), sem("istep")
        arrived = [sem(f"arrived{n}") for n in range(ring)]
        NG = U // G4
        block = c.enter_context(nc.Block())

        @block.gpsimd
        def _(pool):
            with pool.Fori(0, IT) as i:
                for u in range(U):
                    j = i * U + u
                    if dot:
                        pool.wait_ge(used, j + 17 - RING)
                    elif u == 0:
                        pool.wait_ge(used, i * U + 16)
                    if u % 8 == 0:
                        pool.sem_inc(k.passed, 1)
                        pool.tensor_copy(idx[:, u // 8, :], cols(k.src_i, i * U + u, 8)).then_inc(istep, 1)
                        pool.wait_ge(istep, i * 2 + u // 8 + 1)
                    pool.sem_inc(k.passed, 1)
                    pool.indirect_dma_start(got[:, u % ring, :], None, table, bass.IndirectOffsetOnAxis(
                        ap=idx[:, u // 8, u % 8:u % 8 + 1], axis=0)).then_inc(arrived[u % ring], 16)

        @block.vector
        def _(dve):
            dve.sem_inc(picked, 2)
            with dve.Fori(0, IT) as i:
                def use(u):
                    j = i * U + u
                    dve.wait_ge(expanded, j + 2)
                    dve.wait_ge(arrived[u % ring], i * (16 * U // ring) + 16 * (u // ring) + 16)
                    dve.wait_ge(used, j + 16)
                    if u == 0:
                        dve.wait_ge(kept, i + 1)
                    dve.tensor_tensor_reduce(out=prod[:], in0=expand[:, u % 4, 0:width], in1=got[:, u % ring, :],
                                             scale=1.0, scalar=0.0, op0=ALU.mult, op1=ALU.add,
                                             accum_out=score[:, u:u + 1]).then_inc(used, 1)

                dve.wait_ge(turned, i * NG + 4)
                dve.tensor_copy(dcol[:], cols(k.dst, i * U, U)).then_inc(copied, 1)
                for g in range(NG):
                    n = i * NG + g
                    dve.wait_ge(turned, n + 5)
                    if g >= 2:
                        dve.wait_ge(expanded, n * G4 - 3)
                    else:
                        dve.wait_ge(expanded, i * U + 1)
                    dve.tensor_tensor(pick[:, g % 2, :, :], wide[:, g % 2, :].rearrange("p (s q) -> p s q", s=G4),
                                      cols(k.node, i * U + g * G4, G4).unsqueeze(2).broadcast_to([P, G4, P]),
                                      ALU.is_equal).then_inc(picked, 1)
                    if dot and g > 0:
                        for u in range((g - 1) * G4, g * G4):
                            use(u)
                if dot:
                    for u in range((NG - 1) * G4, U):
                        use(u)

        @block.tensor
        def _(pe):
            pe.sem_inc(turned, 4)
            pe.sem_inc(expanded, 1)
            with pe.Fori(0, IT) as i:
                def turn(g):
                    n = i * NG + g
                    pe.wait_ge(picked, n + 1)
                    for s in range(G4):
                        u = g * G4 + s
                        last = pe.transpose(wide[:, g % 2, s * P:(s + 1) * P],
                                            dcol[:, u:u + 1].broadcast_to([P, P]), k.ident[:])
                    last.then_inc(turned, 1)

                pe.wait_ge(copied, i + 1)
                turn(0)
                for g in range(NG):
                    if g + 1 < NG:
                        turn(g + 1)
                    pe.wait_ge(picked, i * NG + g + 3)
                    for u in range(g * G4, (g + 1) * G4):
                        t = pe.value_load(k.slot_tile_i[0:1, bass.ds(i * U + u + 1, 1)], min_val=0, max_val=T - 1)
                        if dot:
                            pe.wait_ge(used, i * U + u + 13)
                            to = expand[:, u % 4, 0:width]
                        else:
                            if u == 0:
                                pe.wait_ge(used, i * U + 16)
                            to = expand[:, 0, u * width:(u + 1) * width]
                        pe.matmul(to, pick[:, g % 2, u % G4, :], tile_of(node_rows, t),
                                  start=True, stop=True).then_inc(expanded, 1)

        @block.scalar
        def _(act):
            if dot:
                act.sem_inc(used, 16)
                act.sem_inc(kept, 1)
                with act.Fori(0, IT) as i:
                    act.wait_ge(used, i * U + U + 16)
                    act.sem_inc(k.passed, 1)
                    act.mul(cols(out_src, i * U, U), score[:], 1.0 / float(np.sqrt(D))).then_inc(kept, 1)
                    act.wait_ge(kept, i + 2)
                    act.sem_inc(k.passed, 1)
            else:
                act.sem_inc(used, 16)
                with act.Fori(0, IT) as i:
                    act.wait_ge(expanded, i * U + U + 1)
                    for u in range(U):
                        act.wait_ge(arrived[u], i * 16 + 16)
                    act.sem_inc(k.passed, 1)
                    act.copy(out_dst[:, bass.ds(i * U, U), :].rearrange("p s h -> p (s h)"),
                             expand[:, 0, 0:U * width]).then_inc(used, 8)
                    act.copy(out_src[:, bass.ds(i * U, U), :].rearrange("p s h -> p (s h)"),
                             got[:].rearrange("p s h -> p (s h)")).then_inc(used, 8)


def segment_maximum(nc, k, name, heads, value, out):
    with ExitStack() as c:
        c.enter_context(nc.cleanup_on_exit())
        sb = lambda n, s, d=F32: c.enter_context(nc.sbuf_tensor(name + n, s, d))
        sem = lambda n: nc.alloc_semaphore(name + n)
        v = sb("v", [SQ, SG, heads, P])
        scan = [sb("scan", [SQ, SG, heads, P]), v]
        pen = sb("pen", [SQ, SG, heads, P])
        edge = sb("edge", [SQ, 2, SG, heads])
        whole = sb("whole", [SQ, 2, SG, heads])
        reset = sb("reset", [SQ, SG, P])
        reach = sb("reach", [SQ, 2, SG, P])
        one = sb("one", [SQ, 2, SG])
        line = sb("line", [heads, 2, S])
        lpen = sb("lpen", [heads, 2, S])
        carry = sb("carry", [heads, 2, S])
        carried = sb("carried", [SQ, 2, SG, heads])
        turns = c.enter_context(nc.psum_tensor(name + "turns", [P, 4, 512], F32))
        lines = c.enter_context(nc.psum_tensor(name + "lines", [P, 2, 512], F32))
        lines2 = c.enter_context(nc.psum_tensor(name + "lines2", [P, 2, 512], F32))
        turned, taken, vstep, ends, lined, carry_s, back, done = (
            sem("turned"), sem("taken"), sem("vstep"), sem("ends"), sem("lined"), sem("carry_s"),
            sem("back"), sem("done"))
        out_t, out_k, final = sem("out_t"), sem("out_k"), sem("final")
        block = c.enter_context(nc.Block())
        per_bank = 4

        @block.tensor
        def _(pe):
            for n in range(SG * heads):
                g, h = n // heads, n % heads
                if n >= 4:
                    pe.wait_ge(taken, n - 3)
                pe.transpose(turns[0:SQ, n % 4, 0:P], value[:, g * SQ:(g + 1) * SQ, h], k.ident[:]).then_inc(turned, 1)
            pe.wait_ge(ends, 1)
            for d in range(2):
                for g in range(SG):
                    pe.transpose(lines[0:heads, d, g * SQ:(g + 1) * SQ], edge[:, d, g, :], k.ident[0:SQ, 0:SQ])
                    last = pe.transpose(lines2[0:heads, d, g * SQ:(g + 1) * SQ], whole[:, d, g, :],
                                        k.ident[0:SQ, 0:SQ])
            last.then_inc(lined, 1)
            pe.wait_ge(carry_s, 1)
            for d in range(2):
                for g in range(SG):
                    last = pe.transpose(turns[0:SQ, 0, (d * SG + g) * heads:(d * SG + g + 1) * heads],
                                        carry[:, d, g * SQ:(g + 1) * SQ], k.ident[0:heads, 0:heads])
            last.then_inc(back, 1)
            pe.wait_ge(final, 1)
            for n in range(SG * heads):
                g, h = n // heads, n % heads
                if n >= 4:
                    pe.wait_ge(out_k, n - 3)
                pe.transpose(turns[:, n % 4, 0:SQ], scan[0][:, g, h, :], k.ident[0:SQ, 0:SQ]).then_inc(out_t, 1)

        @block.scalar
        def _(act):
            for n in range(SG * heads):
                g, h = n // heads, n % heads
                act.wait_ge(turned, n + 1)
                act.copy(v[:, g, h, :], turns[0:SQ, n % 4, 0:P]).then_inc(taken, 1)
            for n in range(SG * heads):
                g, h = n // heads, n % heads
                act.wait_ge(out_t, n + 1)
                act.copy(out[:, g * SQ:(g + 1) * SQ, h], turns[:, n % 4, 0:SQ]).then_inc(out_k, 1)
            act.wait_ge(out_k, SG * heads)

        @block.vector
        def _(dve):
            step = Order(dve, vstep)
            flat = lambda a: a.rearrange("q g p -> q (g p)")
            flat4 = lambda a: a.rearrange("q g h p -> q (g h p)")
            for d, links in enumerate((k.pen_prev, k.pen_next)):
                entry, leave = (0, P - 1) if d == 0 else (P - 1, 0)
                step(dve.memset(reset[:], 0.0))
                step(dve.memset(reset[:, :, entry:entry + 1], BIG))
                a, b, o = flat(reset[:]), flat(links[:]), flat(reach[:, d, :, :])
                if d:
                    a, b, o = a[:, ::-1], b[:, ::-1], o[:, ::-1]
                step(dve.tensor_tensor_scan(o, a, b, 0.0, ALU.add, ALU.min))
                step(dve.tensor_copy(whole[:, d, :, :], reach[:, d, :, leave:leave + 1].broadcast_to([SQ, SG, heads])))
            dve.wait_ge(taken, SG * heads)
            for d, links in enumerate((k.pen_prev, k.pen_next)):
                entry, leave = (0, P - 1) if d == 0 else (P - 1, 0)
                step(dve.tensor_copy(pen[:], links[:].unsqueeze(2).broadcast_to([SQ, SG, heads, P])))
                step(dve.memset(pen[:, :, :, entry:entry + 1], -BIG))
                a, b, o = flat4(pen[:]), flat4(v[:]), flat4(scan[d][:])
                if d:
                    a, b, o = a[:, ::-1], b[:, ::-1], o[:, ::-1]
                step(dve.tensor_tensor_scan(o, a, b, -BIG, ALU.add, ALU.max))
                step(dve.tensor_copy(edge[:, d, :, :], scan[d][:, :, :, leave:leave + 1].rearrange("q g h a -> q g (h a)")))
            dve.sem_inc(ends, 1)
            dve.wait_ge(lined, 1)
            step(dve.tensor_copy(line[:], lines[0:heads, :, 0:S]))
            step(dve.tensor_copy(lpen[:], lines2[0:heads, :, 0:S]))
            step(dve.memset(carry[:], -BIG))
            step(dve.tensor_tensor_scan(carry[:, 0, 1:S], lpen[:, 0, 0:S - 1], line[:, 0, 0:S - 1], -BIG,
                                        ALU.add, ALU.max))
            step(dve.tensor_tensor_scan(carry[:, 1, 0:S - 1][:, ::-1], lpen[:, 1, 1:S][:, ::-1],
                                        line[:, 1, 1:S][:, ::-1], -BIG, ALU.add, ALU.max))
            dve.sem_inc(carry_s, 1)
            dve.wait_ge(back, 1)
            step(dve.tensor_copy(carried[:].rearrange("q d g h -> q (d g h)"), turns[0:SQ, 0, 0:2 * SG * heads]))
            for d in range(2):
                for g in range(SG):
                    step(dve.tensor_tensor(pen[:, g, :, :], carried[:, d, g, :].unsqueeze(2).broadcast_to([SQ, heads, P]),
                                           reach[:, d, g, :].unsqueeze(1).broadcast_to([SQ, heads, P]), ALU.add))
                step(dve.tensor_tensor(flat4(scan[d][:]), flat4(scan[d][:]), flat4(pen[:]), ALU.max))
            step(dve.tensor_tensor(flat4(scan[0][:]), flat4(scan[0][:]), flat4(scan[1][:]), ALU.max))
            dve.sem_inc(final, 1)


def sum_by_destination(nc, k, name, table, index, weight=None, per_head=None, ones=False):
    width = D + (H if per_head is not None else 1 if ones else 0)
    with ExitStack() as c:
        c.enter_context(nc.cleanup_on_exit())
        sb = lambda n, s, d=F32: c.enter_context(nc.sbuf_tensor(name + n, s, d))
        sem = lambda n: nc.alloc_semaphore(name + n)
        idx = sb("idx", [P, 2, 8], I32)
        got = sb("got", [P, RING, D])
        hot = sb("hot", [P, 4, P])
        part = sb("part", [P, 4, width]) if per_head is not None else None
        sums = c.enter_context(nc.psum_tensor(name + "sums", [P, 4, 512], F32))
        arrived = [sem(f"arrived{n}") for n in range(RING)]
        istep, cleared = sem("istep"), sem("cleared")
        made, summed, freed, added = sem("made"), sem("summed"), sem("freed"), sem("added")
        block = c.enter_context(nc.Block())

        @block.gpsimd
        def _(pool):
            pool.sem_inc(freed, 8)
            with pool.Fori(0, IT) as i:
                for u in range(U):
                    if per_head is not None:
                        pool.wait_ge(freed, i * U + u + 1)
                    else:
                        pool.wait_ge(summed, i * U + u + 2)
                    pool.sem_inc(k.passed, 1)
                    if u % 8 == 0:
                        pool.tensor_copy(idx[:, u // 8, :], cols(index, i * U + u, 8)).then_inc(istep, 1)
                        pool.wait_ge(istep, i * 2 + u // 8 + 1)
                        pool.sem_inc(k.passed, 1)
                    pool.indirect_dma_start(got[:, u % RING, :], None, table, bass.IndirectOffsetOnAxis(
                        ap=idx[:, u // 8, u % 8:u % 8 + 1], axis=0)).then_inc(arrived[u % RING], 16)

        @block.vector
        def _(dve):
            dve.memset(k.acc[:], 0.0).then_inc(cleared, 1)
            dve.wait_ge(cleared, 1)
            dve.sem_inc(added, 4)

            def add(j, b):
                t = dve.value_load(k.slot_tile_i[0:1, bass.ds(j, 1)], min_val=0, max_val=T - 1)
                dve.wait_ge(summed, j + 9)
                dve.wait_ge(added, j + 4)
                a = k.acc[:, bass.ds(t, 1), 0:width].rearrange("p a f -> p (a f)")
                dve.tensor_tensor(a, a, sums[:, b, 0:width], ALU.add).then_inc(added, 1)

            with dve.Fori(0, IT) as i:
                for u in range(U):
                    j = i * U + u
                    if weight is None:
                        ins = dve.tensor_scalar(hot[:, u % 4, :], k.iota[:], cols(k.dloc, j, 1), None, ALU.is_equal)
                    else:
                        ins = dve.tensor_scalar(hot[:, u % 4, :], k.iota[:], cols(k.dloc, j, 1), cols(weight, j, 1),
                                                ALU.is_equal, ALU.mult)
                    ins.then_inc(made, 1)
                    if per_head is not None:
                        dve.wait_ge(arrived[u % RING], i * 32 + 16 * (u // RING) + 16)
                        w = per_head[:, bass.ds(j, 1), :].rearrange("p a h -> p (a h)")
                        dve.tensor_tensor(part[:, u % 4, 0:D].rearrange("p (h f) -> p h f", h=H),
                                          got[:, u % RING, :].rearrange("p (h f) -> p h f", h=H),
                                          w.unsqueeze(2).broadcast_to([P, H, HD]), ALU.mult).then_inc(freed, 1)
                        dve.tensor_copy(part[:, u % 4, D:D + H], w).then_inc(made, 1)
                    add(j, (u - 1) % 4)
            add(S, (S - 1) % 4)
            dve.wait_ge(added, S + 5)

        @block.tensor
        def _(pe):
            pe.sem_inc(summed, 8)
            pe.matmul(sums[:, 3, 0:width], k.zero[:, 0:P], k.zero[:, 0:width], start=True, stop=True).then_inc(summed, 1)
            with pe.Fori(0, IT) as i:
                for u in range(U):
                    j = i * U + u
                    pe.wait_ge(added, j + 2)
                    if per_head is not None:
                        pe.wait_ge(freed, j + 9)
                        pe.wait_ge(made, 2 * j + 2)
                        pe.matmul(sums[:, u % 4, 0:width], hot[:, u % 4, :], part[:, u % 4, :],
                                  start=True, stop=True).then_inc(summed, 1)
                    else:
                        pe.wait_ge(made, j + 1)
                        pe.wait_ge(arrived[u % RING], i * 32 + 16 * (u // RING) + 16)
                        if ones:
                            pe.matmul(sums[:, u % 4, D:D + 1], hot[:, u % 4, :], k.ones[:, 0:1], start=True, stop=True)
                        pe.matmul(sums[:, u % 4, 0:D], hot[:, u % 4, :], got[:, u % RING, :],
                                  start=True, stop=True).then_inc(summed, 1)



def project(nc, k, name, sources, weights, width, steps, epilogue, stores=(), chains=None):
    ns = len(sources) if chains is None else 1
    with ExitStack() as c:
        c.enter_context(nc.cleanup_on_exit())
        sb = lambda n, s, d=F32: c.enter_context(nc.sbuf_tensor(name + n, s, d))
        sem = lambda n: nc.alloc_semaphore(name + n)
        xs = sb("xs", [P, 2, CH if chains is not None else ns, D])
        diag = sb("diag", [P, 2, P]) if chains is not None else None
        xt = sb("xt", [P, 2, ns * 2, P])
        flips = c.enter_context(nc.psum_tensor(name + "flips", [P, 2, 512], F32))
        nb = -(-width // 512)
        prods = c.enter_context(nc.psum_tensor(name + "prods", [P, 2, nb, 512], F32))
        staged, flipped, turned, multiplied, finished = (sem("staged"), sem("flipped"), sem("turned"),
                                                         sem("multiplied"), sem("finished"))
        vstep, stored = sem("vstep"), sem("stored")
        loaded = [sem(f"loaded{n}") for n in range(2)]
        block = c.enter_context(nc.Block())

        @block.sync
        def _(sp):
            if chains is not None:
                def load(t, b):
                    sp.wait_ge(flipped, t + 1)
                    for n in range(CH):
                        sp.dma_start(xs[:, b, n, :],
                                     chains[n][0][bass.ds(t * P, P), :]).then_inc(loaded[b], 16)
                over_tiles(sp, load)
            if stores:
                def store_all(t, b):
                    sp.wait_ge(finished, t + 3)
                    for src, dram in stores:
                        sp.dma_start(dram[bass.ds(t * P, P), :], src[:, bass.ds(t, 1), 0:D].rearrange(
                            "p a f -> p (a f)")).then_inc(stored, 16)
                over_tiles(sp, store_all)
                sp.wait_ge(stored, 16 * T * len(stores))

        @block.scalar
        def _(act):
            act.sem_inc(turned, 2)

            def stage(t, b):
                act.wait_ge(flipped, t + 1)
                act.sem_inc(k.passed, 1)
                for s, (src, column) in enumerate(sources):
                    if column is None:
                        ins = act.copy(xs[:, b, s, :], src[:, bass.ds(t, 1), 0:D].rearrange("p a f -> p (a f)"))
                    else:
                        ins = act.activation(xs[:, b, s, :], src[:, bass.ds(t, 1), 0:D].rearrange("p a f -> p (a f)"),
                                             ACT.Copy, scale=cols(column, t, 1))
                    ins.then_inc(staged, 1)

            def keep(t, b):
                act.wait_ge(flipped, t + 3)
                act.wait_ge(multiplied, t + 1)
                act.copy(xt[:, b, :, :].rearrange("p a q -> p (a q)"), flips[:, b, 0:ns * D]).then_inc(turned, 1)

            if chains is None:
                stage(0, 0)
                with act.Fori(0, T // 2) as i:
                    stage(2 * i + 1, 1)
                    keep(2 * i, 0)
                    stage(2 * i + 2, 0)
                    keep(2 * i + 1, 1)
                keep(T - 1, 0)
            else:
                over_tiles(act, keep)

        @block.tensor
        def _(pe):
            pe.sem_inc(flipped, 2)
            pe.sem_inc(multiplied, 2)

            def flip(t, b):
                pe.wait_ge(turned, t + 1)
                if chains is None:
                    pe.wait_ge(staged, (t + 1) * ns)
                    for s in range(ns):
                        for h in range(2):
                            last = pe.transpose(flips[:, b, s * D + h * P:s * D + (h + 1) * P],
                                                xs[:, b, s, h * P:(h + 1) * P], k.ident[:])
                else:
                    pe.wait_ge(loaded[b], (t - b) * (8 * CH) + 16 * CH)
                    pe.wait_ge(staged, t + 1)
                    for h in range(2):
                        for n in range(CH):
                            last = pe.matmul(flips[:, b, h * P:(h + 1) * P], xs[:, b, n, h * P:(h + 1) * P],
                                             diag[:, b, :], start=n == 0, stop=n == CH - 1)
                last.then_inc(flipped, 1)

            def multiply(t, b):
                pe.wait_ge(turned, t + 3)
                pe.wait_ge(finished, t + 1)
                for o in range(nb):
                    w = min(512, width - o * 512)
                    for s in range(ns * 2):
                        last = pe.matmul(prods[:, b, o, 0:w], xt[:, b, s, :], weights[:, s, o * 512:o * 512 + w],
                                         start=s == 0, stop=s == ns * 2 - 1)
                last.then_inc(multiplied, 1)

            flip(0, 0)
            with pe.Fori(0, T // 2) as i:
                flip(2 * i + 1, 1)
                multiply(2 * i, 0)
                flip(2 * i + 2, 0)
                multiply(2 * i + 1, 1)
            multiply(T - 1, 0)

        @block.vector
        def _(dve):
            dve.sem_inc(finished, 2)
            step = Order(dve, vstep)

            def work(t, b):
                dve.wait_ge(multiplied, t + 3)
                step.n = t * steps
                epilogue(dve, step, t, prods[:, b, :, :].rearrange("p a n -> p (a n)"))
                dve.sem_inc(finished, 1)

            def make_diag(t, b):
                dve.wait_ge(flipped, t + 1)
                dve.tensor_scalar(diag[:, b, :], k.ident[:], cols(chains[0][1], t, 1), None, ALU.mult).then_inc(staged, 1)

            if chains is None:
                over_tiles(dve, work)
            else:
                make_diag(0, 0)
                with dve.Fori(0, T // 2) as i:
                    make_diag(2 * i + 1, 1)
                    work(2 * i, 0)
                    make_diag(2 * i + 2, 0)
                    work(2 * i + 1, 1)
                work(T - 1, 0)


def each_tile(nc, k, name, steps, before, work, stores=()):
    with ExitStack() as c:
        c.enter_context(nc.cleanup_on_exit())
        sem = lambda n: nc.alloc_semaphore(name + n)
        vstep, finished, stored = sem("vstep"), sem("finished"), sem("stored")
        block = c.enter_context(nc.Block())

        @block.vector
        def _(dve):
            step = Order(dve, vstep)
            before(dve, step)
            base = step.n

            def one(t, b):
                step.n = base + t * steps
                work(dve, step, t)
                dve.sem_inc(finished, 1)
            over_tiles(dve, one)

        @block.sync
        def _(sp):
            if stores:
                def store(t, b):
                    sp.wait_ge(finished, t + 1)
                    for src, dram in stores:
                        sp.dma_start(dram[bass.ds(t * P, P), :], tile_of(src, t)).then_inc(stored, 16)
                over_tiles(sp, store)
                sp.wait_ge(stored, 16 * T * len(stores))


def statistics(dve, step, k, r, t):
    dve.sem_inc(k.passed, 1)
    step(dve.bn_stats(k.six[:], tile_of(r, t)))
    dve.sem_inc(k.passed, 1)
    step(dve.bn_aggr(k.two[:], k.six[:]))
    step(dve.tensor_copy(k.mv[:, bass.ds(t, 1), :].rearrange("p a f -> p (a f)"), k.two[:]))


def refine_root(dve, step, root, a, square):
    step(dve.reciprocal(root, root))
    step(dve.tensor_tensor(square, root, root, ALU.mult))
    step(dve.tensor_tensor(square, square, a, ALU.mult))
    step(dve.tensor_scalar(square, square, -0.5, 1.5, ALU.mult, ALU.add))
    step(dve.tensor_tensor(root, root, square, ALU.mult))


def normalize(nc, k, name, r, x, out=None):
    with ExitStack() as c:
        c.enter_context(nc.cleanup_on_exit())
        sem = lambda n: nc.alloc_semaphore(name + n)
        given, square = (c.enter_context(nc.sbuf_tensor(name + n, [P, T], F32)) for n in ("given", "square"))
        vstep, rooted, stored, finished = sem("vstep"), sem("rooted"), sem("stored"), sem("finished")
        block = c.enter_context(nc.Block())

        @block.vector
        def _(dve):
            step = Order(dve, vstep)
            step(dve.tensor_scalar(given[:], k.mv[:, :, 1], LN_EPS, None, ALU.add))
            dve.wait_ge(rooted, 1)
            refine_root(dve, step, k.rstd[:], given[:], square[:])

            def one(t, b):
                dve.tensor_scalar(tile_of(x, t), tile_of(r, t), k.mv[:, bass.ds(t, 1), 0:1].rearrange("p a f -> p (a f)"),
                                  cols(k.rstd, t, 1), ALU.subtract, ALU.mult).then_inc(finished, 1)
            over_tiles(dve, one)
            dve.wait_ge(finished, T)

        @block.scalar
        def _(act):
            act.wait_ge(vstep, 1)
            act.activation(k.rstd[:], given[:], ACT.Sqrt).then_inc(rooted, 1)

        @block.sync
        def _(sp):
            if out is not None:
                with sp.Fori(0, T - 1) as t:
                    sp.wait_ge(finished, t + 1)
                    sp.dma_start(out[bass.ds(t * P, P), :], tile_of(x, t)).then_inc(stored, 16)
                sp.wait_ge(finished, T)
                sp.dma_start(out[(T - 1) * P:N, :], x[0:NLAST, T - 1, :]).then_inc(stored, 16)
                sp.wait_ge(stored, 16 * T)


def load(nc, name, pairs):
    with ExitStack() as c:
        c.enter_context(nc.cleanup_on_exit())
        loaded = nc.alloc_semaphore(name + "loaded")
        block = c.enter_context(nc.Block())

        @block.sync
        def _(sp):
            for to, src in pairs:
                sp.dma_start(to, src).then_inc(loaded, 16)
            sp.wait_ge(loaded, 16 * len(pairs))


def halves(w):
    return w.rearrange("(a p) n -> p a n", p=P)


def attention_weights(nc, k, name, value, other, best, heads):
    with ExitStack() as c:
        c.enter_context(nc.cleanup_on_exit())
        sem = lambda n: nc.alloc_semaphore(name + n)
        vstep, ready, done = sem("vstep"), sem("ready"), sem("done")
        block = c.enter_context(nc.Block())
        flat = lambda a: a.rearrange("p s h -> p (s h)")
        v, b = flat(value[:]), flat(best[:])

        @block.vector
        def _(dve):
            step = Order(dve, vstep)
            if other is not None:
                o = flat(other[:])
                for a in (v, b):
                    step(dve.tensor_tensor(a, a, o, ALU.add))
                    step(dve.scalar_tensor_tensor(a, a, 0.2, a, ALU.mult, ALU.max))
            step(dve.tensor_tensor(v, v, b, ALU.subtract))
            dve.sem_inc(ready, 1)

        @block.scalar
        def _(act):
            act.wait_ge(ready, 1)
            act.activation(v, v, ACT.Exp).then_inc(done, 1)
            act.wait_ge(done, 1)


def graph_layers(nc, x, src, dst, edge_type_16, edge_weight1, L0_gnn_W, L0_gnn_b, L1_gnn_W_lin, L1_gnn_b_lin,
                 L1_gnn_W_gat, L1_gnn_attn_l, L1_gnn_attn_r, L1_gnn_gat_bias, L2_gnn_Wq, L2_gnn_bq, L2_gnn_Wk,
                 L2_gnn_bk, L2_gnn_Wv, L2_gnn_bv, L2_gnn_Ws, L2_gnn_bs, L2_gnn_Wl, L2_gnn_bl, L2_gnn_Wr,
                 L2_gnn_gamma, L2_gnn_beta, L2_gnn_alpha_res, L3_gnn_weight, out, debug=None):
    k = Bag()
    dram = lambda n, s, d=F32: nc.dram_tensor(n, s, d).ap()
    k.ordered = [dram(f"ordered{n}", (E + SE,), I32) for n in range(4)]
    k.slots = [dram(f"slots{n}", (2 * SE + 2 * P,), I32) for n in range(4)]
    k.sums = [dram(f"sums{n}", (NP + P, D)) for n in range(CH)]
    feat_d = dram("feat_d", (NP, D))
    el_d = dram("el_d", (NP, H))
    key_d = dram("key_d", (NP, D))
    value_d = dram("value_d", (NP, D))
    h_d = [dram(f"h_d{n}", (NP, D)) for n in range(3)]
    rel_d = dram("rel_d", (R, NP, D))

    with ExitStack() as c:
        sb = lambda n, s, d=F32: c.enter_context(nc.sbuf_tensor(n, s, d))
        k.passed = nc.alloc_semaphore("passed")
        k.X = sb("X", [P, T, D])
        k.iota = sb("iota", [P, P])
        k.ident = sb("ident", [P, P])
        k.low = sb("low", [P, P])
        k.pcol = sb("pcol", [P, 1])
        k.ones = sb("ones", [P, P])
        k.zero = sb("zero", [P, D + H])
        k.starts = sb("starts", [1, 2 * T + 1], I32)
        k.slot_tile = sb("slot_tile", [P, S + 1])
        k.slot_tile_i = sb("slot_tile_i", [1, S + 1], I32)
        k.deg_src = sb("deg_src", [P, T])
        k.edge_pad = sb("edge_pad", [1, P], I32)
        k.src, k.dst, k.rel, k.weight, k.node, k.dloc = (
            sb(n, [P, S]) for n in ("src", "dst", "rel", "weight", "node", "dloc"))
        k.src_i, k.rel_i = sb("src_i", [P, S], I32), sb("rel_i", [P, S], I32)
        k.rows_dst, k.rows_w, k.pen_prev, k.pen_next = (
            sb(n, [SQ, SG, P]) for n in ("rows_dst", "rows_w", "pen_prev", "pen_next"))
        k.six = sb("six", [P, 6])
        k.two = sb("two", [P, 2])
        k.mv = sb("mv", [P, T, 2])
        k.rstd = sb("rstd", [P, T])
        col = sb("col", [P, T])

        prepare(nc, k, x, src, dst)
        order_edges(nc, k, [src, dst, edge_type_16, edge_weight1.rearrange("e a -> (e a)").bitcast(I32)], dst)
        fill_slots(nc, k)

        with ExitStack() as l:
            sl = lambda n, s, d=F32: l.enter_context(nc.sbuf_tensor(n, s, d))
            w, b = sl("w0", [P, 2, D]), sl("b0", [P, D])
            load(nc, "l0", [(w[:], halves(L0_gnn_W)), (b[:], spread(L0_gnn_b))])
            inverse_root(nc, k, col)
            r = sl("r0", [P, T, D])
            scale_tiles(nc, r, k.X, col)
            if debug: debug(nc, 'y', r)
            sum_by_source(nc, k, r)
            z = sl("z0", [P, D])

            def epilogue(dve, step, t, p):
                step(dve.tensor_tensor(z[:], p[:, 0:D], b[:], ALU.add))
                step(dve.scalar_tensor_tensor(z[:], z[:], 0.2, z[:], ALU.mult, ALU.max))
                step(dve.tensor_tensor(tile_of(r, t), tile_of(k.X, t), z[:], ALU.add))
                statistics(dve, step, k, r, t)
            project(nc, k, "p0", [None], w, D, 6, epilogue, chains=[(a, col) for a in k.sums])
            normalize(nc, k, "n0", r, k.X)
            if debug: debug(nc, 'x1', k.X)

        with ExitStack() as l:
            sl = lambda n, s, d=F32: l.enter_context(nc.sbuf_tensor(n, s, d))
            h = sl("h1", [P, T, D])
            er = sl("er", [P, T, H])
            scores = sl("scores", [P, S, H])
            w, w2 = sl("w1", [P, 2, D]), sl("w1g", [P, 2, D])
            b, al, ar, gb = (sl(n, [P, D]) for n in ("b1", "al", "ar", "gb"))
            z = sl("z1", [P, D])
            load(nc, "l1", [(w[:], halves(L1_gnn_W_lin)), (w2[:], halves(L1_gnn_W_gat)), (b[:], spread(L1_gnn_b_lin)),
                            (al[:], spread(L1_gnn_attn_l.rearrange("h f -> (h f)"))),
                            (ar[:], spread(L1_gnn_attn_r.rearrange("h f -> (h f)"))),
                            (gb[:], spread(L1_gnn_gat_bias))])
            project(nc, k, "p1", [(k.X, None)], w, D, 1,
                    lambda dve, step, t, p: step(dve.tensor_tensor(tile_of(h, t), p[:, 0:D], b[:], ALU.add)))
            with ExitStack() as f:
                feat = f.enter_context(nc.sbuf_tensor("feat", [P, T, D], F32))
                el = f.enter_context(nc.sbuf_tensor("el", [P, T, H], F32))

                def epilogue(dve, step, t, p):
                    step(dve.tensor_copy(tile_of(feat, t), p[:, 0:D]))
                    for a, to in ((al, el), (ar, er)):
                        step(dve.tensor_tensor(z[:], tile_of(feat, t), a[:], ALU.mult))
                        step(dve.tensor_reduce(tile_of(to, t), z[:].rearrange("p (h f) -> p h f", h=H), AX.X, ALU.add))
                project(nc, k, "p2", [(h, None)], w2, D, 5, epilogue, stores=[(feat, feat_d)])
                load(nc, "s2", [(el_d.rearrange("(t p) h -> p t h", p=P), el[:])])
            with ExitStack() as f:
                part = f.enter_context(nc.sbuf_tensor("er_edge", [P, S, H], F32))
                score_by_edge(nc, k, "a1", el_d, H, er, scores, part)
                best = f.enter_context(nc.sbuf_tensor("best", [P, S, H], F32))
                segment_maximum(nc, k, "m1", H, scores, best)
                attention_weights(nc, k, "w1", scores, part, best, H)
            with ExitStack() as f:
                k.acc = f.enter_context(nc.sbuf_tensor("acc1", [P, T, D + H], F32))
                sum_by_destination(nc, k, "e1", feat_d, k.src_i, per_head=scores)
                rs = f.enter_context(nc.sbuf_tensor("rs1", [P, T, H], F32))

                def before(dve, step):
                    step(dve.tensor_scalar(rs[:], k.acc[:, :, D:D + H], 1e-30, None, ALU.max))
                    step(dve.reciprocal(rs[:], rs[:]))

                def work(dve, step, t):
                    a = k.acc[:, bass.ds(t, 1), 0:D].rearrange("p a f -> p (a f)")
                    step(dve.tensor_tensor(z[:].rearrange("p (h f) -> p h f", h=H), a.rearrange("p (h f) -> p h f", h=H),
                                           tile_of(rs, t).unsqueeze(2).broadcast_to([P, H, HD]), ALU.mult))
                    step(dve.tensor_tensor(z[:], z[:], gb[:], ALU.add))
                    step(dve.scalar_tensor_tensor(z[:], z[:], 0.01, z[:], ALU.mult, ALU.max))
                    step(dve.tensor_tensor(tile_of(h, t), tile_of(h, t), z[:], ALU.add))
                    step(dve.tensor_tensor(tile_of(h, t), tile_of(h, t), tile_of(k.X, t), ALU.add))
                    statistics(dve, step, k, h, t)
                each_tile(nc, k, "t1", 8, before, work)
                normalize(nc, k, "n1", h, k.X)
            if debug: debug(nc, 'x2', k.X)

        with ExitStack() as l:
            sl = lambda n, s, d=F32: l.enter_context(nc.sbuf_tensor(n, s, d))
            h = sl("h2", [P, T, D])
            lg = sl("lg", [P, S, 1])
            z = sl("z2", [P, D])
            sage = [[sl(f"{n}{i}", [P, D]) for n in ("ga", "be", "bl")] for i in range(3)]
            wlr = [sl(f"wlr{i}", [P, 4, D]) for i in range(3)]
            alpha = sl("alpha", [P, 2])
            load(nc, "l2", [(alpha[:, 0:1], spread(L2_gnn_alpha_res))]
                 + [p for i in range(3) for p in (
                     (sage[i][0][:], spread(L2_gnn_gamma[i, :])), (sage[i][1][:], spread(L2_gnn_beta[i, :])),
                     (sage[i][2][:], spread(L2_gnn_bl[i, :])), (wlr[i][:, 0:2, :], halves(L2_gnn_Wl[i, :, :])),
                     (wlr[i][:, 2:4, :], halves(L2_gnn_Wr[i, :, :])))])
            with ExitStack() as f:
                q = f.enter_context(nc.sbuf_tensor("q2", [P, T, D], F32))
                with ExitStack() as g:
                    sg = lambda n, s: g.enter_context(nc.sbuf_tensor(n, s, F32))
                    kk, vv, w, b = sg("kk", [P, T, D]), sg("vv", [P, T, D]), sg("w2", [P, 2, 4 * D]), sg("b2", [P, 4 * D])
                    load(nc, "l3", [p for i, (m, v) in enumerate(((L2_gnn_Wq, L2_gnn_bq), (L2_gnn_Wk, L2_gnn_bk),
                                                                 (L2_gnn_Wv, L2_gnn_bv), (L2_gnn_Ws, L2_gnn_bs)))
                                    for p in ((w[:, :, i * D:(i + 1) * D], halves(m)),
                                              (b[:, i * D:(i + 1) * D], spread(v)))])

                    def epilogue(dve, step, t, p):
                        for i, to in enumerate((q, kk, vv, h)):
                            step(dve.tensor_tensor(tile_of(to, t), p[:, i * D:(i + 1) * D], b[:, i * D:(i + 1) * D], ALU.add))
                    project(nc, k, "p3", [(k.X, None)], w, 4 * D, 4, epilogue, stores=[(kk, key_d), (vv, value_d)])
                score_by_edge(nc, k, "a2", key_d, D, q, lg[:].rearrange("p s a -> p (s a)"), None)
            with ExitStack() as f:
                best = f.enter_context(nc.sbuf_tensor("best2", [P, S, 1], F32))
                segment_maximum(nc, k, "m2", 1, lg, best)
                attention_weights(nc, k, "w2", lg, None, best, 1)
            k.acc = sl("acc2", [P, T, D + 1])
            sum_by_destination(nc, k, "e2", value_d, k.src_i, weight=lg[:].rearrange("p s a -> p (s a)"), ones=True)

            def before(dve, step):
                step(dve.tensor_scalar(col[:], k.acc[:, :, D], 1e-30, None, ALU.max))
                step(dve.reciprocal(col[:], col[:]))

            def work(dve, step, t):
                a = k.acc[:, bass.ds(t, 1), 0:D].rearrange("p a f -> p (a f)")
                step(dve.scalar_tensor_tensor(tile_of(h, t), a, cols(col, t, 1), tile_of(h, t), ALU.mult, ALU.add))
                step(dve.tensor_scalar(tile_of(h, t), tile_of(h, t), 0.0, None, ALU.max))
            each_tile(nc, k, "t2", 2, before, work, stores=[(h, h_d[0])])
            if debug: debug(nc, 'h0', h)
            fold_scales(nc, alpha, sage)
            for i in range(3):
                sum_by_destination(nc, k, f"e{3 + i}", h_d[i], k.src_i, ones=i == 0)
                if i == 0:
                    inverse_count(nc, k, col)
                ga, be, _ = sage[i]

                def epilogue(dve, step, t, p, ga=ga, be=be, last=i == 2):
                    step(dve.tensor_tensor(z[:], p[:, 0:D], ga[:], ALU.mult))
                    step(dve.tensor_tensor(z[:], z[:], be[:], ALU.add))
                    step(dve.scalar_tensor_tensor(z[:], tile_of(h, t), alpha[:, 1:2], z[:], ALU.mult, ALU.add))
                    if last:
                        step(dve.scalar_tensor_tensor(tile_of(h, t), z[:], 0.0, tile_of(k.X, t), ALU.max, ALU.add))
                        statistics(dve, step, k, h, t)
                    else:
                        step(dve.tensor_scalar(tile_of(h, t), z[:], 0.0, None, ALU.max))
                project(nc, k, f"p{4 + i}", [(k.acc, col), (h, None)], wlr[i], D, 7 if i == 2 else 4, epilogue,
                        stores=[] if i == 2 else [(h, h_d[i + 1])])
            normalize(nc, k, "n2", h, k.X)
            if debug: debug(nc, 'x3', k.X)

        with ExitStack() as l:
            sl = lambda n, s, d=F32: l.enter_context(nc.sbuf_tensor(n, s, d))
            with ExitStack() as f:
                w = f.enter_context(nc.sbuf_tensor("w3", [P, 2, R, D], F32))
                load(nc, "l4", [(w[:, a, :, :], L3_gnn_weight[:, a * P:(a + 1) * P, :].rearrange("r p n -> p r n"))
                                for a in range(2)])
                relation_tables(nc, k, w, rel_d)
            k.acc = sl("acc3", [P, T, D])
            sum_by_destination(nc, k, "e7", rel_d.rearrange("r n f -> (r n) f"), k.rel_i, weight=k.weight)

            def work(dve, step, t):
                step(dve.tensor_tensor(tile_of(k.acc, t), tile_of(k.acc, t), tile_of(k.X, t), ALU.add))
                statistics(dve, step, k, k.acc, t)
            each_tile(nc, k, "t3", 4, lambda dve, step: None, work)
            normalize(nc, k, "n3", k.acc, k.X, out)


def inverse_root(nc, k, col):
    with ExitStack() as c:
        c.enter_context(nc.cleanup_on_exit())
        vstep, rooted = nc.alloc_semaphore("r_v"), nc.alloc_semaphore("r_r")
        safe, given, square = (c.enter_context(nc.sbuf_tensor(n, [P, T], F32)) for n in ("safe", "given", "square"))
        block = c.enter_context(nc.Block())

        @block.vector
        def _(dve):
            step = Order(dve, vstep)
            step(dve.tensor_scalar(given[:], k.deg_src[:], 1.0, None, ALU.max))
            dve.wait_ge(rooted, 1)
            refine_root(dve, step, safe[:], given[:], square[:])
            step(dve.tensor_scalar(col[:], k.deg_src[:], 1.0, None, ALU.min))
            step(dve.tensor_tensor(col[:], col[:], safe[:], ALU.mult))

        @block.scalar
        def _(act):
            act.wait_ge(vstep, 1)
            act.activation(safe[:], given[:], ACT.Sqrt).then_inc(rooted, 1)


def inverse_count(nc, k, col):
    with ExitStack() as c:
        c.enter_context(nc.cleanup_on_exit())
        vstep = nc.alloc_semaphore("c_v")
        block = c.enter_context(nc.Block())

        @block.vector
        def _(dve):
            step = Order(dve, vstep)
            step(dve.tensor_scalar(col[:], k.acc[:, :, D], 1.0, None, ALU.max))
            step(dve.reciprocal(col[:], col[:]))


def fold_scales(nc, alpha, sage):
    with ExitStack() as c:
        c.enter_context(nc.cleanup_on_exit())
        vstep, sig = nc.alloc_semaphore("f_v"), nc.alloc_semaphore("f_s")
        block = c.enter_context(nc.Block())

        @block.scalar
        def _(act):
            act.activation(alpha[:, 0:1], alpha[:, 0:1], ACT.Sigmoid).then_inc(sig, 1)

        @block.vector
        def _(dve):
            step = Order(dve, vstep)
            dve.wait_ge(sig, 1)
            step(dve.tensor_scalar(alpha[:, 1:2], alpha[:, 0:1], -1.0, 1.0, ALU.mult, ALU.add))
            for ga, be, bl in sage:
                step(dve.tensor_scalar(ga[:], ga[:], BN_SCALE, alpha[:, 0:1], ALU.mult, ALU.mult))
                step(dve.tensor_scalar(be[:], be[:], alpha[:, 0:1], None, ALU.mult))
                step(dve.tensor_tensor(bl[:], bl[:], ga[:], ALU.mult))
                step(dve.tensor_tensor(be[:], be[:], bl[:], ALU.add))


def scale_tiles(nc, to, x, col):
    with ExitStack() as c:
        c.enter_context(nc.cleanup_on_exit())
        done = nc.alloc_semaphore("sc_done")
        block = c.enter_context(nc.Block())

        @block.vector
        def _(dve):
            over_tiles(dve, lambda t, b: dve.tensor_scalar(tile_of(to, t), tile_of(x, t), cols(col, t, 1), None,
                                                           ALU.mult).then_inc(done, 1))
            dve.wait_ge(done, T)


def relation_tables(nc, k, w, rel_d):
    RP = R // 2
    with ExitStack() as c:
        c.enter_context(nc.cleanup_on_exit())
        sb = lambda n, s, d=F32: c.enter_context(nc.sbuf_tensor("q_" + n, s, d))
        sem = lambda n: nc.alloc_semaphore("q_" + n)
        xs = sb("xs", [P, 2, D])
        xt = sb("xt", [P, 2, 2, P])
        rows = sb("rows", [P, 2, R, D])
        flips = c.enter_context(nc.psum_tensor("q_flips", [P, 2, 512], F32))
        prods = c.enter_context(nc.psum_tensor("q_prods", [P, 4, 512], F32))
        staged, flipped, turned, multiplied, kept_a, kept_v = (
            sem("staged"), sem("flipped"), sem("turned"), sem("multiplied"), sem("kept_a"), sem("kept_v"))
        stored = [sem(f"stored{b}") for b in range(2)]
        block = c.enter_context(nc.Block())

        @block.sync
        def _(sp):
            def store(t, b):
                sp.wait_ge(kept_a, t * (RP // 2) + RP // 2 + 2)
                sp.wait_ge(kept_v, t * (RP // 2) + RP // 2 + 2)
                sp.dma_start(rel_d[:, bass.ds(t * P, P), :].rearrange("r p f -> p r f"), rows[:, b, :, :]).then_inc(stored[b], 16)
            over_tiles(sp, store)
            sp.wait_ge(stored[0], 16 * (T // 2 + 1))
            sp.wait_ge(stored[1], 16 * (T // 2))

        @block.tensor
        def _(pe):
            pe.sem_inc(flipped, 2)

            def tile(t, b):
                pe.wait_ge(staged, t + 1)
                pe.wait_ge(turned, t + 1)
                for h in range(2):
                    last = pe.transpose(flips[:, b, h * P:(h + 1) * P], xs[:, b, h * P:(h + 1) * P], k.ident[:])
                last.then_inc(flipped, 1)
                pe.wait_ge(turned, t + 3)
                for o in range(RP):
                    pe.wait_ge(kept_a if o % 2 == 0 else kept_v, t * (RP // 2) + o // 2 + 1)
                    for a in range(2):
                        last = pe.matmul(prods[:, o % 4, :], xt[:, b, a, :],
                                         w[:, a, 2 * o:2 * o + 2, :].rearrange("p r n -> p (r n)"),
                                         start=a == 0, stop=a == 1)
                    last.then_inc(multiplied, 1)
            over_tiles(pe, tile)

        @block.scalar
        def _(act):
            act.sem_inc(turned, 2)
            act.sem_inc(kept_a, 2)

            def stage(t, b):
                act.wait_ge(flipped, t + 1)
                act.sem_inc(k.passed, 1)
                act.copy(xs[:, b, :], tile_of(k.X, t)).then_inc(staged, 1)

            def tile(t, b):
                act.wait_ge(flipped, t + 3)
                act.copy(xt[:, b, :, :].rearrange("p a q -> p (a q)"), flips[:, b, 0:D]).then_inc(turned, 1)
                if reused(t):
                    act.wait_ge(stored[b], (t - b) * 8)
                for o in range(0, RP, 2):
                    act.wait_ge(multiplied, t * RP + o + 1)
                    act.copy(rows[:, b, 2 * o:2 * o + 2, :].rearrange("p r n -> p (r n)"),
                             prods[:, o % 4, :]).then_inc(kept_a, 1)
            stage(0, 0)
            stage(1, 1)
            tile(0, 0)
            stage(2, 0)
            tile(1, 1)
            with act.Fori(1, T // 2) as i:
                stage(2 * i + 1, 1)
                tile(2 * i, 0)
                stage(2 * i + 2, 0)
                tile(2 * i + 1, 1)
            tile(T - 1, 0)

        @block.vector
        def _(dve):
            dve.sem_inc(kept_v, 2)

            def tile(t, b):
                if reused(t):
                    dve.wait_ge(stored[b], (t - b) * 8)
                for o in range(1, RP, 2):
                    dve.wait_ge(multiplied, t * RP + o + 1)
                    dve.tensor_copy(rows[:, b, 2 * o:2 * o + 2, :].rearrange("p r n -> p (r n)"),
                                    prods[:, o % 4, :]).then_inc(kept_v, 1)
            over_tiles_after_two(dve, tile)


_INS = ['x', 'src', 'dst', 'edge_type_16', 'edge_weight1', 'L0_gnn_W', 'L0_gnn_b', 'L1_gnn_W_lin', 'L1_gnn_b_lin',
        'L1_gnn_W_gat', 'L1_gnn_attn_l', 'L1_gnn_attn_r', 'L1_gnn_gat_bias', 'L2_gnn_Wq', 'L2_gnn_bq', 'L2_gnn_Wk',
        'L2_gnn_bk', 'L2_gnn_Wv', 'L2_gnn_bv', 'L2_gnn_Ws', 'L2_gnn_bs', 'L2_gnn_Wl', 'L2_gnn_bl', 'L2_gnn_Wr',
        'L2_gnn_gamma', 'L2_gnn_beta', 'L2_gnn_alpha_res', 'L3_gnn_weight']


def kernel(**inputs):
    import concourse.bacc as _bacc
    from concourse.bass_utils import run_bass_kernel_spmd as _run

    nc = _bacc.Bacc("TRN2", target_bir_lowering=False, num_devices=1)
    arrays, args = {}, {}
    for name in _INS:
        a = np.ascontiguousarray(inputs[name])
        if a.ndim == 0:
            a = a.reshape(1)
        arrays[f"in_{name}"] = a
        args[name] = nc.dram_tensor(f"in_{name}", a.shape, mybir.dt.from_np(a.dtype), kind="ExternalInput").ap()
    out = nc.dram_tensor("out_0", (N, D), F32, kind="ExternalOutput").ap()
    graph_layers(nc, out=out, **args)
    r = _run(nc, [arrays], core_ids=[0])
    return r.results[0]["out_0"]
```

```python
from contextlib import ExitStack

import numpy as np
import concourse.bass as bass
from concourse import mybir

F32 = mybir.dt.float32
BF16 = mybir.dt.bfloat16
F16 = mybir.dt.float16
I32 = mybir.dt.int32
ALU = mybir.AluOpType
ACT = mybir.ActivationFunctionType
AX = mybir.AxisListType

P = 128
N = 3125
D = 256
E = 50000
H = 8
HD = D // H
R = 16
T = (N + P - 1) // P
NP = T * P
NLAST = N - (T - 1) * P
EP = 125
EC = E // EP
U = 16
IT = -(-(E // P + T) // U)
S = IT * U
SE = S * P
SG = 4
SQ = S // SG
RING = 8
G4 = 4
CH = 4
NTRASH = NP
BIG = 1.0e30
PAD_DST = float(1 << 20)
LN_EPS = 1e-5
BN_SCALE = 1.0 / float(np.sqrt(1.0 + 1e-5))


class Bag:
    pass


class Order:

    def __init__(self, eng, sem, base=0):
        self.eng, self.sem, self.n = eng, sem, base

    def __call__(self, ins):
        ins.then_inc(self.sem, 1)
        self.n = self.n + 1
        self.eng.wait_ge(self.sem, self.n)


def cols(ap, start, count):
    return ap[:, bass.ds(start, count)]


def tile_of(ap, t):
    return ap[:, bass.ds(t, 1), :].rearrange("p a f -> p (a f)")


def over_tiles(eng, body):
    with eng.Fori(0, T // 2) as i:
        body(2 * i, 0)
        body(2 * i + 1, 1)
    body(T - 1, 0)


def over_tiles_after_two(eng, body):
    body(0, 0)
    body(1, 1)
    with eng.Fori(1, T // 2) as i:
        body(2 * i, 0)
        body(2 * i + 1, 1)
    body(T - 1, 0)


def reused(t):
    return not isinstance(t, int) or t >= 2


def spread(ap, p=P):
    return bass.AP(ap.tensor, ap.offset, [[0, p]] + [list(x) for x in ap.ap])



def prepare(nc, k, x, src, dst):
    with ExitStack() as c:
        c.enter_context(nc.cleanup_on_exit())
        sb = lambda n, s, d=F32: c.enter_context(nc.sbuf_tensor("p_" + n, s, d))
        sem = lambda n: nc.alloc_semaphore("p_" + n)
        dn = sb("dn", [EP, EC], I32)
        nxt = sb("nxt", [EP, 1], I32)
        sn = sb("sn", [EP, EC], I32)
        bits = sb("bits", [EP, EC], I32)
        dtile = sb("dtile", [EP, EC])
        junk = sb("junk", [EP, EC])
        junk2 = sb("junk2", [EP, EC])
        per = sb("per", [EP, T + 2])
        row = sb("row", [1, 8, T + 2])
        rowi = sb("rowi", [1, 2, T + 2], I32)
        ends = sb("ends", [T, 1])
        ioj = sb("ioj", [T, S + 1])
        cmpj = sb("cmpj", [T, S + 1])
        ends_all = sb("ends_all", [T, T])
        turns, group_turns = sb("turns", [1, S]), sb("group_turns", [1, S // 4])
        small = c.enter_context(nc.psum_tensor("small", [P, 512], F32))
        mapp = c.enter_context(nc.psum_tensor("mapp", [P, 512], F32))
        x_in, e_in, zeroed = sem("x_in"), sem("e_in"), sem("zeroed")
        made, vstep, pstep = sem("made"), sem("vstep"), sem("pstep")
        counted = sem("counted")
        sums, rowed, mapped = sem("sums"), sem("rowed"), sem("mapped")
        block = c.enter_context(nc.Block())

        @block.sync
        def _(sp):
            sp.dma_start(sn[:], src.rearrange("(p c) -> p c", c=EC)).then_inc(e_in, 16)
            sp.dma_start(dn[:], dst.rearrange("(p c) -> p c", c=EC)).then_inc(e_in, 16)
            sp.wait_ge(zeroed, 1)
            sp.dma_start(nxt[0:EP - 1, :], dst.rearrange("(p c) -> p c", c=EC)[1:EP, 0:1],
                         allow_slow_non_contiguous=True).then_inc(e_in, 16)
            sp.dma_start(k.X[:, 0:T - 1, :], x[0:(T - 1) * P, :].rearrange("(t p) f -> p t f", p=P)).then_inc(x_in, 16)
            sp.wait_ge(zeroed, 2)
            sp.dma_start(k.X[0:NLAST, T - 1, :], x[(T - 1) * P:N, :]).then_inc(x_in, 16)
            sp.wait_ge(x_in, 32)

        @block.gpsimd
        def _(pool):
            step = Order(pool, pstep)
            pool.memset(nxt[:], NP).then_inc(zeroed, 1)
            pool.memset(k.X[:, T - 1, :], 0.0).then_inc(zeroed, 1)
            pool.iota(k.iota[:], [[1, P]], base=0, channel_multiplier=0,
                      allow_small_or_imprecise_dtypes=True).then_inc(made, 1)
            pool.iota(k.iota_b[:], [[1, P]], base=0, channel_multiplier=0,
                      allow_small_or_imprecise_dtypes=True).then_inc(made, 1)
            pool.iota(k.pcol[:], [[1, 1]], base=0, channel_multiplier=1,
                      allow_small_or_imprecise_dtypes=True).then_inc(made, 1)
            pool.iota(ioj[:], [[1, S + 1]], base=-1, channel_multiplier=0,
                      allow_small_or_imprecise_dtypes=True).then_inc(made, 1)
            pool.memset(k.ones[:], 1.0).then_inc(made, 1)
            pool.memset(k.zero_b[:], 0.0).then_inc(made, 1)
            pool.memset(k.zero[:], 0.0).then_inc(made, 1)
            step(pool.memset(k.ident[:], 0.0))
            pool.affine_select(out=k.ident[:], in_=k.ident[:], compare_op=ALU.not_equal, fill=1.0, base=0,
                               pattern=[[-1, P]], channel_multiplier=1).then_inc(made, 1)

        @block.vector
        def _(dve):
            step = Order(dve, vstep)
            dve.wait_ge(made, 8)
            dve.tensor_scalar(k.low[:], k.iota[:], k.pcol[:, 0:1], None, ALU.is_lt).then_inc(vstep, 1)
            dve.memset(per[:], 0.0).then_inc(vstep, 1)
            step.n = 2
            dve.wait_ge(vstep, 2)
            dve.wait_ge(e_in, 48)
            step(dve.tensor_single_scalar(bits[:], sn[:], P - 1, ALU.bitwise_and))
            step(dve.tensor_copy(k.slo[:], bits[:]))
            step(dve.tensor_single_scalar(bits[:], sn[:], 7, ALU.arith_shift_right))
            step(dve.tensor_copy(k.shi[:], bits[:]))
            step(dve.tensor_single_scalar(bits[:], dn[:], 7, ALU.arith_shift_right))
            step(dve.tensor_copy(dtile[:], bits[:]))
            for t in range(T):
                step(dve.tensor_scalar(junk[:], dtile[:], float(t), 0.0, ALU.is_equal, ALU.add,
                                       accum_out=per[:, t:t + 1]))
            step(dve.tensor_tensor(junk2[:, 0:EC - 1], dn[:, 1:EC], dn[:, 0:EC - 1], ALU.is_lt))
            step(dve.tensor_tensor(junk2[:, EC - 1:EC], nxt[:], dn[:, EC - 1:EC], ALU.is_lt))
            step(dve.tensor_reduce(per[:, T:T + 1], junk2[:], AX.X, ALU.add))
            dve.sem_inc(sums, 1)
            dve.wait_ge(counted, 1)
            step(dve.tensor_copy(row[0:1, 0, :], small[0:1, 0:T + 2]))
            step(dve.tensor_scalar(row[0:1, 1, :], row[0:1, 0, :], float(P - 1), None, ALU.add))
            step(dve.tensor_copy(rowi[0:1, 0, :], row[0:1, 1, :]))
            step(dve.tensor_single_scalar(rowi[0:1, 1, :], rowi[0:1, 0, :], 7, ALU.arith_shift_right))
            step(dve.tensor_copy(row[0:1, 2, :], rowi[0:1, 1, :]))
            step(dve.tensor_scalar(row[0:1, 2, :], row[0:1, 2, :], 1.0, None, ALU.max))
            step(dve.tensor_tensor_scan(row[0:1, 3, 0:T], k.zero[0:1, 0:T], row[0:1, 0, 0:T], 0.0, ALU.add, ALU.add))
            step(dve.tensor_tensor_scan(row[0:1, 4, 0:T], k.zero[0:1, 0:T], row[0:1, 2, 0:T], 0.0, ALU.add, ALU.add))
            step(dve.tensor_tensor(row[0:1, 5, 0:T], row[0:1, 3, 0:T], row[0:1, 0, 0:T], ALU.subtract))
            step(dve.tensor_tensor(row[0:1, 6, 0:T], row[0:1, 4, 0:T], row[0:1, 2, 0:T], ALU.subtract))
            step(dve.tensor_scalar(row[0:1, 6, 0:T], row[0:1, 6, 0:T], float(P), None, ALU.mult))
            step(dve.tensor_copy(k.starts[0:1, 0:T], row[0:1, 5, 0:T]))
            step(dve.tensor_copy(k.starts[0:1, T:2 * T], row[0:1, 6, 0:T]))
            step(dve.tensor_scalar(row[0:1, 7, 0:1], row[0:1, 0, T:T + 1], 1.0, None, ALU.min))
            step(dve.tensor_copy(k.starts[0:1, 2 * T:2 * T + 1], row[0:1, 7, 0:1]))
            dve.sem_inc(rowed, 1)
            dve.wait_ge(counted, 2)
            step(dve.tensor_copy(ends[:], small[0:T, 64:65]))
            step(dve.tensor_scalar(cmpj[:], ioj[:], ends[:, 0:1], None, ALU.is_ge))
            dve.sem_inc(mapped, 1)
            dve.wait_ge(counted, 3)
            step(dve.tensor_scalar(k.slot_tile[:], mapp[:, 0:S + 1], float(T - 1), None, ALU.min))
            step(dve.tensor_copy(k.slot_tile_i[0:1, :], k.slot_tile[0:1, :]))
            step(dve.tensor_tensor(turns[:], k.slot_tile[0:1, 1:S + 1], k.slot_tile[0:1, 0:S], ALU.not_equal))
            step(dve.tensor_copy(k.turns_i[:], turns[:]))
            step(dve.tensor_reduce(group_turns[:], turns[:].rearrange("p (g u) -> p g u", u=4), AX.X, ALU.add))
            step(dve.tensor_copy(k.group_turns_i[:], group_turns[:]))

        @block.tensor
        def _(pe):
            pe.wait_ge(made, 8)
            pe.wait_ge(sums, 1)
            pe.matmul(small[0:1, 0:T + 2], k.ones[0:EP, 0:1], per[:], start=True, stop=True).then_inc(counted, 1)
            pe.wait_ge(rowed, 1)
            pe.matmul(small[0:T, 64:65], row[0:1, 4, 0:T], k.ones[0:1, 0:1], start=True, stop=True).then_inc(counted, 1)
            pe.wait_ge(mapped, 1)
            pe.matmul(mapp[:, 0:S + 1], k.ones[0:T, :], cmpj[:], start=True, stop=True).then_inc(counted, 1)


def order_edges(nc, k, fields, dst):
    with ExitStack() as c:
        c.enter_context(nc.cleanup_on_exit())
        sb = lambda n, s, d=F32: c.enter_context(nc.sbuf_tensor("o_" + n, s, d))
        sem = lambda n: nc.alloc_semaphore("o_" + n)
        padi = sb("padi", [P, SE // P], I32)
        padz = sb("padz", [P, SE // P], I32)
        dni = sb("dni", [EP, EC], I32)
        dnf = sb("dnf", [EP, EC])
        en = sb("en", [EP, EC])
        BK = EP * 25
        NB = E // BK
        keys = sb("keys", [EP, BK], I32)
        keyf = sb("keyf", [EP, BK])
        place = sb("place", [EP, BK])
        before = sb("before", [EP, BK])
        hit = sb("hit", [EP, BK])
        two = sb("two", [EP, 2])
        rank = sb("rank", [EP, EC])
        ranki = sb("ranki", [EP, EC], I32)
        rk1 = sb("rk1", [EP, 1], I32)
        fl = [sb(f"fl{n}", [EP, EC], I32) for n in range(4)]
        f1 = sb("f1", [EP, 4], I32)
        padded, pads, copied = sem("padded"), sem("pads"), sem("copied")
        iot, keyed, vstep, ranked, put = sem("iot"), sem("keyed"), sem("vstep"), sem("ranked"), sem("put")
        bl, fields_in, pstep = sem("bl"), sem("fields_in"), sem("pstep")
        block = c.enter_context(nc.Block())

        @block.sync
        def _(sp):
            unordered = sp.value_load(k.starts[0:1, 2 * T:2 * T + 1], min_val=0, max_val=1)
            sp.wait_ge(padded, 2)
            for f in range(4):
                sp.dma_start(k.ordered[f][E:E + SE].rearrange("(p c) -> p c", p=P),
                             (padi if f == 1 else padz)[:]).then_inc(pads, 16)
            with sp.If(unordered == 0):
                for f in range(4):
                    sp.dma_start(k.ordered[f][0:E].rearrange("(a b) -> a b", a=16),
                                 fields[f].rearrange("(a b) -> a b", a=16)).then_inc(copied, 16)
                sp.wait_ge(copied, 64)
            with sp.If(unordered != 0):
                sp.dma_start(dni[:], dst.rearrange("(p c) -> p c", c=EC)).then_inc(fields_in, 16)
                for f in range(4):
                    sp.dma_start(fl[f][:], fields[f].rearrange("(p c) -> p c", c=EC)).then_inc(fields_in, 16)
                with sp.Fori(0, NB) as b:
                    sp.wait_ge(bl, b + 1)
                    sp.dma_start(keys[:],
                                 bass.AP(dst.tensor, 0, [[0, EP], [1, E]])[:, bass.ds(b * BK, BK)]).then_inc(keyed, 16)
                sp.wait_ge(bl, NB + 1)
            sp.wait_ge(pads, 64)

        @block.gpsimd
        def _(pool):
            unordered = pool.value_load(k.starts[0:1, 2 * T:2 * T + 1], min_val=0, max_val=1)
            step = Order(pool, pstep)
            pool.memset(padi[:], int(PAD_DST)).then_inc(padded, 1)
            pool.memset(padz[:], 0).then_inc(padded, 1)
            with pool.If(unordered != 0):
                pool.iota(en[:], [[1, EC]], base=0, channel_multiplier=EC,
                          allow_small_or_imprecise_dtypes=True).then_inc(iot, 1)
                pool.iota(place[:], [[1, BK]], base=0, channel_multiplier=0,
                          allow_small_or_imprecise_dtypes=True).then_inc(iot, 1)
                pool.wait_ge(ranked, 1)
                pool.wait_ge(fields_in, 80)
                with pool.Fori(0, EC) as i:
                    step.n = i * 5
                    step(pool.tensor_copy(rk1[:], cols(ranki, i, 1)))
                    for f in range(4):
                        step(pool.tensor_copy(f1[:, f:f + 1], cols(fl[f], i, 1)))
                    for f in range(4):
                        pool.sem_inc(k.passed, 1)
                        pool.indirect_dma_start(k.ordered[f].rearrange("(e a) -> e a", a=1),
                                                bass.IndirectOffsetOnAxis(ap=rk1[:, 0:1], axis=0),
                                                f1[:, f:f + 1], None).then_inc(put, 16)
                    pool.wait_ge(put, i * 64 + 64)
                    pool.sem_inc(k.passed, 1)

        @block.vector
        def _(dve):
            unordered = dve.value_load(k.starts[0:1, 2 * T:2 * T + 1], min_val=0, max_val=1)
            with dve.If(unordered != 0):
                step = Order(dve, vstep)
                dve.sem_inc(bl, 1)
                dve.wait_ge(fields_in, 80)
                dve.wait_ge(iot, 2)
                step(dve.tensor_copy(dnf[:], dni[:]))
                step(dve.memset(rank[:], 0.0))
                with dve.Fori(0, NB) as b:
                    step.n = 2 + b * (2 + EC * 5)
                    dve.wait_ge(keyed, b * 16 + 16)
                    step(dve.tensor_copy(keyf[:], keys[:]))
                    dve.sem_inc(k.passed, 1)
                    with dve.Fori(0, EC) as i:
                        step.n = 3 + b * (2 + EC * 5) + i * 5
                        step(dve.tensor_scalar(hit[:], keyf[:], cols(dnf, i, 1), 0.0, ALU.is_lt, ALU.add,
                                               accum_out=two[:, 0:1]))
                        step(dve.tensor_scalar(before[:], place[:], cols(en, i, 1), None, ALU.is_lt))
                        step(dve.scalar_tensor_tensor(hit[:], keyf[:], cols(dnf, i, 1), before[:], ALU.is_equal,
                                                      ALU.mult, accum_out=two[:, 1:2]))
                        step(dve.tensor_tensor(cols(rank, i, 1), cols(rank, i, 1), two[:, 0:1], ALU.add))
                        step(dve.tensor_tensor(cols(rank, i, 1), cols(rank, i, 1), two[:, 1:2], ALU.add))
                        dve.sem_inc(k.passed, 1)
                    step.n = 3 + b * (2 + EC * 5) + EC * 5
                    step(dve.tensor_scalar(en[:], en[:], float(-BK), None, ALU.add))
                    dve.sem_inc(bl, 1)
                dve.tensor_copy(ranki[:], rank[:]).then_inc(ranked, 1)


def fill_slots(nc, k):
    with ExitStack() as c:
        c.enter_context(nc.cleanup_on_exit())
        sb = lambda n, s, d=F32: c.enter_context(nc.sbuf_tensor("f_" + n, s, d))
        sem = lambda n: nc.alloc_semaphore("f_" + n)
        rows_i = sb("rows_i", [SQ, 2, SG, P], I32)
        rows_t = sb("rows_t", [SQ, SG, P], I32)
        rows_f = sb("rows_f", [SQ, 2, SG, P])
        rows_p = sb("rows_p", [SQ, SG, P], I32)
        rows_n = sb("rows_n", [SQ, SG, P], I32)
        shifted = sb("shifted", [SQ, SG, P])
        lob = sb("lob", [EP, 8, P], BF16)
        hib = sb("hib", [EP, 8, T], BF16)
        flips = c.enter_context(nc.psum_tensor("flips", [P, 4, 512], F32))
        hist = c.enter_context(nc.psum_tensor("hist", [P, 512], F32))
        hot, used, cleared = sem("hot"), sem("used"), sem("cleared")
        laid, rows, vstep, turned, flipped, kept = (sem("laid"), sem("rows"), sem("vstep"), sem("turned"),
                                                    sem("flipped"), sem("kept"))
        ends_in, pstep = sem("ends_in"), sem("pstep")
        block = c.enter_context(nc.Block())

        @block.sync
        def _(sp):
            sp.wait_ge(ends_in, 32)
            for t in range(T):
                first = sp.value_load(k.starts[0:1, t:t + 1], min_val=0, max_val=E)
                place = sp.value_load(k.starts[0:1, T + t:T + t + 1], min_val=0, max_val=SE)
                for f in range(4):
                    sp.dma_start(k.slots[f][bass.ds(place + P, SE)].rearrange("(a b) -> a b", a=16),
                                 k.ordered[f][bass.ds(first, SE)].rearrange("(a b) -> a b", a=16)).then_inc(laid, 16)
                sp.wait_ge(laid, 64 * (t + 1))
            flat = lambda f, o: k.slots[f][o:o + SE].rearrange("(g q p) -> q g p", q=SQ, p=P)
            sp.dma_start(rows_i[:, 0, :, :], flat(0, P)).then_inc(rows, 16)
            sp.dma_start(rows_i[:, 1, :, :], flat(1, P)).then_inc(rows, 16)
            sp.dma_start(rows_t[:], flat(2, P)).then_inc(rows, 16)
            sp.dma_start(k.rows_w[:], k.slots[3][P:P + SE].bitcast(F32).rearrange("(g q p) -> q g p", q=SQ, p=P)).then_inc(rows, 16)
            sp.dma_start(rows_p[:], flat(1, P - 1)).then_inc(rows, 16)
            sp.dma_start(rows_n[:], flat(1, P + 1)).then_inc(rows, 16)
            sp.wait_ge(rows, 96)

        @block.gpsimd
        def _(pool):
            pool.memset(k.edge_pad[:], -1).then_inc(pstep, 1)
            pool.wait_ge(pstep, 1)
            for at in (0, P + SE):
                pool.dma_start(k.slots[1][at:at + P].rearrange("(a b) -> a b", a=1), k.edge_pad[:]).then_inc(ends_in, 16)
            pool.wait_ge(ends_in, 32)

        @block.vector
        def _(dve):
            dve.sem_inc(used, 1)
            with dve.Fori(0, EC // 8) as i:
                dve.wait_ge(used, i + 1)
                for u in range(8):
                    dve.tensor_scalar(lob[:, u, :], k.iota_b[0:EP, :], cols(k.slo, i * 8 + u, 1), None,
                                      ALU.is_equal).then_inc(hot, 1)
                    dve.tensor_scalar(hib[:, u, :], k.iota_b[0:EP, 0:T], cols(k.shi, i * 8 + u, 1), None,
                                      ALU.is_equal).then_inc(hot, 1)
            step = Order(dve, vstep)
            dve.wait_ge(cleared, 1)
            step(dve.tensor_copy(k.deg_src[:], hist[:, 0:T]))
            dve.wait_ge(rows, 96)
            step(dve.tensor_copy(rows_f[:, 0, :, :], rows_i[:, 0, :, :]))
            step(dve.tensor_copy(k.rows_dst[:], rows_i[:, 1, :, :]))
            step(dve.tensor_copy(rows_f[:, 1, :, :], rows_t[:]))
            dve.sem_inc(turned, 1)
            for links, whole in ((rows_p, k.pen_prev), (rows_n, k.pen_next)):
                step(dve.tensor_copy(shifted[:], links[:]))
                step(dve.tensor_tensor(whole[:], k.rows_dst[:], shifted[:], ALU.is_equal))
                step(dve.tensor_scalar(whole[:], whole[:], -1.0, BIG, ALU.add, ALU.mult))
            for f, to in enumerate((k.src, k.dst, k.rel, k.weight)):
                dve.wait_ge(flipped, f + 1)
                step(dve.tensor_copy(to[:, 0:S].rearrange("p (g q) -> p g q", g=SG),
                                     flips[:, f, 0:S].rearrange("p (g q) -> p g q", g=SG)))
            step(dve.tensor_scalar(k.node[:], k.slot_tile[:, 1:S + 1], float(P), k.pcol[:, 0:1], ALU.mult, ALU.add))
            step(dve.tensor_scalar(k.dloc[:], k.node[:], -1.0, k.pcol[:, 0:1], ALU.mult, ALU.add))
            step(dve.tensor_tensor(k.dloc[:], k.dloc[:], k.dst[:], ALU.add))
            step(dve.tensor_copy(k.src_i[:], k.src[:]))
            step(dve.tensor_scalar(k.rel[:], k.rel[:], float(NP), None, ALU.mult))
            step(dve.tensor_tensor(k.rel[:], k.rel[:], k.src[:], ALU.add))
            step(dve.tensor_copy(k.rel_i[:], k.rel[:]))

        @block.tensor
        def _(pe):
            pe.matmul(hist[:, 0:T], k.zero_b[0:EP, 0:P], k.zero_b[0:EP, 0:T], start=True, stop=False)
            with pe.Fori(0, EC // 8) as i:
                for u in range(8):
                    pe.wait_ge(hot, i * 16 + 2 * u + 2)
                    last = pe.matmul(hist[:, 0:T], lob[:, u, :], hib[:, u, :], start=False, stop=False)
                last.then_inc(used, 1)
            pe.matmul(hist[:, 0:T], k.zero_b[0:EP, 0:P], k.zero_b[0:EP, 0:T], start=False, stop=True).then_inc(cleared, 1)
            pe.wait_ge(turned, 1)
            for f in range(4):
                for g in range(SG):
                    rows_of = (rows_f[:, 0, g, :], k.rows_dst[:, g, :], rows_f[:, 1, g, :], k.rows_w[:, g, :])[f]
                    last = pe.transpose(flips[:, f, g * SQ:(g + 1) * SQ], rows_of, k.ident[0:SQ, 0:SQ])
                last.then_inc(flipped, 1)



def count_pairs(nc, k, pairs_d):
    HALF = NP // 2
    BANKS = -(-NP // 512)
    COPIES = BANKS + 1
    with ExitStack() as c:
        c.enter_context(nc.cleanup_on_exit())
        sb = lambda n, s, d=F32: c.enter_context(nc.sbuf_tensor("c_" + n, s, d))
        sem = lambda n: nc.alloc_semaphore("c_" + n)
        places = sb("places", [P, HALF], F16)
        upper = sb("upper", [P, S])
        hot_d = sb("hot_d", [P, 4, P], BF16)
        hot_s = sb("hot_s", [P, 4, NP + 1], BF16)
        zero = sb("zero", [P, 512], BF16)
        rows = sb("rows", [P, 2, NP])
        counts = c.enter_context(nc.psum_tensor("c_counts", [P, BANKS, 512], F32))
        ready, made, used, full, copied = sem("ready"), sem("made"), sem("used"), sem("full"), sem("copied")
        made_d = sem("made_d")
        stored = [sem(f"stored{b}") for b in range(2)]
        width = [min(512, NP - b * 512) for b in range(BANKS)]
        taken = [w + (b == BANKS - 1) for b, w in enumerate(width)]
        block = c.enter_context(nc.Block())

        @block.gpsimd
        def _(pool):
            pool.iota(places[:], [[1, HALF]], base=0, channel_multiplier=0,
                      allow_small_or_imprecise_dtypes=True).then_inc(ready, 1)
            pool.memset(zero[:], 0.0).then_inc(ready, 1)
            pool.memset(hot_s[:, :, NP:NP + 1], 1.0).then_inc(ready, 1)

        @block.vector
        def _(dve):
            dve.tensor_scalar(upper[:], k.src[:], float(-HALF), None, ALU.add).then_inc(ready, 1)
            dve.wait_ge(ready, 4)
            with dve.Fori(0, S // 4) as i:
                for u in range(4):
                    j = i * 4 + u
                    dve.wait_ge(used, j + 1)
                    dve.tensor_scalar(hot_d[:, u, :], k.iota_b[:], cols(k.dloc, j, 1), None,
                                      ALU.is_equal).then_inc(made, 1)
                    dve.tensor_scalar(hot_s[:, u, 0:HALF], places[:], cols(k.src, j, 1), None,
                                      ALU.is_equal).then_inc(made, 1)
                    dve.tensor_scalar(hot_s[:, u, HALF:NP], places[:], cols(upper, j, 1), None,
                                      ALU.is_equal).then_inc(made, 1)

        @block.tensor
        def _(pe):
            pe.sem_inc(used, 4)
            pe.wait_ge(ready, 4)

            def zeros(b, start):
                return pe.matmul(counts[:, b, 0:taken[b]], zero[:, 0:P], zero[:, 0:taken[b]],
                                 start=start, stop=not start)

            def multiply(u, j):
                pe.wait_ge(made, j * 3 + 3)
                for b in range(BANKS):
                    last = pe.matmul(counts[:, b, 0:taken[b]], hot_d[:, u, :],
                                     hot_s[:, u, b * 512:b * 512 + taken[b]], start=False, stop=False)
                last.then_inc(used, 1)

            for b in range(BANKS):
                zeros(b, True)
            with pe.Fori(0, S // 4) as i:
                turns = pe.value_load(k.group_turns_i[0:1, bass.ds(i, 1)], min_val=0, max_val=4)
                with pe.If(turns == 0):
                    for u in range(4):
                        multiply(u, i * 4 + u)
                with pe.If(turns != 0):
                    for u in range(4):
                        j = i * 4 + u
                        first = pe.value_load(k.turns_i[0:1, bass.ds(j, 1)], min_val=0, max_val=1)
                        with pe.If(first != 0):
                            t = pe.value_load(k.slot_tile_i[0:1, bass.ds(j + 1, 1)], min_val=0, max_val=T - 1)
                            for b in range(BANKS):
                                last = zeros(b, False)
                            last.then_inc(full, 1)
                            for b in range(BANKS):
                                pe.wait_ge(copied, t * COPIES + (b + 1 if b < BANKS - 1 else COPIES))
                                zeros(b, True)
                        multiply(u, j)
            for b in range(BANKS):
                last = zeros(b, False)
            last.then_inc(full, 1)

        @block.scalar
        def _(act):
            act.sem_inc(copied, COPIES)

            def copy(t, b):
                act.wait_ge(full, t + 1)
                act.sem_inc(k.passed, 1)
                if reused(t):
                    act.wait_ge(stored[b], (t - b) * 8)
                act.sem_inc(k.passed, 1)
                for n in range(BANKS):
                    if n == BANKS - 1:
                        act.copy(cols(k.deg_dst, t, 1), counts[:, n, width[n]:width[n] + 1]).then_inc(copied, 1)
                    act.copy(rows[:, b, n * 512:n * 512 + width[n]], counts[:, n, 0:width[n]]).then_inc(copied, 1)
            over_tiles_after_two(act, copy)

        @block.sync
        def _(sp):
            def store(t, b):
                sp.wait_ge(copied, t * COPIES + 2 * COPIES)
                sp.dma_start(pairs_d[bass.ds(t * P, P), :], rows[:, b, :]).then_inc(stored[b], 16)
            over_tiles(sp, store)
            sp.wait_ge(stored[0], 16 * (T // 2 + 1))
            sp.wait_ge(stored[1], 16 * (T // 2))


def dense_product(nc, k, name, mat_d, rows, to, column, turned_d=None):
    TG = -(-T // 4)
    with ExitStack() as c:
        c.enter_context(nc.cleanup_on_exit())
        sb = lambda n, s, d=F32: c.enter_context(nc.sbuf_tensor(name + n, s, d))
        sem = lambda n: nc.alloc_semaphore(name + n)
        blk = sb("blk", [P, 2, T, P])
        line = sb("line", [P, 2, NP]) if turned_d is not None else None
        prods = c.enter_context(nc.psum_tensor(name + "prods", [P, 2, 512], F32))
        flips = c.enter_context(nc.psum_tensor(name + "flips", [P, 4, 512], F32))
        multiplied, taken, flipped, lined = sem("multiplied"), sem("taken"), sem("flipped"), sem("lined")
        loaded = [sem(f"loaded{b}") for b in range(2)]
        stored = [sem(f"stored{b}") for b in range(2)]
        block = c.enter_context(nc.Block())

        @block.sync
        def _(sp):
            def load_block(t, b):
                sp.wait_ge(multiplied, t + 1)
                sp.dma_start(blk[:, b, :, :], mat_d[:, bass.ds(t * P, P)].rearrange(
                    "(a p) q -> p a q", p=P)).then_inc(loaded[b], 16)
            over_tiles(sp, load_block)

        @block.gpsimd
        def _(pool):
            if turned_d is not None:
                def store(t, b):
                    pool.wait_ge(lined, t * TG + TG + 4)
                    pool.sem_inc(k.passed, 1)
                    pool.dma_start(turned_d[bass.ds(t * P, P), :], line[:, b, :]).then_inc(stored[b], 16)
                over_tiles(pool, store)
                pool.wait_ge(stored[0], 16 * (T // 2 + 1))
                pool.wait_ge(stored[1], 16 * (T // 2))

        @block.tensor
        def _(pe):
            pe.sem_inc(multiplied, 2)

            def before(g):
                return g - 4 if g >= 4 else max(n for n in range(TG) if n % 4 == g) - TG

            def tile(t, b):
                pe.wait_ge(loaded[b], (t - b) * 8 + 16)
                if turned_d is not None:
                    for g in range(TG):
                        pe.wait_ge(lined, t * TG + before(g) + 5)
                        for a in range(4 * g, min(T, 4 * g + 4)):
                            last = pe.transpose(flips[:, (g % 4), (a % 4) * P:(a % 4 + 1) * P],
                                                blk[:, b, a, :], k.ident[:])
                        last.then_inc(flipped, 1)
                        if g == 0:
                            pe.wait_ge(taken, t + 1)
                        for a in range(4 * g, min(T, 4 * g + 4)):
                            last = pe.matmul(prods[:, b, 0:D], blk[:, b, a, :], rows[:, a, 0:D],
                                             start=a == 0, stop=a == T - 1)
                    last.then_inc(multiplied, 1)
                else:
                    pe.wait_ge(taken, t + 1)
                    for a in range(T):
                        last = pe.matmul(prods[:, b, 0:D], blk[:, b, a, :], rows[:, a, 0:D],
                                         start=a == 0, stop=a == T - 1)
                    last.then_inc(multiplied, 1)
            over_tiles(pe, tile)

        @block.vector
        def _(dve):
            dve.sem_inc(taken, 2)

            def take(t, b):
                dve.wait_ge(multiplied, t + 3)
                dve.tensor_scalar(to[:, bass.ds(t, 1), 0:D].rearrange("p a f -> p (a f)"), prods[:, b, 0:D],
                                  cols(column, t, 1), None, ALU.mult).then_inc(taken, 1)
            over_tiles(dve, take)
            dve.wait_ge(taken, T + 2)

        @block.scalar
        def _(act):
            if turned_d is not None:
                act.sem_inc(lined, 4)

                def copy(t, b):
                    if reused(t):
                        act.wait_ge(stored[b], (t - b) * 8)
                    for g in range(TG):
                        n = min(4, T - 4 * g) * P
                        act.wait_ge(flipped, t * TG + g + 1)
                        act.copy(line[:, b, 4 * g * P:4 * g * P + n], flips[:, g % 4, 0:n]).then_inc(lined, 1)
                over_tiles_after_two(act, copy)



def score_by_edge(nc, k, name, table, width, node_rows, out_src, out_dst):
    dot = out_dst is None
    with ExitStack() as c:
        c.enter_context(nc.cleanup_on_exit())
        sb = lambda n, s, d=F32: c.enter_context(nc.sbuf_tensor(name + n, s, d))
        pb = lambda n, s: c.enter_context(nc.psum_tensor(name + n, s, F32))
        sem = lambda n: nc.alloc_semaphore(name + n)
        dcol = sb("dcol", [P, U])
        pick = sb("pick", [P, 2, G4, P])
        idx = sb("idx", [P, 2, 8], I32)
        got = sb("got", [P, U, width])
        prod = sb("prod", [P, width])
        score = sb("score", [P, U])
        wide = pb("wide", [P, 2, 512])
        expand = pb("expand", [P, 4, 512])
        copied, turned, picked = sem("copied"), sem("turned"), sem("picked")
        expanded, used, kept, indexed = sem("expanded"), sem("used"), sem("kept"), sem("indexed")
        arrived = [sem(f"arrived{n}") for n in range(U)]
        NG = U // G4
        HU = U // 2
        block = c.enter_context(nc.Block())

        def copy_indices(eng, i, h):
            eng.wait_ge(used, i * U + h * HU + 8 if dot else (i * 2 + h) * 2 + 2)
            eng.sem_inc(k.passed, 1)
            copy = eng.copy if dot else eng.tensor_copy
            copy(idx[:, h, :], cols(k.src_i, i * U + h * HU, HU)).then_inc(indexed, 1)

        @block.gpsimd
        def _(pool):
            with pool.Fori(0, IT) as i:
                for u in range(U):
                    if u % HU == 0:
                        pool.wait_ge(indexed, i * 2 + u // HU + 1)
                        pool.sem_inc(k.passed, 1)
                    pool.indirect_dma_start(got[:, u, :], None, table, bass.IndirectOffsetOnAxis(
                        ap=idx[:, u // HU, u % HU:u % HU + 1], axis=0)).then_inc(arrived[u], 16)

        @block.vector
        def _(dve):
            dve.sem_inc(picked, 2)
            if dot:
                dve.sem_inc(kept, 1)
            with dve.Fori(0, IT) as i:
                def use(u):
                    j = i * U + u
                    dve.wait_ge(expanded, j + 2)
                    dve.wait_ge(arrived[u], i * 16 + 16)
                    dve.wait_ge(used, j + 16)
                    dve.tensor_tensor_reduce(out=prod[:], in0=expand[:, u % 4, 0:width], in1=got[:, u, :],
                                             scale=1.0, scalar=0.0, op0=ALU.mult, op1=ALU.add,
                                             accum_out=score[:, u:u + 1]).then_inc(used, 1)

                dve.wait_ge(turned, i * NG + 4)
                dve.tensor_copy(dcol[:], cols(k.dst, i * U, U)).then_inc(copied, 1)
                for g in range(NG):
                    n = i * NG + g
                    if not dot and g % 2 == 0:
                        copy_indices(dve, i, g // 2)
                    dve.wait_ge(turned, n + 5)
                    if g >= 2:
                        dve.wait_ge(expanded, n * G4 - 3)
                    else:
                        dve.wait_ge(expanded, i * U + 1)
                    dve.tensor_tensor(pick[:, g % 2, :, :], wide[:, g % 2, :].rearrange("p (s q) -> p s q", s=G4),
                                      cols(k.node, i * U + g * G4, G4).unsqueeze(2).broadcast_to([P, G4, P]),
                                      ALU.is_equal).then_inc(picked, 1)
                    if dot and g > 0:
                        for u in range((g - 1) * G4, g * G4):
                            use(u)
                if dot:
                    for u in range((NG - 1) * G4, U):
                        use(u)
                    dve.wait_ge(used, i * U + U + 16)
                    dve.tensor_scalar(cols(out_src, i * U, U), score[:], 1.0 / float(np.sqrt(D)), None,
                                      ALU.mult).then_inc(kept, 1)
                    dve.wait_ge(kept, i + 2)

        @block.tensor
        def _(pe):
            pe.sem_inc(turned, 4)
            pe.sem_inc(expanded, 1)
            with pe.Fori(0, IT) as i:
                def turn(g):
                    n = i * NG + g
                    pe.wait_ge(picked, n + 1)
                    for s in range(G4):
                        u = g * G4 + s
                        last = pe.transpose(wide[:, g % 2, s * P:(s + 1) * P],
                                            dcol[:, u:u + 1].broadcast_to([P, P]), k.ident[:])
                    last.then_inc(turned, 1)

                pe.wait_ge(copied, i + 1)
                turn(0)
                for g in range(NG):
                    if g + 1 < NG:
                        turn(g + 1)
                    pe.wait_ge(picked, i * NG + g + 3)
                    for u in range(g * G4, (g + 1) * G4):
                        t = pe.value_load(k.slot_tile_i[0:1, bass.ds(i * U + u + 1, 1)], min_val=0, max_val=T - 1)
                        if dot:
                            pe.wait_ge(used, i * U + u + 13)
                            to = expand[:, u % 4, 0:width]
                        else:
                            if u % HU == 0:
                                pe.wait_ge(used, (i * 2 + u // HU) * 2 + 2)
                            to = expand[:, u // HU, (u % HU) * width:(u % HU + 1) * width]
                        pe.matmul(to, pick[:, g % 2, u % G4, :], tile_of(node_rows, t),
                                  start=True, stop=True).then_inc(expanded, 1)

        @block.scalar
        def _(act):
            if dot:
                act.sem_inc(used, 16)
                with act.Fori(0, IT) as i:
                    for h in range(2):
                        copy_indices(act, i, h)
            else:
                act.sem_inc(used, 4)
                with act.Fori(0, IT) as i:
                    for h in range(2):
                        act.wait_ge(expanded, i * U + (h + 1) * HU + 1)
                        for u in range(h * HU, (h + 1) * HU):
                            act.wait_ge(arrived[u], i * 16 + 16)
                        act.sem_inc(k.passed, 1)
                        act.copy(out_dst[:, bass.ds(i * U + h * HU, HU), :].rearrange("p s h -> p (s h)"),
                                 expand[:, h, 0:HU * width]).then_inc(used, 1)
                        act.copy(out_src[:, bass.ds(i * U + h * HU, HU), :].rearrange("p s h -> p (s h)"),
                                 got[:, h * HU:(h + 1) * HU, :].rearrange("p s h -> p (s h)")).then_inc(used, 1)


def segment_maximum(nc, k, name, heads, value, out):
    with ExitStack() as c:
        c.enter_context(nc.cleanup_on_exit())
        sb = lambda n, s, d=F32: c.enter_context(nc.sbuf_tensor(name + n, s, d))
        sem = lambda n: nc.alloc_semaphore(name + n)
        v = sb("v", [SQ, SG, heads, P])
        scan = [sb("scan", [SQ, SG, heads, P]), v]
        pen = sb("pen", [SQ, SG, heads, P])
        edge = sb("edge", [SQ, 2, SG, heads])
        whole = sb("whole", [SQ, 2, SG, heads])
        reset = sb("reset", [SQ, SG, P])
        reach = sb("reach", [SQ, 2, SG, P])
        one = sb("one", [SQ, 2, SG])
        line = sb("line", [heads, 2, S])
        lpen = sb("lpen", [heads, 2, S])
        carry = sb("carry", [heads, 2, S])
        carried = sb("carried", [SQ, 2, SG, heads])
        turns = c.enter_context(nc.psum_tensor(name + "turns", [P, 4, 512], F32))
        lines = c.enter_context(nc.psum_tensor(name + "lines", [P, 2, 512], F32))
        lines2 = c.enter_context(nc.psum_tensor(name + "lines2", [P, 2, 512], F32))
        turned, taken, vstep, ends, lined, carry_s, back, done = (
            sem("turned"), sem("taken"), sem("vstep"), sem("ends"), sem("lined"), sem("carry_s"),
            sem("back"), sem("done"))
        out_t, out_k, final = sem("out_t"), sem("out_k"), sem("final")
        block = c.enter_context(nc.Block())
        per_bank = 4

        @block.tensor
        def _(pe):
            for n in range(SG * heads):
                g, h = n // heads, n % heads
                if n >= 4:
                    pe.wait_ge(taken, n - 3)
                pe.transpose(turns[0:SQ, n % 4, 0:P], value[:, g * SQ:(g + 1) * SQ, h], k.ident[:]).then_inc(turned, 1)
            pe.wait_ge(ends, 1)
            for d in range(2):
                for g in range(SG):
                    pe.transpose(lines[0:heads, d, g * SQ:(g + 1) * SQ], edge[:, d, g, :], k.ident[0:SQ, 0:SQ])
                    last = pe.transpose(lines2[0:heads, d, g * SQ:(g + 1) * SQ], whole[:, d, g, :],
                                        k.ident[0:SQ, 0:SQ])
            last.then_inc(lined, 1)
            pe.wait_ge(carry_s, 1)
            for d in range(2):
                for g in range(SG):
                    last = pe.transpose(turns[0:SQ, 0, (d * SG + g) * heads:(d * SG + g + 1) * heads],
                                        carry[:, d, g * SQ:(g + 1) * SQ], k.ident[0:heads, 0:heads])
            last.then_inc(back, 1)
            pe.wait_ge(final, 1)
            for n in range(SG * heads):
                g, h = n // heads, n % heads
                if n >= 4:
                    pe.wait_ge(out_k, n - 3)
                pe.transpose(turns[:, n % 4, 0:SQ], scan[0][:, g, h, :], k.ident[0:SQ, 0:SQ]).then_inc(out_t, 1)

        @block.scalar
        def _(act):
            for n in range(SG * heads):
                g, h = n // heads, n % heads
                act.wait_ge(turned, n + 1)
                act.copy(v[:, g, h, :], turns[0:SQ, n % 4, 0:P]).then_inc(taken, 1)
            for n in range(SG * heads):
                g, h = n // heads, n % heads
                act.wait_ge(out_t, n + 1)
                act.copy(out[:, g * SQ:(g + 1) * SQ, h], turns[:, n % 4, 0:SQ]).then_inc(out_k, 1)
            act.wait_ge(out_k, SG * heads)

        @block.vector
        def _(dve):
            step = Order(dve, vstep)
            flat = lambda a: a.rearrange("q g p -> q (g p)")
            flat4 = lambda a: a.rearrange("q g h p -> q (g h p)")
            for d, links in enumerate((k.pen_prev, k.pen_next)):
                entry, leave = (0, P - 1) if d == 0 else (P - 1, 0)
                step(dve.memset(reset[:], 0.0))
                step(dve.memset(reset[:, :, entry:entry + 1], BIG))
                a, b, o = flat(reset[:]), flat(links[:]), flat(reach[:, d, :, :])
                if d:
                    a, b, o = a[:, ::-1], b[:, ::-1], o[:, ::-1]
                step(dve.tensor_tensor_scan(o, a, b, 0.0, ALU.add, ALU.min))
                step(dve.tensor_copy(whole[:, d, :, :], reach[:, d, :, leave:leave + 1].broadcast_to([SQ, SG, heads])))
            dve.wait_ge(taken, SG * heads)
            for d, links in enumerate((k.pen_prev, k.pen_next)):
                entry, leave = (0, P - 1) if d == 0 else (P - 1, 0)
                step(dve.tensor_copy(pen[:], links[:].unsqueeze(2).broadcast_to([SQ, SG, heads, P])))
                step(dve.memset(pen[:, :, :, entry:entry + 1], -BIG))
                a, b, o = flat4(pen[:]), flat4(v[:]), flat4(scan[d][:])
                if d:
                    a, b, o = a[:, ::-1], b[:, ::-1], o[:, ::-1]
                step(dve.tensor_tensor_scan(o, a, b, -BIG, ALU.add, ALU.max))
                step(dve.tensor_copy(edge[:, d, :, :], scan[d][:, :, :, leave:leave + 1].rearrange("q g h a -> q g (h a)")))
            dve.sem_inc(ends, 1)
            dve.wait_ge(lined, 1)
            step(dve.tensor_copy(line[:], lines[0:heads, :, 0:S]))
            step(dve.tensor_copy(lpen[:], lines2[0:heads, :, 0:S]))
            step(dve.memset(carry[:], -BIG))
            step(dve.tensor_tensor_scan(carry[:, 0, 1:S], lpen[:, 0, 0:S - 1], line[:, 0, 0:S - 1], -BIG,
                                        ALU.add, ALU.max))
            step(dve.tensor_tensor_scan(carry[:, 1, 0:S - 1][:, ::-1], lpen[:, 1, 1:S][:, ::-1],
                                        line[:, 1, 1:S][:, ::-1], -BIG, ALU.add, ALU.max))
            dve.sem_inc(carry_s, 1)
            dve.wait_ge(back, 1)
            step(dve.tensor_copy(carried[:].rearrange("q d g h -> q (d g h)"), turns[0:SQ, 0, 0:2 * SG * heads]))
            for d in range(2):
                for g in range(SG):
                    step(dve.tensor_tensor(pen[:, g, :, :], carried[:, d, g, :].unsqueeze(2).broadcast_to([SQ, heads, P]),
                                           reach[:, d, g, :].unsqueeze(1).broadcast_to([SQ, heads, P]), ALU.add))
                step(dve.tensor_tensor(flat4(scan[d][:]), flat4(scan[d][:]), flat4(pen[:]), ALU.max))
            step(dve.tensor_tensor(flat4(scan[0][:]), flat4(scan[0][:]), flat4(scan[1][:]), ALU.max))
            dve.sem_inc(final, 1)


def sum_by_destination(nc, k, name, table, index, weight=None, per_head=None, ones=False):
    width = D + (H if per_head is not None else 1 if ones else 0)
    with ExitStack() as c:
        c.enter_context(nc.cleanup_on_exit())
        sb = lambda n, s, d=F32: c.enter_context(nc.sbuf_tensor(name + n, s, d))
        sem = lambda n: nc.alloc_semaphore(name + n)
        idx = sb("idx", [P, 2, 8], I32)
        got = sb("got", [P, U, D])
        hot = sb("hot", [P, 4, P])
        part = sb("part", [P, 4, width]) if per_head is not None else None
        sums = c.enter_context(nc.psum_tensor(name + "sums", [P, 4, 512], F32))
        arrived = [sem(f"arrived{n}") for n in range(U)]
        indexed, cleared = sem("indexed"), sem("cleared")
        made, summed, freed, added = sem("made"), sem("summed"), sem("freed"), sem("added")
        block = c.enter_context(nc.Block())

        @block.gpsimd
        def _(pool):
            with pool.Fori(0, IT) as i:
                for u in range(U):
                    if u % 8 == 0:
                        pool.wait_ge(indexed, i * 2 + u // 8 + 1)
                        pool.sem_inc(k.passed, 1)
                    pool.indirect_dma_start(got[:, u, :], None, table, bass.IndirectOffsetOnAxis(
                        ap=idx[:, u // 8, u % 8:u % 8 + 1], axis=0)).then_inc(arrived[u], 16)

        @block.scalar
        def _(act):
            act.sem_inc(freed, 16)
            with act.Fori(0, IT) as i:
                for u in range(0, U, 8):
                    if per_head is not None:
                        act.wait_ge(freed, i * U + u + 8)
                    else:
                        act.wait_ge(summed, i * U + u + 1)
                    act.sem_inc(k.passed, 1)
                    act.copy(idx[:, u // 8, :], cols(index, i * U + u, 8)).then_inc(indexed, 1)

        @block.vector
        def _(dve):
            dve.memset(k.acc[:], 0.0).then_inc(cleared, 1)
            dve.wait_ge(cleared, 1)
            dve.sem_inc(added, 4)

            def add(j, b):
                t = dve.value_load(k.slot_tile_i[0:1, bass.ds(j, 1)], min_val=0, max_val=T - 1)
                dve.wait_ge(summed, j + 9)
                dve.wait_ge(added, j + 4)
                a = k.acc[:, bass.ds(t, 1), 0:width].rearrange("p a f -> p (a f)")
                dve.tensor_tensor(a, a, sums[:, b, 0:width], ALU.add).then_inc(added, 1)

            with dve.Fori(0, IT) as i:
                for u in range(U):
                    j = i * U + u
                    if weight is None:
                        ins = dve.tensor_scalar(hot[:, u % 4, :], k.iota[:], cols(k.dloc, j, 1), None, ALU.is_equal)
                    else:
                        ins = dve.tensor_scalar(hot[:, u % 4, :], k.iota[:], cols(k.dloc, j, 1), cols(weight, j, 1),
                                                ALU.is_equal, ALU.mult)
                    ins.then_inc(made, 1)
                    if per_head is not None:
                        dve.wait_ge(arrived[u], i * 16 + 16)
                        w = per_head[:, bass.ds(j, 1), :].rearrange("p a h -> p (a h)")
                        dve.tensor_tensor(part[:, u % 4, 0:D].rearrange("p (h f) -> p h f", h=H),
                                          got[:, u, :].rearrange("p (h f) -> p h f", h=H),
                                          w.unsqueeze(2).broadcast_to([P, H, HD]), ALU.mult).then_inc(freed, 1)
                        dve.tensor_copy(part[:, u % 4, D:D + H], w).then_inc(made, 1)
                    add(j, (u - 1) % 4)
            add(S, (S - 1) % 4)
            dve.wait_ge(added, S + 5)

        @block.tensor
        def _(pe):
            pe.sem_inc(summed, 8)
            pe.matmul(sums[:, 3, 0:width], k.zero[:, 0:P], k.zero[:, 0:width], start=True, stop=True).then_inc(summed, 1)
            with pe.Fori(0, IT) as i:
                for u in range(U):
                    j = i * U + u
                    pe.wait_ge(added, j + 2)
                    if per_head is not None:
                        pe.wait_ge(freed, j + 17)
                        pe.wait_ge(made, 2 * j + 2)
                        pe.matmul(sums[:, u % 4, 0:width], hot[:, u % 4, :], part[:, u % 4, :],
                                  start=True, stop=True).then_inc(summed, 1)
                    else:
                        pe.wait_ge(made, j + 1)
                        pe.wait_ge(arrived[u], i * 16 + 16)
                        if ones:
                            pe.matmul(sums[:, u % 4, D:D + 1], hot[:, u % 4, :], k.ones[:, 0:1], start=True, stop=True)
                        pe.matmul(sums[:, u % 4, 0:D], hot[:, u % 4, :], got[:, u, :],
                                  start=True, stop=True).then_inc(summed, 1)



def project(nc, k, name, sources, weights, width, steps, epilogue, stores=(), chains=None):
    ns = len(sources) if chains is None else 1
    with ExitStack() as c:
        c.enter_context(nc.cleanup_on_exit())
        sb = lambda n, s, d=F32: c.enter_context(nc.sbuf_tensor(name + n, s, d))
        sem = lambda n: nc.alloc_semaphore(name + n)
        xs = sb("xs", [P, 2, CH if chains is not None else ns, D])
        diag = sb("diag", [P, 2, P]) if chains is not None else None
        xt = sb("xt", [P, 2, ns * 2, P])
        flips = c.enter_context(nc.psum_tensor(name + "flips", [P, 2, 512], F32))
        nb = -(-width // 512)
        prods = c.enter_context(nc.psum_tensor(name + "prods", [P, 2, nb, 512], F32))
        staged, flipped, turned, multiplied, finished = (sem("staged"), sem("flipped"), sem("turned"),
                                                         sem("multiplied"), sem("finished"))
        vstep, stored = sem("vstep"), sem("stored")
        loaded = [sem(f"loaded{n}") for n in range(2)]
        block = c.enter_context(nc.Block())

        @block.sync
        def _(sp):
            if chains is not None:
                def load(t, b):
                    sp.wait_ge(flipped, t + 1)
                    for n in range(CH):
                        sp.dma_start(xs[:, b, n, :],
                                     chains[n][0][bass.ds(t * P, P), :]).then_inc(loaded[b], 16)
                over_tiles(sp, load)
            if stores:
                def store_all(t, b):
                    sp.wait_ge(finished, t + 3)
                    for src, dram in stores:
                        sp.dma_start(dram[bass.ds(t * P, P), :], src[:, bass.ds(t, 1), 0:D].rearrange(
                            "p a f -> p (a f)")).then_inc(stored, 16)
                over_tiles(sp, store_all)
                sp.wait_ge(stored, 16 * T * len(stores))

        @block.scalar
        def _(act):
            act.sem_inc(turned, 2)

            def stage(t, b):
                act.wait_ge(flipped, t + 1)
                act.sem_inc(k.passed, 1)
                for s, (src, column) in enumerate(sources):
                    if column is None:
                        ins = act.copy(xs[:, b, s, :], src[:, bass.ds(t, 1), 0:D].rearrange("p a f -> p (a f)"))
                    else:
                        ins = act.activation(xs[:, b, s, :], src[:, bass.ds(t, 1), 0:D].rearrange("p a f -> p (a f)"),
                                             ACT.Copy, scale=cols(column, t, 1))
                    ins.then_inc(staged, 1)

            def keep(t, b):
                act.wait_ge(flipped, t + 3)
                act.wait_ge(multiplied, t + 1)
                act.copy(xt[:, b, :, :].rearrange("p a q -> p (a q)"), flips[:, b, 0:ns * D]).then_inc(turned, 1)

            if chains is None:
                stage(0, 0)
                with act.Fori(0, T // 2) as i:
                    stage(2 * i + 1, 1)
                    keep(2 * i, 0)
                    stage(2 * i + 2, 0)
                    keep(2 * i + 1, 1)
                keep(T - 1, 0)
            else:
                over_tiles(act, keep)

        @block.tensor
        def _(pe):
            pe.sem_inc(flipped, 2)
            pe.sem_inc(multiplied, 2)

            def flip(t, b):
                pe.wait_ge(turned, t + 1)
                if chains is None:
                    pe.wait_ge(staged, (t + 1) * ns)
                    for s in range(ns):
                        for h in range(2):
                            last = pe.transpose(flips[:, b, s * D + h * P:s * D + (h + 1) * P],
                                                xs[:, b, s, h * P:(h + 1) * P], k.ident[:])
                else:
                    pe.wait_ge(loaded[b], (t - b) * (8 * CH) + 16 * CH)
                    pe.wait_ge(staged, t + 1)
                    for h in range(2):
                        for n in range(CH):
                            last = pe.matmul(flips[:, b, h * P:(h + 1) * P], xs[:, b, n, h * P:(h + 1) * P],
                                             diag[:, b, :], start=n == 0, stop=n == CH - 1)
                last.then_inc(flipped, 1)

            def multiply(t, b):
                pe.wait_ge(turned, t + 3)
                pe.wait_ge(finished, t + 1)
                for o in range(nb):
                    w = min(512, width - o * 512)
                    for s in range(ns * 2):
                        last = pe.matmul(prods[:, b, o, 0:w], xt[:, b, s, :], weights[:, s, o * 512:o * 512 + w],
                                         start=s == 0, stop=s == ns * 2 - 1)
                last.then_inc(multiplied, 1)

            flip(0, 0)
            with pe.Fori(0, T // 2) as i:
                flip(2 * i + 1, 1)
                multiply(2 * i, 0)
                flip(2 * i + 2, 0)
                multiply(2 * i + 1, 1)
            multiply(T - 1, 0)

        @block.vector
        def _(dve):
            dve.sem_inc(finished, 2)
            step = Order(dve, vstep)

            def work(t, b):
                dve.wait_ge(multiplied, t + 3)
                step.n = t * steps
                epilogue(dve, step, t, prods[:, b, :, :].rearrange("p a n -> p (a n)"))
                dve.sem_inc(finished, 1)

            def make_diag(t, b):
                dve.wait_ge(flipped, t + 1)
                dve.tensor_scalar(diag[:, b, :], k.ident[:], cols(chains[0][1], t, 1), None, ALU.mult).then_inc(staged, 1)

            if chains is None:
                over_tiles(dve, work)
            else:
                make_diag(0, 0)
                with dve.Fori(0, T // 2) as i:
                    make_diag(2 * i + 1, 1)
                    work(2 * i, 0)
                    make_diag(2 * i + 2, 0)
                    work(2 * i + 1, 1)
                work(T - 1, 0)


def each_tile(nc, k, name, steps, before, work, stores=()):
    with ExitStack() as c:
        c.enter_context(nc.cleanup_on_exit())
        sem = lambda n: nc.alloc_semaphore(name + n)
        vstep, finished, stored = sem("vstep"), sem("finished"), sem("stored")
        block = c.enter_context(nc.Block())

        @block.vector
        def _(dve):
            step = Order(dve, vstep)
            before(dve, step)
            base = step.n

            def one(t, b):
                step.n = base + t * steps
                work(dve, step, t)
                dve.sem_inc(finished, 1)
            over_tiles(dve, one)

        @block.sync
        def _(sp):
            if stores:
                def store(t, b):
                    sp.wait_ge(finished, t + 1)
                    for src, dram in stores:
                        sp.dma_start(dram[bass.ds(t * P, P), :], tile_of(src, t)).then_inc(stored, 16)
                over_tiles(sp, store)
                sp.wait_ge(stored, 16 * T * len(stores))


def statistics(dve, step, k, r, t):
    dve.sem_inc(k.passed, 1)
    step(dve.bn_stats(k.six[:], tile_of(r, t)))
    dve.sem_inc(k.passed, 1)
    step(dve.bn_aggr(k.two[:], k.six[:]))
    step(dve.tensor_copy(k.mv[:, bass.ds(t, 1), :].rearrange("p a f -> p (a f)"), k.two[:]))


def refine_root(dve, step, root, a, square):
    step(dve.reciprocal(root, root))
    step(dve.tensor_tensor(square, root, root, ALU.mult))
    step(dve.tensor_tensor(square, square, a, ALU.mult))
    step(dve.tensor_scalar(square, square, -0.5, 1.5, ALU.mult, ALU.add))
    step(dve.tensor_tensor(root, root, square, ALU.mult))


def normalize(nc, k, name, r, x, out=None):
    with ExitStack() as c:
        c.enter_context(nc.cleanup_on_exit())
        sem = lambda n: nc.alloc_semaphore(name + n)
        given, square = (c.enter_context(nc.sbuf_tensor(name + n, [P, T], F32)) for n in ("given", "square"))
        vstep, rooted, stored, finished = sem("vstep"), sem("rooted"), sem("stored"), sem("finished")
        block = c.enter_context(nc.Block())

        @block.vector
        def _(dve):
            step = Order(dve, vstep)
            step(dve.tensor_scalar(given[:], k.mv[:, :, 1], LN_EPS, None, ALU.add))
            dve.wait_ge(rooted, 1)
            refine_root(dve, step, k.rstd[:], given[:], square[:])

            def one(t, b):
                dve.tensor_scalar(tile_of(x, t), tile_of(r, t), k.mv[:, bass.ds(t, 1), 0:1].rearrange("p a f -> p (a f)"),
                                  cols(k.rstd, t, 1), ALU.subtract, ALU.mult).then_inc(finished, 1)
            over_tiles(dve, one)
            dve.wait_ge(finished, T)

        @block.scalar
        def _(act):
            act.wait_ge(vstep, 1)
            act.activation(k.rstd[:], given[:], ACT.Sqrt).then_inc(rooted, 1)

        @block.sync
        def _(sp):
            if out is not None:
                with sp.Fori(0, T - 1) as t:
                    sp.wait_ge(finished, t + 1)
                    sp.dma_start(out[bass.ds(t * P, P), :], tile_of(x, t)).then_inc(stored, 16)
                sp.wait_ge(finished, T)
                sp.dma_start(out[(T - 1) * P:N, :], x[0:NLAST, T - 1, :]).then_inc(stored, 16)
                sp.wait_ge(stored, 16 * T)


def load(nc, name, pairs):
    with ExitStack() as c:
        c.enter_context(nc.cleanup_on_exit())
        loaded = nc.alloc_semaphore(name + "loaded")
        block = c.enter_context(nc.Block())

        @block.sync
        def _(sp):
            for to, src in pairs:
                sp.dma_start(to, src).then_inc(loaded, 16)
            sp.wait_ge(loaded, 16 * len(pairs))


def halves(w):
    return w.rearrange("(a p) n -> p a n", p=P)


def attention_weights(nc, k, name, value, other, best, heads):
    with ExitStack() as c:
        c.enter_context(nc.cleanup_on_exit())
        sem = lambda n: nc.alloc_semaphore(name + n)
        vstep, ready, done = sem("vstep"), sem("ready"), sem("done")
        block = c.enter_context(nc.Block())
        flat = lambda a: a.rearrange("p s h -> p (s h)")
        v, b = flat(value[:]), flat(best[:])

        @block.vector
        def _(dve):
            step = Order(dve, vstep)
            if other is not None:
                o = flat(other[:])
                for a in (v, b):
                    step(dve.tensor_tensor(a, a, o, ALU.add))
                    step(dve.scalar_tensor_tensor(a, a, 0.2, a, ALU.mult, ALU.max))
            step(dve.tensor_tensor(v, v, b, ALU.subtract))
            dve.sem_inc(ready, 1)

        @block.scalar
        def _(act):
            act.wait_ge(ready, 1)
            act.activation(v, v, ACT.Exp).then_inc(done, 1)
            act.wait_ge(done, 1)


def graph_layers(nc, x, src, dst, edge_type_16, edge_weight1, L0_gnn_W, L0_gnn_b, L1_gnn_W_lin, L1_gnn_b_lin,
                 L1_gnn_W_gat, L1_gnn_attn_l, L1_gnn_attn_r, L1_gnn_gat_bias, L2_gnn_Wq, L2_gnn_bq, L2_gnn_Wk,
                 L2_gnn_bk, L2_gnn_Wv, L2_gnn_bv, L2_gnn_Ws, L2_gnn_bs, L2_gnn_Wl, L2_gnn_bl, L2_gnn_Wr,
                 L2_gnn_gamma, L2_gnn_beta, L2_gnn_alpha_res, L3_gnn_weight, out, debug=None):
    k = Bag()
    dram = lambda n, s, d=F32: nc.dram_tensor(n, s, d).ap()
    k.ordered = [dram(f"ordered{n}", (E + SE,), I32) for n in range(4)]
    k.slots = [dram(f"slots{n}", (2 * SE + 2 * P,), I32) for n in range(4)]
    pairs_d, turned_d = dram("pairs_d", (NP, NP)), dram("turned_d", (NP, NP))
    feat_d = dram("feat_d", (NP, D))
    el_d = dram("el_d", (NP, H))
    key_d = dram("key_d", (NP, D))
    value_d = dram("value_d", (NP, D))
    rel_d = dram("rel_d", (R, NP, D))

    with ExitStack() as c:
        sb = lambda n, s, d=F32: c.enter_context(nc.sbuf_tensor(n, s, d))
        k.passed = nc.alloc_semaphore("passed")
        k.X = sb("X", [P, T, D])
        k.iota = sb("iota", [P, P])
        k.ident = sb("ident", [P, P])
        k.low = sb("low", [P, P])
        k.pcol = sb("pcol", [P, 1])
        k.ones = sb("ones", [P, P])
        k.zero = sb("zero", [P, D + H])
        k.starts = sb("starts", [1, 2 * T + 1], I32)
        k.slot_tile = sb("slot_tile", [P, S + 1])
        k.slot_tile_i = sb("slot_tile_i", [1, S + 1], I32)
        k.turns_i, k.group_turns_i = sb("turns_i", [1, S], I32), sb("group_turns_i", [1, S // 4], I32)
        k.deg_src, k.deg_dst = sb("deg_src", [P, T]), sb("deg_dst", [P, T])
        k.iota_b, k.zero_b = sb("iota_b", [P, P], BF16), sb("zero_b", [P, P], BF16)
        k.edge_pad = sb("edge_pad", [1, P], I32)
        k.src, k.dst, k.rel, k.weight, k.node, k.dloc = (
            sb(n, [P, S]) for n in ("src", "dst", "rel", "weight", "node", "dloc"))
        k.src_i, k.rel_i = sb("src_i", [P, S], I32), sb("rel_i", [P, S], I32)
        k.rows_dst, k.rows_w, k.pen_prev, k.pen_next = (
            sb(n, [SQ, SG, P]) for n in ("rows_dst", "rows_w", "pen_prev", "pen_next"))
        k.six = sb("six", [P, 6])
        k.two = sb("two", [P, 2])
        k.mv = sb("mv", [P, T, 2])
        k.rstd = sb("rstd", [P, T])
        col = sb("col", [P, T])

        k.slo, k.shi = (c.enter_context(nc.sbuf_tensor(n, [EP, EC], F32)) for n in ("slo", "shi"))
        prepare(nc, k, x, src, dst)
        order_edges(nc, k, [src, dst, edge_type_16, edge_weight1.rearrange("e a -> (e a)").bitcast(I32)], dst)
        fill_slots(nc, k)
        count_pairs(nc, k, pairs_d)

        with ExitStack() as l:
            sl = lambda n, s, d=F32: l.enter_context(nc.sbuf_tensor(n, s, d))
            w, b = sl("w0", [P, 2, D]), sl("b0", [P, D])
            load(nc, "l0", [(w[:], halves(L0_gnn_W)), (b[:], spread(L0_gnn_b))])
            inverse_root(nc, k, col)
            r = sl("r0", [P, T, D])
            scale_tiles(nc, r, k.X, col)
            if debug: debug(nc, 'y', r)
            agg = sl("agg0", [P, T, D])
            dense_product(nc, k, "d0", pairs_d, r, agg, col, turned_d)
            z = sl("z0", [P, D])

            def epilogue(dve, step, t, p):
                step(dve.tensor_tensor(z[:], p[:, 0:D], b[:], ALU.add))
                step(dve.scalar_tensor_tensor(z[:], z[:], 0.2, z[:], ALU.mult, ALU.max))
                step(dve.tensor_tensor(tile_of(r, t), tile_of(k.X, t), z[:], ALU.add))
                statistics(dve, step, k, r, t)
            project(nc, k, "p0", [(agg, None)], w, D, 6, epilogue)
            normalize(nc, k, "n0", r, k.X)
            if debug: debug(nc, 'x1', k.X)

        with ExitStack() as l:
            sl = lambda n, s, d=F32: l.enter_context(nc.sbuf_tensor(n, s, d))
            h = sl("h1", [P, T, D])
            er = sl("er", [P, T, H])
            scores = sl("scores", [P, S, H])
            w, w2 = sl("w1", [P, 2, D]), sl("w1g", [P, 2, D])
            b, al, ar, gb = (sl(n, [P, D]) for n in ("b1", "al", "ar", "gb"))
            z = sl("z1", [P, D])
            load(nc, "l1", [(w[:], halves(L1_gnn_W_lin)), (w2[:], halves(L1_gnn_W_gat)), (b[:], spread(L1_gnn_b_lin)),
                            (al[:], spread(L1_gnn_attn_l.rearrange("h f -> (h f)"))),
                            (ar[:], spread(L1_gnn_attn_r.rearrange("h f -> (h f)"))),
                            (gb[:], spread(L1_gnn_gat_bias))])
            project(nc, k, "p1", [(k.X, None)], w, D, 1,
                    lambda dve, step, t, p: step(dve.tensor_tensor(tile_of(h, t), p[:, 0:D], b[:], ALU.add)))
            with ExitStack() as f:
                feat = f.enter_context(nc.sbuf_tensor("feat", [P, T, D], F32))
                el = f.enter_context(nc.sbuf_tensor("el", [P, T, H], F32))

                def epilogue(dve, step, t, p):
                    step(dve.tensor_copy(tile_of(feat, t), p[:, 0:D]))
                    for a, to in ((al, el), (ar, er)):
                        step(dve.tensor_tensor(z[:], tile_of(feat, t), a[:], ALU.mult))
                        step(dve.tensor_reduce(tile_of(to, t), z[:].rearrange("p (h f) -> p h f", h=H), AX.X, ALU.add))
                project(nc, k, "p2", [(h, None)], w2, D, 5, epilogue, stores=[(feat, feat_d)])
                load(nc, "s2", [(el_d.rearrange("(t p) h -> p t h", p=P), el[:])])
            with ExitStack() as f:
                part = f.enter_context(nc.sbuf_tensor("er_edge", [P, S, H], F32))
                score_by_edge(nc, k, "a1", el_d, H, er, scores, part)
                best = f.enter_context(nc.sbuf_tensor("best", [P, S, H], F32))
                segment_maximum(nc, k, "m1", H, scores, best)
                attention_weights(nc, k, "w1", scores, part, best, H)
            with ExitStack() as f:
                k.acc = f.enter_context(nc.sbuf_tensor("acc1", [P, T, D + H], F32))
                sum_by_destination(nc, k, "e1", feat_d, k.src_i, per_head=scores)
                rs = f.enter_context(nc.sbuf_tensor("rs1", [P, T, H], F32))

                def before(dve, step):
                    step(dve.tensor_scalar(rs[:], k.acc[:, :, D:D + H], 1e-30, None, ALU.max))
                    step(dve.reciprocal(rs[:], rs[:]))

                def work(dve, step, t):
                    a = k.acc[:, bass.ds(t, 1), 0:D].rearrange("p a f -> p (a f)")
                    step(dve.tensor_tensor(z[:].rearrange("p (h f) -> p h f", h=H), a.rearrange("p (h f) -> p h f", h=H),
                                           tile_of(rs, t).unsqueeze(2).broadcast_to([P, H, HD]), ALU.mult))
                    step(dve.tensor_tensor(z[:], z[:], gb[:], ALU.add))
                    step(dve.scalar_tensor_tensor(z[:], z[:], 0.01, z[:], ALU.mult, ALU.max))
                    step(dve.tensor_tensor(tile_of(h, t), tile_of(h, t), z[:], ALU.add))
                    step(dve.tensor_tensor(tile_of(h, t), tile_of(h, t), tile_of(k.X, t), ALU.add))
                    statistics(dve, step, k, h, t)
                each_tile(nc, k, "t1", 8, before, work)
                normalize(nc, k, "n1", h, k.X)
            if debug: debug(nc, 'x2', k.X)

        with ExitStack() as l:
            sl = lambda n, s, d=F32: l.enter_context(nc.sbuf_tensor(n, s, d))
            h = sl("h2", [P, T, D])
            lg = sl("lg", [P, S, 1])
            z = sl("z2", [P, D])
            sage = [[sl(f"{n}{i}", [P, D]) for n in ("ga", "be", "bl")] for i in range(3)]
            wlr = [sl(f"wlr{i}", [P, 4, D]) for i in range(3)]
            alpha = sl("alpha", [P, 2])
            load(nc, "l2", [(alpha[:, 0:1], spread(L2_gnn_alpha_res))]
                 + [p for i in range(3) for p in (
                     (sage[i][0][:], spread(L2_gnn_gamma[i, :])), (sage[i][1][:], spread(L2_gnn_beta[i, :])),
                     (sage[i][2][:], spread(L2_gnn_bl[i, :])), (wlr[i][:, 0:2, :], halves(L2_gnn_Wl[i, :, :])),
                     (wlr[i][:, 2:4, :], halves(L2_gnn_Wr[i, :, :])))])
            with ExitStack() as f:
                q = f.enter_context(nc.sbuf_tensor("q2", [P, T, D], F32))
                with ExitStack() as g:
                    sg = lambda n, s: g.enter_context(nc.sbuf_tensor(n, s, F32))
                    kk, vv, w, b = sg("kk", [P, T, D]), sg("vv", [P, T, D]), sg("w2", [P, 2, 4 * D]), sg("b2", [P, 4 * D])
                    load(nc, "l3", [p for i, (m, v) in enumerate(((L2_gnn_Wq, L2_gnn_bq), (L2_gnn_Wk, L2_gnn_bk),
                                                                 (L2_gnn_Wv, L2_gnn_bv), (L2_gnn_Ws, L2_gnn_bs)))
                                    for p in ((w[:, :, i * D:(i + 1) * D], halves(m)),
                                              (b[:, i * D:(i + 1) * D], spread(v)))])

                    def epilogue(dve, step, t, p):
                        for i, to in enumerate((q, kk, vv, h)):
                            step(dve.tensor_tensor(tile_of(to, t), p[:, i * D:(i + 1) * D], b[:, i * D:(i + 1) * D], ALU.add))
                    project(nc, k, "p3", [(k.X, None)], w, 4 * D, 4, epilogue, stores=[(kk, key_d), (vv, value_d)])
                score_by_edge(nc, k, "a2", key_d, D, q, lg[:].rearrange("p s a -> p (s a)"), None)
            with ExitStack() as f:
                best = f.enter_context(nc.sbuf_tensor("best2", [P, S, 1], F32))
                segment_maximum(nc, k, "m2", 1, lg, best)
                attention_weights(nc, k, "w2", lg, None, best, 1)
            k.acc = sl("acc2", [P, T, D + 1])
            sum_by_destination(nc, k, "e2", value_d, k.src_i, weight=lg[:].rearrange("p s a -> p (s a)"), ones=True)

            def before(dve, step):
                step(dve.tensor_scalar(col[:], k.acc[:, :, D], 1e-30, None, ALU.max))
                step(dve.reciprocal(col[:], col[:]))

            def work(dve, step, t):
                a = k.acc[:, bass.ds(t, 1), 0:D].rearrange("p a f -> p (a f)")
                step(dve.scalar_tensor_tensor(tile_of(h, t), a, cols(col, t, 1), tile_of(h, t), ALU.mult, ALU.add))
                step(dve.tensor_scalar(tile_of(h, t), tile_of(h, t), 0.0, None, ALU.max))
            each_tile(nc, k, "t2", 2, before, work)
            if debug: debug(nc, 'h0', h)
            fold_scales(nc, alpha, sage)
            inverse_count(nc, k, col)
            for i in range(3):
                dense_product(nc, k, f"d{1 + i}", turned_d, h, k.acc, col)
                ga, be, _ = sage[i]

                def epilogue(dve, step, t, p, ga=ga, be=be, last=i == 2):
                    step(dve.tensor_tensor(z[:], p[:, 0:D], ga[:], ALU.mult))
                    step(dve.tensor_tensor(z[:], z[:], be[:], ALU.add))
                    step(dve.scalar_tensor_tensor(z[:], tile_of(h, t), alpha[:, 1:2], z[:], ALU.mult, ALU.add))
                    if last:
                        step(dve.scalar_tensor_tensor(tile_of(h, t), z[:], 0.0, tile_of(k.X, t), ALU.max, ALU.add))
                        statistics(dve, step, k, h, t)
                    else:
                        step(dve.tensor_scalar(tile_of(h, t), z[:], 0.0, None, ALU.max))
                project(nc, k, f"p{4 + i}", [(k.acc, None), (h, None)], wlr[i], D, 7 if i == 2 else 4, epilogue)
            normalize(nc, k, "n2", h, k.X)
            if debug: debug(nc, 'x3', k.X)

        with ExitStack() as l:
            sl = lambda n, s, d=F32: l.enter_context(nc.sbuf_tensor(n, s, d))
            with ExitStack() as f:
                w = f.enter_context(nc.sbuf_tensor("w3", [P, 2, R, D], F32))
                load(nc, "l4", [(w[:, a, :, :], L3_gnn_weight[:, a * P:(a + 1) * P, :].rearrange("r p n -> p r n"))
                                for a in range(2)])
                relation_tables(nc, k, w, rel_d)
            k.acc = sl("acc3", [P, T, D])
            sum_by_destination(nc, k, "e7", rel_d.rearrange("r n f -> (r n) f"), k.rel_i, weight=k.weight)

            def work(dve, step, t):
                step(dve.tensor_tensor(tile_of(k.acc, t), tile_of(k.acc, t), tile_of(k.X, t), ALU.add))
                statistics(dve, step, k, k.acc, t)
            each_tile(nc, k, "t3", 4, lambda dve, step: None, work)
            normalize(nc, k, "n3", k.acc, k.X, out)


def inverse_root(nc, k, col):
    with ExitStack() as c:
        c.enter_context(nc.cleanup_on_exit())
        vstep, rooted = nc.alloc_semaphore("r_v"), nc.alloc_semaphore("r_r")
        safe, given, square = (c.enter_context(nc.sbuf_tensor(n, [P, T], F32)) for n in ("safe", "given", "square"))
        block = c.enter_context(nc.Block())

        @block.vector
        def _(dve):
            step = Order(dve, vstep)
            step(dve.tensor_scalar(given[:], k.deg_src[:], 1.0, None, ALU.max))
            dve.wait_ge(rooted, 1)
            refine_root(dve, step, safe[:], given[:], square[:])
            step(dve.tensor_scalar(col[:], k.deg_src[:], 1.0, None, ALU.min))
            step(dve.tensor_tensor(col[:], col[:], safe[:], ALU.mult))

        @block.scalar
        def _(act):
            act.wait_ge(vstep, 1)
            act.activation(safe[:], given[:], ACT.Sqrt).then_inc(rooted, 1)


def inverse_count(nc, k, col):
    with ExitStack() as c:
        c.enter_context(nc.cleanup_on_exit())
        vstep = nc.alloc_semaphore("c_v")
        block = c.enter_context(nc.Block())

        @block.vector
        def _(dve):
            step = Order(dve, vstep)
            step(dve.tensor_scalar(col[:], k.deg_dst[:], 1.0, None, ALU.max))
            step(dve.reciprocal(col[:], col[:]))


def fold_scales(nc, alpha, sage):
    with ExitStack() as c:
        c.enter_context(nc.cleanup_on_exit())
        vstep, sig = nc.alloc_semaphore("f_v"), nc.alloc_semaphore("f_s")
        block = c.enter_context(nc.Block())

        @block.scalar
        def _(act):
            act.activation(alpha[:, 0:1], alpha[:, 0:1], ACT.Sigmoid).then_inc(sig, 1)

        @block.vector
        def _(dve):
            step = Order(dve, vstep)
            dve.wait_ge(sig, 1)
            step(dve.tensor_scalar(alpha[:, 1:2], alpha[:, 0:1], -1.0, 1.0, ALU.mult, ALU.add))
            for ga, be, bl in sage:
                step(dve.tensor_scalar(ga[:], ga[:], BN_SCALE, alpha[:, 0:1], ALU.mult, ALU.mult))
                step(dve.tensor_scalar(be[:], be[:], alpha[:, 0:1], None, ALU.mult))
                step(dve.tensor_tensor(bl[:], bl[:], ga[:], ALU.mult))
                step(dve.tensor_tensor(be[:], be[:], bl[:], ALU.add))


def scale_tiles(nc, to, x, col):
    with ExitStack() as c:
        c.enter_context(nc.cleanup_on_exit())
        done = nc.alloc_semaphore("sc_done")
        block = c.enter_context(nc.Block())

        @block.vector
        def _(dve):
            over_tiles(dve, lambda t, b: dve.tensor_scalar(tile_of(to, t), tile_of(x, t), cols(col, t, 1), None,
                                                           ALU.mult).then_inc(done, 1))
            dve.wait_ge(done, T)


def relation_tables(nc, k, w, rel_d):
    RP = R // 2
    with ExitStack() as c:
        c.enter_context(nc.cleanup_on_exit())
        sb = lambda n, s, d=F32: c.enter_context(nc.sbuf_tensor("q_" + n, s, d))
        sem = lambda n: nc.alloc_semaphore("q_" + n)
        xs = sb("xs", [P, 2, D])
        xt = sb("xt", [P, 2, 2, P])
        rows = sb("rows", [P, 2, R, D])
        flips = c.enter_context(nc.psum_tensor("q_flips", [P, 2, 512], F32))
        prods = c.enter_context(nc.psum_tensor("q_prods", [P, 4, 512], F32))
        staged, flipped, turned, multiplied, kept_a, kept_v = (
            sem("staged"), sem("flipped"), sem("turned"), sem("multiplied"), sem("kept_a"), sem("kept_v"))
        stored = [sem(f"stored{b}") for b in range(2)]
        block = c.enter_context(nc.Block())

        @block.sync
        def _(sp):
            def store(t, b):
                sp.wait_ge(kept_a, t * (RP // 2) + RP // 2 + 2)
                sp.wait_ge(kept_v, t * (RP // 2) + RP // 2 + 2)
                sp.dma_start(rel_d[:, bass.ds(t * P, P), :].rearrange("r p f -> p r f"), rows[:, b, :, :]).then_inc(stored[b], 16)
            over_tiles(sp, store)
            sp.wait_ge(stored[0], 16 * (T // 2 + 1))
            sp.wait_ge(stored[1], 16 * (T // 2))

        @block.tensor
        def _(pe):
            pe.sem_inc(flipped, 2)

            def tile(t, b):
                pe.wait_ge(staged, t + 1)
                pe.wait_ge(turned, t + 1)
                for h in range(2):
                    last = pe.transpose(flips[:, b, h * P:(h + 1) * P], xs[:, b, h * P:(h + 1) * P], k.ident[:])
                last.then_inc(flipped, 1)
                pe.wait_ge(turned, t + 3)
                for o in range(RP):
                    pe.wait_ge(kept_a if o % 2 == 0 else kept_v, t * (RP // 2) + o // 2 + 1)
                    for a in range(2):
                        last = pe.matmul(prods[:, o % 4, :], xt[:, b, a, :],
                                         w[:, a, 2 * o:2 * o + 2, :].rearrange("p r n -> p (r n)"),
                                         start=a == 0, stop=a == 1)
                    last.then_inc(multiplied, 1)
            over_tiles(pe, tile)

        @block.scalar
        def _(act):
            act.sem_inc(turned, 2)
            act.sem_inc(kept_a, 2)

            def stage(t, b):
                act.wait_ge(flipped, t + 1)
                act.sem_inc(k.passed, 1)
                act.copy(xs[:, b, :], tile_of(k.X, t)).then_inc(staged, 1)

            def tile(t, b):
                act.wait_ge(flipped, t + 3)
                act.copy(xt[:, b, :, :].rearrange("p a q -> p (a q)"), flips[:, b, 0:D]).then_inc(turned, 1)
                if reused(t):
                    act.wait_ge(stored[b], (t - b) * 8)
                for o in range(0, RP, 2):
                    act.wait_ge(multiplied, t * RP + o + 1)
                    act.copy(rows[:, b, 2 * o:2 * o + 2, :].rearrange("p r n -> p (r n)"),
                             prods[:, o % 4, :]).then_inc(kept_a, 1)
            stage(0, 0)
            stage(1, 1)
            tile(0, 0)
            stage(2, 0)
            tile(1, 1)
            with act.Fori(1, T // 2) as i:
                stage(2 * i + 1, 1)
                tile(2 * i, 0)
                stage(2 * i + 2, 0)
                tile(2 * i + 1, 1)
            tile(T - 1, 0)

        @block.vector
        def _(dve):
            dve.sem_inc(kept_v, 2)

            def tile(t, b):
                if reused(t):
                    dve.wait_ge(stored[b], (t - b) * 8)
                for o in range(1, RP, 2):
                    dve.wait_ge(multiplied, t * RP + o + 1)
                    dve.tensor_copy(rows[:, b, 2 * o:2 * o + 2, :].rearrange("p r n -> p (r n)"),
                                    prods[:, o % 4, :]).then_inc(kept_v, 1)
            over_tiles_after_two(dve, tile)


_INS = ['x', 'src', 'dst', 'edge_type_16', 'edge_weight1', 'L0_gnn_W', 'L0_gnn_b', 'L1_gnn_W_lin', 'L1_gnn_b_lin',
        'L1_gnn_W_gat', 'L1_gnn_attn_l', 'L1_gnn_attn_r', 'L1_gnn_gat_bias', 'L2_gnn_Wq', 'L2_gnn_bq', 'L2_gnn_Wk',
        'L2_gnn_bk', 'L2_gnn_Wv', 'L2_gnn_bv', 'L2_gnn_Ws', 'L2_gnn_bs', 'L2_gnn_Wl', 'L2_gnn_bl', 'L2_gnn_Wr',
        'L2_gnn_gamma', 'L2_gnn_beta', 'L2_gnn_alpha_res', 'L3_gnn_weight']


def kernel(**inputs):
    import concourse.bacc as _bacc
    from concourse.bass_utils import run_bass_kernel_spmd as _run

    nc = _bacc.Bacc("TRN2", target_bir_lowering=False, num_devices=1)
    arrays, args = {}, {}
    for name in _INS:
        a = np.ascontiguousarray(inputs[name])
        if a.ndim == 0:
            a = a.reshape(1)
        arrays[f"in_{name}"] = a
        args[name] = nc.dram_tensor(f"in_{name}", a.shape, mybir.dt.from_np(a.dtype), kind="ExternalInput").ap()
    out = nc.dram_tensor("out_0", (N, D), F32, kind="ExternalOutput").ap()
    graph_layers(nc, out=out, **args)
    r = _run(nc, [arrays], core_ids=[0])
    return r.results[0]["out_0"]
```

```python
from contextlib import ExitStack

import numpy as np
import concourse.bass as bass
from concourse import mybir

F32 = mybir.dt.float32
BF16 = mybir.dt.bfloat16
F16 = mybir.dt.float16
I32 = mybir.dt.int32
ALU = mybir.AluOpType
ACT = mybir.ActivationFunctionType
AX = mybir.AxisListType

P = 128
N = 3125
D = 256
E = 50000
H = 8
HD = D // H
R = 16
T = (N + P - 1) // P
NP = T * P
NLAST = N - (T - 1) * P
EP = 125
EC = E // EP
U = 16
IT = -(-(E // P + T) // U)
S = IT * U
SE = S * P
SG = 4
SQ = S // SG
RING = 8
G4 = 4
CH = 4
NTRASH = NP
BIG = 1.0e30
PAD_DST = float(1 << 20)
LN_EPS = 1e-5
BN_SCALE = 1.0 / float(np.sqrt(1.0 + 1e-5))


class Bag:
    pass


class Order:

    def __init__(self, eng, sem, base=0):
        self.eng, self.sem, self.n = eng, sem, base

    def __call__(self, ins):
        ins.then_inc(self.sem, 1)
        self.n = self.n + 1
        self.eng.wait_ge(self.sem, self.n)


def cols(ap, start, count):
    return ap[:, bass.ds(start, count)]


def tile_of(ap, t):
    return ap[:, bass.ds(t, 1), :].rearrange("p a f -> p (a f)")


def over_tiles(eng, body):
    with eng.Fori(0, T // 2) as i:
        body(2 * i, 0)
        body(2 * i + 1, 1)
    body(T - 1, 0)


def over_tiles_after_two(eng, body):
    body(0, 0)
    body(1, 1)
    with eng.Fori(1, T // 2) as i:
        body(2 * i, 0)
        body(2 * i + 1, 1)
    body(T - 1, 0)


def reused(t):
    return not isinstance(t, int) or t >= 2


def spread(ap, p=P):
    return bass.AP(ap.tensor, ap.offset, [[0, p]] + [list(x) for x in ap.ap])



def prepare(nc, k, x, src, dst):
    with ExitStack() as c:
        c.enter_context(nc.cleanup_on_exit())
        sb = lambda n, s, d=F32: c.enter_context(nc.sbuf_tensor("p_" + n, s, d))
        sem = lambda n: nc.alloc_semaphore("p_" + n)
        dn = sb("dn", [EP, EC], I32)
        nxt = sb("nxt", [EP, 1], I32)
        sn = sb("sn", [EP, EC], I32)
        bits = sb("bits", [EP, EC], I32)
        dtile = sb("dtile", [EP, EC])
        junk = sb("junk", [EP, EC])
        junk2 = sb("junk2", [EP, EC])
        per = sb("per", [EP, T + 2])
        row = sb("row", [1, 8, T + 2])
        rowi = sb("rowi", [1, 2, T + 2], I32)
        ends = sb("ends", [T, 1])
        ioj = sb("ioj", [T, S + 1])
        cmpj = sb("cmpj", [T, S + 1])
        turns, group_turns = sb("turns", [1, S]), sb("group_turns", [1, S // 4])
        small = c.enter_context(nc.psum_tensor("small", [P, 512], F32))
        mapp = c.enter_context(nc.psum_tensor("mapp", [P, 512], F32))
        x_in, e_in, zeroed = sem("x_in"), sem("e_in"), sem("zeroed")
        made, vstep, pstep = sem("made"), sem("vstep"), sem("pstep")
        counted = sem("counted")
        sums, rowed, mapped = sem("sums"), sem("rowed"), sem("mapped")
        block = c.enter_context(nc.Block())

        @block.sync
        def _(sp):
            sp.dma_start(sn[:], src.rearrange("(p c) -> p c", c=EC)).then_inc(e_in, 16)
            sp.dma_start(dn[:], dst.rearrange("(p c) -> p c", c=EC)).then_inc(e_in, 16)
            sp.wait_ge(zeroed, 1)
            sp.dma_start(nxt[0:EP - 1, :], dst.rearrange("(p c) -> p c", c=EC)[1:EP, 0:1],
                         allow_slow_non_contiguous=True).then_inc(e_in, 16)
            sp.dma_start(k.X[:, 0:T - 1, :], x[0:(T - 1) * P, :].rearrange("(t p) f -> p t f", p=P)).then_inc(x_in, 16)
            sp.wait_ge(zeroed, 2)
            sp.dma_start(k.X[0:NLAST, T - 1, :], x[(T - 1) * P:N, :]).then_inc(x_in, 16)
            sp.wait_ge(x_in, 32)

        @block.gpsimd
        def _(pool):
            step = Order(pool, pstep)
            pool.memset(nxt[:], NP).then_inc(zeroed, 1)
            pool.memset(k.X[:, T - 1, :], 0.0).then_inc(zeroed, 1)
            pool.iota(k.iota[:], [[1, P]], base=0, channel_multiplier=0,
                      allow_small_or_imprecise_dtypes=True).then_inc(made, 1)
            pool.iota(k.iota_b[:], [[1, P]], base=0, channel_multiplier=0,
                      allow_small_or_imprecise_dtypes=True).then_inc(made, 1)
            pool.iota(k.pcol[:], [[1, 1]], base=0, channel_multiplier=1,
                      allow_small_or_imprecise_dtypes=True).then_inc(made, 1)
            pool.iota(ioj[:], [[1, S + 1]], base=-1, channel_multiplier=0,
                      allow_small_or_imprecise_dtypes=True).then_inc(made, 1)
            pool.memset(k.ones[:], 1.0).then_inc(made, 1)
            pool.memset(k.zero_b[:], 0.0).then_inc(made, 1)
            pool.memset(k.zero[:], 0.0).then_inc(made, 1)
            step(pool.memset(k.ident[:], 0.0))
            pool.affine_select(out=k.ident[:], in_=k.ident[:], compare_op=ALU.not_equal, fill=1.0, base=0,
                               pattern=[[-1, P]], channel_multiplier=1).then_inc(made, 1)

        @block.vector
        def _(dve):
            step = Order(dve, vstep)
            dve.wait_ge(made, 8)
            dve.tensor_scalar(k.low[:], k.iota[:], k.pcol[:, 0:1], None, ALU.is_lt).then_inc(vstep, 1)
            dve.memset(per[:], 0.0).then_inc(vstep, 1)
            step.n = 2
            dve.wait_ge(vstep, 2)
            dve.wait_ge(e_in, 48)
            step(dve.tensor_single_scalar(bits[:], sn[:], P - 1, ALU.bitwise_and))
            step(dve.tensor_copy(k.slo[:], bits[:]))
            step(dve.tensor_single_scalar(bits[:], sn[:], 7, ALU.arith_shift_right))
            step(dve.tensor_copy(k.shi[:], bits[:]))
            step(dve.tensor_single_scalar(bits[:], dn[:], 7, ALU.arith_shift_right))
            step(dve.tensor_copy(dtile[:], bits[:]))
            for t in range(T):
                step(dve.tensor_scalar(junk[:], dtile[:], float(t), 0.0, ALU.is_equal, ALU.add,
                                       accum_out=per[:, t:t + 1]))
            step(dve.tensor_tensor(junk2[:, 0:EC - 1], dn[:, 1:EC], dn[:, 0:EC - 1], ALU.is_lt))
            step(dve.tensor_tensor(junk2[:, EC - 1:EC], nxt[:], dn[:, EC - 1:EC], ALU.is_lt))
            step(dve.tensor_reduce(per[:, T:T + 1], junk2[:], AX.X, ALU.add))
            dve.sem_inc(sums, 1)
            dve.wait_ge(counted, 1)
            step(dve.tensor_copy(row[0:1, 0, :], small[0:1, 0:T + 2]))
            step(dve.tensor_scalar(row[0:1, 1, :], row[0:1, 0, :], float(P - 1), None, ALU.add))
            step(dve.tensor_copy(rowi[0:1, 0, :], row[0:1, 1, :]))
            step(dve.tensor_single_scalar(rowi[0:1, 1, :], rowi[0:1, 0, :], 7, ALU.arith_shift_right))
            step(dve.tensor_copy(row[0:1, 2, :], rowi[0:1, 1, :]))
            step(dve.tensor_scalar(row[0:1, 2, :], row[0:1, 2, :], 1.0, None, ALU.max))
            step(dve.tensor_tensor_scan(row[0:1, 3, 0:T], k.zero[0:1, 0:T], row[0:1, 0, 0:T], 0.0, ALU.add, ALU.add))
            step(dve.tensor_tensor_scan(row[0:1, 4, 0:T], k.zero[0:1, 0:T], row[0:1, 2, 0:T], 0.0, ALU.add, ALU.add))
            step(dve.tensor_tensor(row[0:1, 5, 0:T], row[0:1, 3, 0:T], row[0:1, 0, 0:T], ALU.subtract))
            step(dve.tensor_tensor(row[0:1, 6, 0:T], row[0:1, 4, 0:T], row[0:1, 2, 0:T], ALU.subtract))
            step(dve.tensor_scalar(row[0:1, 6, 0:T], row[0:1, 6, 0:T], float(P), None, ALU.mult))
            step(dve.tensor_copy(k.starts[0:1, 0:T], row[0:1, 5, 0:T]))
            step(dve.tensor_copy(k.starts[0:1, T:2 * T], row[0:1, 6, 0:T]))
            step(dve.tensor_scalar(row[0:1, 7, 0:1], row[0:1, 0, T:T + 1], 1.0, None, ALU.min))
            step(dve.tensor_copy(k.starts[0:1, 2 * T:2 * T + 1], row[0:1, 7, 0:1]))
            dve.sem_inc(rowed, 1)
            dve.wait_ge(counted, 2)
            step(dve.tensor_copy(ends[:], small[0:T, 64:65]))
            step(dve.tensor_scalar(cmpj[:], ioj[:], ends[:, 0:1], None, ALU.is_ge))
            dve.sem_inc(mapped, 1)
            dve.wait_ge(counted, 3)
            step(dve.tensor_scalar(k.slot_tile[:], mapp[:, 0:S + 1], float(T - 1), None, ALU.min))
            step(dve.tensor_copy(k.slot_tile_i[0:1, :], k.slot_tile[0:1, :]))
            step(dve.tensor_tensor(turns[:], k.slot_tile[0:1, 1:S + 1], k.slot_tile[0:1, 0:S], ALU.not_equal))
            step(dve.tensor_copy(k.turns_i[:], turns[:]))
            step(dve.tensor_reduce(group_turns[:], turns[:].rearrange("p (g u) -> p g u", u=4), AX.X, ALU.add))
            step(dve.tensor_copy(k.group_turns_i[:], group_turns[:]))

        @block.tensor
        def _(pe):
            pe.wait_ge(made, 8)
            pe.wait_ge(sums, 1)
            pe.matmul(small[0:1, 0:T + 2], k.ones[0:EP, 0:1], per[:], start=True, stop=True).then_inc(counted, 1)
            pe.wait_ge(rowed, 1)
            pe.matmul(small[0:T, 64:65], row[0:1, 4, 0:T], k.ones[0:1, 0:1], start=True, stop=True).then_inc(counted, 1)
            pe.wait_ge(mapped, 1)
            pe.matmul(mapp[:, 0:S + 1], k.ones[0:T, :], cmpj[:], start=True, stop=True).then_inc(counted, 1)


def order_edges(nc, k, fields, dst):
    with ExitStack() as c:
        c.enter_context(nc.cleanup_on_exit())
        sb = lambda n, s, d=F32: c.enter_context(nc.sbuf_tensor("o_" + n, s, d))
        sem = lambda n: nc.alloc_semaphore("o_" + n)
        padi = sb("padi", [P, SE // P], I32)
        padz = sb("padz", [P, SE // P], I32)
        dni = sb("dni", [EP, EC], I32)
        dnf = sb("dnf", [EP, EC])
        en = sb("en", [EP, EC])
        BK = EP * 25
        NB = E // BK
        keys = sb("keys", [EP, BK], I32)
        keyf = sb("keyf", [EP, BK])
        place = sb("place", [EP, BK])
        before = sb("before", [EP, BK])
        hit = sb("hit", [EP, BK])
        two = sb("two", [EP, 2])
        rank = sb("rank", [EP, EC])
        ranki = sb("ranki", [EP, EC], I32)
        rk1 = sb("rk1", [EP, 1], I32)
        fl = [sb(f"fl{n}", [EP, EC], I32) for n in range(4)]
        f1 = sb("f1", [EP, 4], I32)
        padded, pads, copied = sem("padded"), sem("pads"), sem("copied")
        iot, keyed, vstep, ranked, put = sem("iot"), sem("keyed"), sem("vstep"), sem("ranked"), sem("put")
        bl, fields_in, pstep = sem("bl"), sem("fields_in"), sem("pstep")
        block = c.enter_context(nc.Block())

        @block.sync
        def _(sp):
            unordered = sp.value_load(k.starts[0:1, 2 * T:2 * T + 1], min_val=0, max_val=1)
            sp.wait_ge(padded, 2)
            for f in range(4):
                sp.dma_start(k.ordered[f][E:E + SE].rearrange("(p c) -> p c", p=P),
                             (padi if f == 1 else padz)[:]).then_inc(pads, 16)
            with sp.If(unordered == 0):
                for f in range(4):
                    sp.dma_start(k.ordered[f][0:E].rearrange("(a b) -> a b", a=16),
                                 fields[f].rearrange("(a b) -> a b", a=16)).then_inc(copied, 16)
                sp.wait_ge(copied, 64)
            with sp.If(unordered != 0):
                sp.dma_start(dni[:], dst.rearrange("(p c) -> p c", c=EC)).then_inc(fields_in, 16)
                for f in range(4):
                    sp.dma_start(fl[f][:], fields[f].rearrange("(p c) -> p c", c=EC)).then_inc(fields_in, 16)
                with sp.Fori(0, NB) as b:
                    sp.wait_ge(bl, b + 1)
                    sp.dma_start(keys[:],
                                 bass.AP(dst.tensor, 0, [[0, EP], [1, E]])[:, bass.ds(b * BK, BK)]).then_inc(keyed, 16)
                sp.wait_ge(bl, NB + 1)
            sp.wait_ge(pads, 64)

        @block.gpsimd
        def _(pool):
            unordered = pool.value_load(k.starts[0:1, 2 * T:2 * T + 1], min_val=0, max_val=1)
            step = Order(pool, pstep)
            pool.memset(padi[:], int(PAD_DST)).then_inc(padded, 1)
            pool.memset(padz[:], 0).then_inc(padded, 1)
            with pool.If(unordered != 0):
                pool.iota(en[:], [[1, EC]], base=0, channel_multiplier=EC,
                          allow_small_or_imprecise_dtypes=True).then_inc(iot, 1)
                pool.iota(place[:], [[1, BK]], base=0, channel_multiplier=0,
                          allow_small_or_imprecise_dtypes=True).then_inc(iot, 1)
                pool.wait_ge(ranked, 1)
                pool.wait_ge(fields_in, 80)
                with pool.Fori(0, EC) as i:
                    step.n = i * 5
                    step(pool.tensor_copy(rk1[:], cols(ranki, i, 1)))
                    for f in range(4):
                        step(pool.tensor_copy(f1[:, f:f + 1], cols(fl[f], i, 1)))
                    for f in range(4):
                        pool.sem_inc(k.passed, 1)
                        pool.indirect_dma_start(k.ordered[f].rearrange("(e a) -> e a", a=1),
                                                bass.IndirectOffsetOnAxis(ap=rk1[:, 0:1], axis=0),
                                                f1[:, f:f + 1], None).then_inc(put, 16)
                    pool.wait_ge(put, i * 64 + 64)
                    pool.sem_inc(k.passed, 1)

        @block.vector
        def _(dve):
            unordered = dve.value_load(k.starts[0:1, 2 * T:2 * T + 1], min_val=0, max_val=1)
            with dve.If(unordered != 0):
                step = Order(dve, vstep)
                dve.sem_inc(bl, 1)
                dve.wait_ge(fields_in, 80)
                dve.wait_ge(iot, 2)
                step(dve.tensor_copy(dnf[:], dni[:]))
                step(dve.memset(rank[:], 0.0))
                with dve.Fori(0, NB) as b:
                    step.n = 2 + b * (2 + EC * 5)
                    dve.wait_ge(keyed, b * 16 + 16)
                    step(dve.tensor_copy(keyf[:], keys[:]))
                    dve.sem_inc(k.passed, 1)
                    with dve.Fori(0, EC) as i:
                        step.n = 3 + b * (2 + EC * 5) + i * 5
                        step(dve.tensor_scalar(hit[:], keyf[:], cols(dnf, i, 1), 0.0, ALU.is_lt, ALU.add,
                                               accum_out=two[:, 0:1]))
                        step(dve.tensor_scalar(before[:], place[:], cols(en, i, 1), None, ALU.is_lt))
                        step(dve.scalar_tensor_tensor(hit[:], keyf[:], cols(dnf, i, 1), before[:], ALU.is_equal,
                                                      ALU.mult, accum_out=two[:, 1:2]))
                        step(dve.tensor_tensor(cols(rank, i, 1), cols(rank, i, 1), two[:, 0:1], ALU.add))
                        step(dve.tensor_tensor(cols(rank, i, 1), cols(rank, i, 1), two[:, 1:2], ALU.add))
                        dve.sem_inc(k.passed, 1)
                    step.n = 3 + b * (2 + EC * 5) + EC * 5
                    step(dve.tensor_scalar(en[:], en[:], float(-BK), None, ALU.add))
                    dve.sem_inc(bl, 1)
                dve.tensor_copy(ranki[:], rank[:]).then_inc(ranked, 1)


def fill_slots(nc, k):
    with ExitStack() as c:
        c.enter_context(nc.cleanup_on_exit())
        sb = lambda n, s, d=F32: c.enter_context(nc.sbuf_tensor("f_" + n, s, d))
        sem = lambda n: nc.alloc_semaphore("f_" + n)
        rows_i = sb("rows_i", [SQ, 2, SG, P], I32)
        rows_t = sb("rows_t", [SQ, SG, P], I32)
        rows_f = sb("rows_f", [SQ, 2, SG, P])
        rows_p = sb("rows_p", [SQ, SG, P], I32)
        rows_n = sb("rows_n", [SQ, SG, P], I32)
        shifted = sb("shifted", [SQ, SG, P])
        lob = sb("lob", [EP, 8, P], BF16)
        hib = sb("hib", [EP, 8, T], BF16)
        flips = c.enter_context(nc.psum_tensor("flips", [P, 4, 512], F32))
        hist = c.enter_context(nc.psum_tensor("hist", [P, 512], F32))
        hot, used, cleared = sem("hot"), sem("used"), sem("cleared")
        laid, rows, vstep, turned, flipped, kept = (sem("laid"), sem("rows"), sem("vstep"), sem("turned"),
                                                    sem("flipped"), sem("kept"))
        ends_in, pstep = sem("ends_in"), sem("pstep")
        block = c.enter_context(nc.Block())

        @block.sync
        def _(sp):
            sp.wait_ge(ends_in, 32)
            for t in range(T):
                first = sp.value_load(k.starts[0:1, t:t + 1], min_val=0, max_val=E)
                place = sp.value_load(k.starts[0:1, T + t:T + t + 1], min_val=0, max_val=SE)
                for f in range(4):
                    sp.dma_start(k.slots[f][bass.ds(place + P, SE)].rearrange("(a b) -> a b", a=16),
                                 k.ordered[f][bass.ds(first, SE)].rearrange("(a b) -> a b", a=16)).then_inc(laid, 16)
                sp.wait_ge(laid, 64 * (t + 1))
            flat = lambda f, o: k.slots[f][o:o + SE].rearrange("(g q p) -> q g p", q=SQ, p=P)
            sp.dma_start(rows_i[:, 0, :, :], flat(0, P)).then_inc(rows, 16)
            sp.dma_start(rows_i[:, 1, :, :], flat(1, P)).then_inc(rows, 16)
            sp.dma_start(rows_t[:], flat(2, P)).then_inc(rows, 16)
            sp.dma_start(k.rows_w[:], k.slots[3][P:P + SE].bitcast(F32).rearrange("(g q p) -> q g p", q=SQ, p=P)).then_inc(rows, 16)
            sp.dma_start(rows_p[:], flat(1, P - 1)).then_inc(rows, 16)
            sp.dma_start(rows_n[:], flat(1, P + 1)).then_inc(rows, 16)
            sp.wait_ge(rows, 96)

        @block.gpsimd
        def _(pool):
            pool.memset(k.edge_pad[:], -1).then_inc(pstep, 1)
            pool.wait_ge(pstep, 1)
            for at in (0, P + SE):
                pool.dma_start(k.slots[1][at:at + P].rearrange("(a b) -> a b", a=1), k.edge_pad[:]).then_inc(ends_in, 16)
            pool.wait_ge(ends_in, 32)

        @block.vector
        def _(dve):
            dve.sem_inc(used, 1)
            with dve.Fori(0, EC // 8) as i:
                dve.wait_ge(used, i + 1)
                for u in range(8):
                    dve.tensor_scalar(lob[:, u, :], k.iota_b[0:EP, :], cols(k.slo, i * 8 + u, 1), None,
                                      ALU.is_equal).then_inc(hot, 1)
                    dve.tensor_scalar(hib[:, u, :], k.iota_b[0:EP, 0:T], cols(k.shi, i * 8 + u, 1), None,
                                      ALU.is_equal).then_inc(hot, 1)
            step = Order(dve, vstep)
            dve.wait_ge(cleared, 1)
            step(dve.tensor_copy(k.deg_src[:], hist[:, 0:T]))
            dve.wait_ge(rows, 96)
            step(dve.tensor_copy(rows_f[:, 0, :, :], rows_i[:, 0, :, :]))
            step(dve.tensor_copy(k.rows_dst[:], rows_i[:, 1, :, :]))
            step(dve.tensor_copy(rows_f[:, 1, :, :], rows_t[:]))
            dve.sem_inc(turned, 1)
            for links, whole in ((rows_p, k.pen_prev), (rows_n, k.pen_next)):
                step(dve.tensor_copy(shifted[:], links[:]))
                step(dve.tensor_tensor(whole[:], k.rows_dst[:], shifted[:], ALU.is_equal))
                step(dve.tensor_scalar(whole[:], whole[:], -1.0, BIG, ALU.add, ALU.mult))
            for f, to in enumerate((k.src, k.dst, k.rel, k.weight)):
                dve.wait_ge(flipped, f + 1)
                step(dve.tensor_copy(to[:, 0:S].rearrange("p (g q) -> p g q", g=SG),
                                     flips[:, f, 0:S].rearrange("p (g q) -> p g q", g=SG)))
            step(dve.tensor_scalar(k.node[:], k.slot_tile[:, 1:S + 1], float(P), k.pcol[:, 0:1], ALU.mult, ALU.add))
            step(dve.tensor_scalar(k.dloc[:], k.node[:], -1.0, k.pcol[:, 0:1], ALU.mult, ALU.add))
            step(dve.tensor_tensor(k.dloc[:], k.dloc[:], k.dst[:], ALU.add))
            step(dve.tensor_copy(k.src_i[:], k.src[:]))
            step(dve.tensor_scalar(k.rel[:], k.rel[:], float(NP), None, ALU.mult))
            step(dve.tensor_tensor(k.rel[:], k.rel[:], k.src[:], ALU.add))
            step(dve.tensor_copy(k.rel_i[:], k.rel[:]))

        @block.tensor
        def _(pe):
            pe.matmul(hist[:, 0:T], k.zero_b[0:EP, 0:P], k.zero_b[0:EP, 0:T], start=True, stop=False)
            with pe.Fori(0, EC // 8) as i:
                for u in range(8):
                    pe.wait_ge(hot, i * 16 + 2 * u + 2)
                    last = pe.matmul(hist[:, 0:T], lob[:, u, :], hib[:, u, :], start=False, stop=False)
                last.then_inc(used, 1)
            pe.matmul(hist[:, 0:T], k.zero_b[0:EP, 0:P], k.zero_b[0:EP, 0:T], start=False, stop=True).then_inc(cleared, 1)
            pe.wait_ge(turned, 1)
            for f in range(4):
                for g in range(SG):
                    rows_of = (rows_f[:, 0, g, :], k.rows_dst[:, g, :], rows_f[:, 1, g, :], k.rows_w[:, g, :])[f]
                    last = pe.transpose(flips[:, f, g * SQ:(g + 1) * SQ], rows_of, k.ident[0:SQ, 0:SQ])
                last.then_inc(flipped, 1)



def count_pairs(nc, k, pairs_d):
    HALF = NP // 2
    BANKS = -(-NP // 512)
    COPIES = BANKS + 1
    with ExitStack() as c:
        c.enter_context(nc.cleanup_on_exit())
        sb = lambda n, s, d=F32: c.enter_context(nc.sbuf_tensor("c_" + n, s, d))
        sem = lambda n: nc.alloc_semaphore("c_" + n)
        places = sb("places", [P, HALF], F16)
        upper = sb("upper", [P, S])
        hot_d = sb("hot_d", [P, 4, P], BF16)
        hot_s = sb("hot_s", [P, 4, NP + 1], BF16)
        zero = sb("zero", [P, 512], BF16)
        rows = sb("rows", [P, 2, NP])
        counts = c.enter_context(nc.psum_tensor("c_counts", [P, BANKS, 512], F32))
        ready, made, used, full, copied = sem("ready"), sem("made"), sem("used"), sem("full"), sem("copied")
        made_d = sem("made_d")
        stored = [sem(f"stored{b}") for b in range(2)]
        width = [min(512, NP - b * 512) for b in range(BANKS)]
        taken = [w + (b == BANKS - 1) for b, w in enumerate(width)]
        block = c.enter_context(nc.Block())

        @block.gpsimd
        def _(pool):
            pool.iota(places[:], [[1, HALF]], base=0, channel_multiplier=0,
                      allow_small_or_imprecise_dtypes=True).then_inc(ready, 1)
            pool.memset(zero[:], 0.0).then_inc(ready, 1)
            pool.memset(hot_s[:, :, NP:NP + 1], 1.0).then_inc(ready, 1)

        @block.vector
        def _(dve):
            dve.tensor_scalar(upper[:], k.src[:], float(-HALF), None, ALU.add).then_inc(ready, 1)
            dve.wait_ge(ready, 4)
            with dve.Fori(0, S // 4) as i:
                for u in range(4):
                    j = i * 4 + u
                    dve.wait_ge(used, j + 1)
                    dve.tensor_scalar(hot_d[:, u, :], k.iota_b[:], cols(k.dloc, j, 1), None,
                                      ALU.is_equal).then_inc(made, 1)
                    dve.tensor_scalar(hot_s[:, u, 0:HALF], places[:], cols(k.src, j, 1), None,
                                      ALU.is_equal).then_inc(made, 1)
                    dve.tensor_scalar(hot_s[:, u, HALF:NP], places[:], cols(upper, j, 1), None,
                                      ALU.is_equal).then_inc(made, 1)

        @block.tensor
        def _(pe):
            pe.sem_inc(used, 4)
            pe.wait_ge(ready, 4)

            def zeros(b, start):
                return pe.matmul(counts[:, b, 0:taken[b]], zero[:, 0:P], zero[:, 0:taken[b]],
                                 start=start, stop=not start)

            def multiply(u, j):
                pe.wait_ge(made, j * 3 + 3)
                for b in range(BANKS):
                    last = pe.matmul(counts[:, b, 0:taken[b]], hot_d[:, u, :],
                                     hot_s[:, u, b * 512:b * 512 + taken[b]], start=False, stop=False)
                last.then_inc(used, 1)

            for b in range(BANKS):
                zeros(b, True)
            with pe.Fori(0, S // 4) as i:
                turns = pe.value_load(k.group_turns_i[0:1, bass.ds(i, 1)], min_val=0, max_val=4)
                with pe.If(turns == 0):
                    for u in range(4):
                        multiply(u, i * 4 + u)
                with pe.If(turns != 0):
                    for u in range(4):
                        j = i * 4 + u
                        first = pe.value_load(k.turns_i[0:1, bass.ds(j, 1)], min_val=0, max_val=1)
                        with pe.If(first != 0):
                            t = pe.value_load(k.slot_tile_i[0:1, bass.ds(j + 1, 1)], min_val=0, max_val=T - 1)
                            for b in range(BANKS):
                                last = zeros(b, False)
                            last.then_inc(full, 1)
                            for b in range(BANKS):
                                pe.wait_ge(copied, t * COPIES + (b + 1 if b < BANKS - 1 else COPIES))
                                zeros(b, True)
                        multiply(u, j)
            for b in range(BANKS):
                last = zeros(b, False)
            last.then_inc(full, 1)

        @block.scalar
        def _(act):
            act.sem_inc(copied, COPIES)

            def copy(t, b):
                act.wait_ge(full, t + 1)
                act.sem_inc(k.passed, 1)
                if reused(t):
                    act.wait_ge(stored[b], (t - b) * 8)
                act.sem_inc(k.passed, 1)
                for n in range(BANKS):
                    if n == BANKS - 1:
                        act.copy(cols(k.deg_dst, t, 1), counts[:, n, width[n]:width[n] + 1]).then_inc(copied, 1)
                    act.copy(rows[:, b, n * 512:n * 512 + width[n]], counts[:, n, 0:width[n]]).then_inc(copied, 1)
            over_tiles_after_two(act, copy)

        @block.sync
        def _(sp):
            def store(t, b):
                sp.wait_ge(copied, t * COPIES + 2 * COPIES)
                sp.dma_start(pairs_d[bass.ds(t * P, P), :], rows[:, b, :]).then_inc(stored[b], 16)
            over_tiles(sp, store)
            sp.wait_ge(stored[0], 16 * (T // 2 + 1))
            sp.wait_ge(stored[1], 16 * (T // 2))


def dense_product(nc, k, name, mat_d, rows, to, column, turned_d=None):
    TG = -(-T // 4)
    with ExitStack() as c:
        c.enter_context(nc.cleanup_on_exit())
        sb = lambda n, s, d=F32: c.enter_context(nc.sbuf_tensor(name + n, s, d))
        sem = lambda n: nc.alloc_semaphore(name + n)
        blk = sb("blk", [P, 2, T, P])
        line = sb("line", [P, 2, NP]) if turned_d is not None else None
        prods = c.enter_context(nc.psum_tensor(name + "prods", [P, 2, 512], F32))
        flips = c.enter_context(nc.psum_tensor(name + "flips", [P, 4, 512], F32))
        multiplied, taken, flipped, lined = sem("multiplied"), sem("taken"), sem("flipped"), sem("lined")
        loaded = [sem(f"loaded{b}") for b in range(2)]
        stored = [sem(f"stored{b}") for b in range(2)]
        block = c.enter_context(nc.Block())

        @block.sync
        def _(sp):
            def load_block(t, b):
                sp.wait_ge(multiplied, t + 1)
                sp.dma_start(blk[:, b, :, :], mat_d[:, bass.ds(t * P, P)].rearrange(
                    "(a p) q -> p a q", p=P)).then_inc(loaded[b], 16)
            over_tiles(sp, load_block)

        @block.gpsimd
        def _(pool):
            if turned_d is not None:
                def store(t, b):
                    pool.wait_ge(lined, t * TG + TG + 4)
                    pool.sem_inc(k.passed, 1)
                    pool.dma_start(turned_d[bass.ds(t * P, P), :], line[:, b, :]).then_inc(stored[b], 16)
                over_tiles(pool, store)
                pool.wait_ge(stored[0], 16 * (T // 2 + 1))
                pool.wait_ge(stored[1], 16 * (T // 2))

        @block.tensor
        def _(pe):
            pe.sem_inc(multiplied, 2)

            def before(g):
                return g - 4 if g >= 4 else max(n for n in range(TG) if n % 4 == g) - TG

            def tile(t, b):
                pe.wait_ge(loaded[b], (t - b) * 8 + 16)
                if turned_d is not None:
                    for g in range(TG):
                        pe.wait_ge(lined, t * TG + before(g) + 5)
                        for a in range(4 * g, min(T, 4 * g + 4)):
                            last = pe.transpose(flips[:, (g % 4), (a % 4) * P:(a % 4 + 1) * P],
                                                blk[:, b, a, :], k.ident[:])
                        last.then_inc(flipped, 1)
                        if g == 0:
                            pe.wait_ge(taken, t + 1)
                        for a in range(4 * g, min(T, 4 * g + 4)):
                            last = pe.matmul(prods[:, b, 0:D], blk[:, b, a, :], rows[:, a, 0:D],
                                             start=a == 0, stop=a == T - 1)
                    last.then_inc(multiplied, 1)
                else:
                    pe.wait_ge(taken, t + 1)
                    for a in range(T):
                        last = pe.matmul(prods[:, b, 0:D], blk[:, b, a, :], rows[:, a, 0:D],
                                         start=a == 0, stop=a == T - 1)
                    last.then_inc(multiplied, 1)
            over_tiles(pe, tile)

        @block.vector
        def _(dve):
            dve.sem_inc(taken, 2)

            def take(t, b):
                dve.wait_ge(multiplied, t + 3)
                dve.tensor_scalar(to[:, bass.ds(t, 1), 0:D].rearrange("p a f -> p (a f)"), prods[:, b, 0:D],
                                  cols(column, t, 1), None, ALU.mult).then_inc(taken, 1)
            over_tiles(dve, take)
            dve.wait_ge(taken, T + 2)

        @block.scalar
        def _(act):
            if turned_d is not None:
                act.sem_inc(lined, 4)

                def copy(t, b):
                    if reused(t):
                        act.wait_ge(stored[b], (t - b) * 8)
                    for g in range(TG):
                        n = min(4, T - 4 * g) * P
                        act.wait_ge(flipped, t * TG + g + 1)
                        act.copy(line[:, b, 4 * g * P:4 * g * P + n], flips[:, g % 4, 0:n]).then_inc(lined, 1)
                over_tiles_after_two(act, copy)


def dense_attention(nc, k, query_d, key_t, value, pairs_d, h):
    CHUNKS = -(-NP // 512)
    width = [min(512, NP - n * 512) for n in range(CHUNKS)]
    GROUPS = -(-T // 4)
    SCALE = 1.0 / float(np.sqrt(D))
    BUFS = 3

    def before(n, count):
        return n - BUFS if n >= BUFS else max(m for m in range(count) if m % BUFS == n) - count

    with ExitStack() as c:
        c.enter_context(nc.cleanup_on_exit())
        sb = lambda n, s, d=F32: c.enter_context(nc.sbuf_tensor("g_" + n, s, d))
        sem = lambda n: nc.alloc_semaphore("g_" + n)
        q = sb("q", [P, 2, 2, P])
        pairs = sb("pairs", [P, 2, NP])
        absent = sb("absent", [P, 2, NP], BF16)
        probs = sb("probs", [P, 2, NP])
        tops = sb("tops", [P, CHUNKS])
        top1 = sb("top1", [P, 1])
        top = sb("top", [P, 2])
        inv = sb("inv", [P, 1])
        turned = sb("turned", [P, BUFS, 4, P])
        scores = c.enter_context(nc.psum_tensor("g_scores", [P, BUFS, 512], F32))
        flips = c.enter_context(nc.psum_tensor("g_flips", [P, BUFS, 512], F32))
        sums = c.enter_context(nc.psum_tensor("g_sums", [P, 2, 512], F32))
        oned, flagged, scored, masked, vstep, topped, exped, weighed = (
            sem("oned"), sem("flagged"), sem("scored"), sem("masked"), sem("vstep"), sem("topped"),
            sem("exped"), sem("weighed"))
        flipped, copied, multiplied, finished = sem("flipped"), sem("copied"), sem("multiplied"), sem("finished")
        asked = [sem(f"asked{b}") for b in range(2)]
        loaded = [sem(f"loaded{b}") for b in range(2)]
        block = c.enter_context(nc.Block())

        @block.sync
        def _(sp):
            def fetch(t, b):
                sp.wait_ge(weighed, t + 1)
                sp.dma_start(pairs[:, b, :], pairs_d[bass.ds(t * P, P), :]).then_inc(loaded[b], 16)
                sp.dma_start(q[:, b, :, :], query_d[:, :, bass.ds(t * P, P)]).then_inc(asked[b], 16)
            over_tiles(sp, fetch)

        @block.gpsimd
        def _(pool):
            pool.sem_inc(weighed, 2)
            pool.memset(value[:, :, D:D + 1], 1.0).then_inc(oned, 1)

            def flag(t, b):
                pool.wait_ge(loaded[b], (t - b) * 8 + 16)
                pool.sem_inc(k.passed, 1)
                pool.tensor_scalar(absent[:, b, :], pairs[:, b, :], 0.0, -BIG, ALU.is_equal, ALU.mult).then_inc(flagged, 1)

            def weigh(t, b):
                pool.wait_ge(exped, t + 1)
                pool.sem_inc(k.passed, 1)
                pool.tensor_tensor(probs[:, b, :], probs[:, b, :], pairs[:, b, :], ALU.mult).then_inc(weighed, 1)
            flag(0, 0)
            with pool.Fori(0, T // 2) as i:
                flag(2 * i + 1, 1)
                weigh(2 * i, 0)
                flag(2 * i + 2, 0)
                weigh(2 * i + 1, 1)
            weigh(T - 1, 0)

        @block.tensor
        def _(pe):
            pe.sem_inc(multiplied, BUFS)

            def score(t, b):
                pe.wait_ge(asked[b], (t - b) * 8 + 16)
                for n in range(CHUNKS):
                    pe.wait_ge(masked, t * CHUNKS + before(n, CHUNKS) + BUFS + 1)
                    for a in range(2):
                        last = pe.matmul(scores[:, n % BUFS, 0:width[n]], q[:, b, a, :],
                                         key_t[:, a, n * 512:n * 512 + width[n]], start=a == 0, stop=a == 1)
                    last.then_inc(scored, 1)

            def total(t, b):
                def flip(g):
                    pe.wait_ge(copied, t * GROUPS + before(g, GROUPS) + BUFS + 1)
                    for a in range(4 * g, min(T, 4 * g + 4)):
                        last = pe.transpose(flips[:, g % BUFS, (a % 4) * P:(a % 4 + 1) * P],
                                            probs[:, b, a * P:(a + 1) * P], k.ident[:])
                    last.then_inc(flipped, 1)

                pe.wait_ge(weighed, t + 3)
                flip(0)
                for g in range(GROUPS):
                    if g + 1 < GROUPS:
                        flip(g + 1)
                    if g == 0:
                        pe.wait_ge(finished, t + 1)
                    pe.wait_ge(copied, t * GROUPS + g + BUFS + 1)
                    for a in range(4 * g, min(T, 4 * g + 4)):
                        last = pe.matmul(sums[:, b, 0:D + 1], turned[:, g % BUFS, a % 4, :], value[:, a, :],
                                         start=a == 0, stop=a == T - 1)
                    last.then_inc(multiplied, 1)

            pe.wait_ge(oned, 1)
            score(0, 0)
            with pe.Fori(0, T // 2) as i:
                score(2 * i + 1, 1)
                total(2 * i, 0)
                score(2 * i + 2, 0)
                total(2 * i + 1, 1)
            total(T - 1, 0)

        @block.vector
        def _(dve):
            dve.sem_inc(masked, BUFS)
            dve.sem_inc(finished, 2)
            step = Order(dve, vstep)

            def mask(t, b):
                dve.wait_ge(flagged, t + 1)
                for n in range(CHUNKS):
                    dve.wait_ge(scored, t * CHUNKS + n + 1)
                    dve.sem_inc(k.passed, 1)
                    dve.tensor_tensor_reduce(out=probs[:, b, n * 512:n * 512 + width[n]], in0=scores[:, n % BUFS, 0:width[n]],
                                             in1=absent[:, b, n * 512:n * 512 + width[n]], scale=1.0, scalar=-3.0 * BIG,
                                             op0=ALU.add, op1=ALU.max, accum_out=tops[:, n:n + 1]).then_inc(masked, 1)
                dve.wait_ge(masked, (t + 1) * CHUNKS + BUFS)
                step.n = 0 if isinstance(t, int) else t * 6 - 4
                step(dve.tensor_reduce(top1[:], tops[:], AX.X, ALU.max))
                step(dve.tensor_scalar(top[:, b:b + 1], top1[:], -SCALE, None, ALU.mult))
                dve.sem_inc(topped, 1)

            def finish(t, b):
                dve.wait_ge(multiplied, (t + 1) * GROUPS + BUFS)
                step.n = t * 6 + (2 if isinstance(t, int) else 4)
                step(dve.tensor_scalar(inv[:], sums[:, b, D:D + 1], 1e-30, None, ALU.max))
                step(dve.reciprocal(inv[:], inv[:]))
                step(dve.scalar_tensor_tensor(tile_of(h, t), sums[:, b, 0:D], inv[:], tile_of(h, t), ALU.mult, ALU.add))
                step(dve.tensor_scalar(tile_of(h, t), tile_of(h, t), 0.0, None, ALU.max))
                dve.sem_inc(finished, 1)

            mask(0, 0)
            with dve.Fori(0, T // 2) as i:
                mask(2 * i + 1, 1)
                finish(2 * i, 0)
                mask(2 * i + 2, 0)
                finish(2 * i + 1, 1)
            finish(T - 1, 0)

        @block.scalar
        def _(act):
            act.sem_inc(copied, BUFS)

            def exp(t, b):
                act.wait_ge(topped, t + 1)
                act.activation(probs[:, b, :], probs[:, b, :], ACT.Exp, bias=top[:, b:b + 1], scale=SCALE).then_inc(exped, 1)

            def copy(t, b):
                for g in range(GROUPS):
                    n = min(4, T - 4 * g) * P
                    act.wait_ge(flipped, t * GROUPS + g + 1)
                    act.wait_ge(multiplied, t * GROUPS + before(g, GROUPS) + BUFS + 1)
                    act.copy(turned[:, g % BUFS, :, :].rearrange("p a q -> p (a q)")[:, 0:n],
                             flips[:, g % BUFS, 0:n]).then_inc(copied, 1)
            exp(0, 0)
            with act.Fori(0, T // 2) as i:
                copy(2 * i, 0)
                exp(2 * i + 1, 1)
                copy(2 * i + 1, 1)
                exp(2 * i + 2, 0)
            copy(T - 1, 0)



def score_by_edge(nc, k, name, table, width, node_rows, out_src, out_dst):
    dot = out_dst is None
    with ExitStack() as c:
        c.enter_context(nc.cleanup_on_exit())
        sb = lambda n, s, d=F32: c.enter_context(nc.sbuf_tensor(name + n, s, d))
        pb = lambda n, s: c.enter_context(nc.psum_tensor(name + n, s, F32))
        sem = lambda n: nc.alloc_semaphore(name + n)
        dcol = sb("dcol", [P, U])
        pick = sb("pick", [P, 2, G4, P])
        idx = sb("idx", [P, 2, 8], I32)
        got = sb("got", [P, U, width])
        prod = sb("prod", [P, width])
        score = sb("score", [P, U])
        wide = pb("wide", [P, 2, 512])
        expand = pb("expand", [P, 4, 512])
        copied, turned, picked = sem("copied"), sem("turned"), sem("picked")
        expanded, used, kept, indexed = sem("expanded"), sem("used"), sem("kept"), sem("indexed")
        arrived = [sem(f"arrived{n}") for n in range(U)]
        NG = U // G4
        HU = U // 2
        block = c.enter_context(nc.Block())

        def copy_indices(eng, i, h):
            eng.wait_ge(used, i * U + h * HU + 8 if dot else (i * 2 + h) * 2 + 2)
            eng.sem_inc(k.passed, 1)
            copy = eng.copy if dot else eng.tensor_copy
            copy(idx[:, h, :], cols(k.src_i, i * U + h * HU, HU)).then_inc(indexed, 1)

        @block.gpsimd
        def _(pool):
            with pool.Fori(0, IT) as i:
                for u in range(U):
                    if u % HU == 0:
                        pool.wait_ge(indexed, i * 2 + u // HU + 1)
                        pool.sem_inc(k.passed, 1)
                    pool.indirect_dma_start(got[:, u, :], None, table, bass.IndirectOffsetOnAxis(
                        ap=idx[:, u // HU, u % HU:u % HU + 1], axis=0)).then_inc(arrived[u], 16)

        @block.vector
        def _(dve):
            dve.sem_inc(picked, 2)
            if dot:
                dve.sem_inc(kept, 1)
            with dve.Fori(0, IT) as i:
                def use(u):
                    j = i * U + u
                    dve.wait_ge(expanded, j + 2)
                    dve.wait_ge(arrived[u], i * 16 + 16)
                    dve.wait_ge(used, j + 16)
                    dve.tensor_tensor_reduce(out=prod[:], in0=expand[:, u % 4, 0:width], in1=got[:, u, :],
                                             scale=1.0, scalar=0.0, op0=ALU.mult, op1=ALU.add,
                                             accum_out=score[:, u:u + 1]).then_inc(used, 1)

                dve.wait_ge(turned, i * NG + 4)
                dve.tensor_copy(dcol[:], cols(k.dst, i * U, U)).then_inc(copied, 1)
                for g in range(NG):
                    n = i * NG + g
                    if not dot and g % 2 == 0:
                        copy_indices(dve, i, g // 2)
                    dve.wait_ge(turned, n + 5)
                    if g >= 2:
                        dve.wait_ge(expanded, n * G4 - 3)
                    else:
                        dve.wait_ge(expanded, i * U + 1)
                    dve.tensor_tensor(pick[:, g % 2, :, :], wide[:, g % 2, :].rearrange("p (s q) -> p s q", s=G4),
                                      cols(k.node, i * U + g * G4, G4).unsqueeze(2).broadcast_to([P, G4, P]),
                                      ALU.is_equal).then_inc(picked, 1)
                    if dot and g > 0:
                        for u in range((g - 1) * G4, g * G4):
                            use(u)
                if dot:
                    for u in range((NG - 1) * G4, U):
                        use(u)
                    dve.wait_ge(used, i * U + U + 16)
                    dve.tensor_scalar(cols(out_src, i * U, U), score[:], 1.0 / float(np.sqrt(D)), None,
                                      ALU.mult).then_inc(kept, 1)
                    dve.wait_ge(kept, i + 2)

        @block.tensor
        def _(pe):
            pe.sem_inc(turned, 4)
            pe.sem_inc(expanded, 1)
            with pe.Fori(0, IT) as i:
                def turn(g):
                    n = i * NG + g
                    pe.wait_ge(picked, n + 1)
                    for s in range(G4):
                        u = g * G4 + s
                        last = pe.transpose(wide[:, g % 2, s * P:(s + 1) * P],
                                            dcol[:, u:u + 1].broadcast_to([P, P]), k.ident[:])
                    last.then_inc(turned, 1)

                pe.wait_ge(copied, i + 1)
                turn(0)
                for g in range(NG):
                    if g + 1 < NG:
                        turn(g + 1)
                    pe.wait_ge(picked, i * NG + g + 3)
                    for u in range(g * G4, (g + 1) * G4):
                        t = pe.value_load(k.slot_tile_i[0:1, bass.ds(i * U + u + 1, 1)], min_val=0, max_val=T - 1)
                        if dot:
                            pe.wait_ge(used, i * U + u + 13)
                            to = expand[:, u % 4, 0:width]
                        else:
                            if u % HU == 0:
                                pe.wait_ge(used, (i * 2 + u // HU) * 2 + 2)
                            to = expand[:, u // HU, (u % HU) * width:(u % HU + 1) * width]
                        pe.matmul(to, pick[:, g % 2, u % G4, :], tile_of(node_rows, t),
                                  start=True, stop=True).then_inc(expanded, 1)

        @block.scalar
        def _(act):
            if dot:
                act.sem_inc(used, 16)
                with act.Fori(0, IT) as i:
                    for h in range(2):
                        copy_indices(act, i, h)
            else:
                act.sem_inc(used, 4)
                with act.Fori(0, IT) as i:
                    for h in range(2):
                        act.wait_ge(expanded, i * U + (h + 1) * HU + 1)
                        for u in range(h * HU, (h + 1) * HU):
                            act.wait_ge(arrived[u], i * 16 + 16)
                        act.sem_inc(k.passed, 1)
                        act.copy(out_dst[:, bass.ds(i * U + h * HU, HU), :].rearrange("p s h -> p (s h)"),
                                 expand[:, h, 0:HU * width]).then_inc(used, 1)
                        act.copy(out_src[:, bass.ds(i * U + h * HU, HU), :].rearrange("p s h -> p (s h)"),
                                 got[:, h * HU:(h + 1) * HU, :].rearrange("p s h -> p (s h)")).then_inc(used, 1)


def segment_maximum(nc, k, name, heads, value, out):
    with ExitStack() as c:
        c.enter_context(nc.cleanup_on_exit())
        sb = lambda n, s, d=F32: c.enter_context(nc.sbuf_tensor(name + n, s, d))
        sem = lambda n: nc.alloc_semaphore(name + n)
        v = sb("v", [SQ, SG, heads, P])
        scan = [sb("scan", [SQ, SG, heads, P]), v]
        pen = sb("pen", [SQ, SG, heads, P])
        edge = sb("edge", [SQ, 2, SG, heads])
        whole = sb("whole", [SQ, 2, SG, heads])
        reset = sb("reset", [SQ, SG, P])
        reach = sb("reach", [SQ, 2, SG, P])
        one = sb("one", [SQ, 2, SG])
        line = sb("line", [heads, 2, S])
        lpen = sb("lpen", [heads, 2, S])
        carry = sb("carry", [heads, 2, S])
        carried = sb("carried", [SQ, 2, SG, heads])
        turns = c.enter_context(nc.psum_tensor(name + "turns", [P, 4, 512], F32))
        lines = c.enter_context(nc.psum_tensor(name + "lines", [P, 2, 512], F32))
        lines2 = c.enter_context(nc.psum_tensor(name + "lines2", [P, 2, 512], F32))
        turned, taken, vstep, ends, lined, carry_s, back, done = (
            sem("turned"), sem("taken"), sem("vstep"), sem("ends"), sem("lined"), sem("carry_s"),
            sem("back"), sem("done"))
        out_t, out_k, final = sem("out_t"), sem("out_k"), sem("final")
        block = c.enter_context(nc.Block())
        per_bank = 4

        @block.tensor
        def _(pe):
            for n in range(SG * heads):
                g, h = n // heads, n % heads
                if n >= 4:
                    pe.wait_ge(taken, n - 3)
                pe.transpose(turns[0:SQ, n % 4, 0:P], value[:, g * SQ:(g + 1) * SQ, h], k.ident[:]).then_inc(turned, 1)
            pe.wait_ge(ends, 1)
            for d in range(2):
                for g in range(SG):
                    pe.transpose(lines[0:heads, d, g * SQ:(g + 1) * SQ], edge[:, d, g, :], k.ident[0:SQ, 0:SQ])
                    last = pe.transpose(lines2[0:heads, d, g * SQ:(g + 1) * SQ], whole[:, d, g, :],
                                        k.ident[0:SQ, 0:SQ])
            last.then_inc(lined, 1)
            pe.wait_ge(carry_s, 1)
            for d in range(2):
                for g in range(SG):
                    last = pe.transpose(turns[0:SQ, 0, (d * SG + g) * heads:(d * SG + g + 1) * heads],
                                        carry[:, d, g * SQ:(g + 1) * SQ], k.ident[0:heads, 0:heads])
            last.then_inc(back, 1)
            pe.wait_ge(final, 1)
            for n in range(SG * heads):
                g, h = n // heads, n % heads
                if n >= 4:
                    pe.wait_ge(out_k, n - 3)
                pe.transpose(turns[:, n % 4, 0:SQ], scan[0][:, g, h, :], k.ident[0:SQ, 0:SQ]).then_inc(out_t, 1)

        @block.scalar
        def _(act):
            for n in range(SG * heads):
                g, h = n // heads, n % heads
                act.wait_ge(turned, n + 1)
                act.copy(v[:, g, h, :], turns[0:SQ, n % 4, 0:P]).then_inc(taken, 1)
            for n in range(SG * heads):
                g, h = n // heads, n % heads
                act.wait_ge(out_t, n + 1)
                act.copy(out[:, g * SQ:(g + 1) * SQ, h], turns[:, n % 4, 0:SQ]).then_inc(out_k, 1)
            act.wait_ge(out_k, SG * heads)

        @block.vector
        def _(dve):
            step = Order(dve, vstep)
            flat = lambda a: a.rearrange("q g p -> q (g p)")
            flat4 = lambda a: a.rearrange("q g h p -> q (g h p)")
            for d, links in enumerate((k.pen_prev, k.pen_next)):
                entry, leave = (0, P - 1) if d == 0 else (P - 1, 0)
                step(dve.memset(reset[:], 0.0))
                step(dve.memset(reset[:, :, entry:entry + 1], BIG))
                a, b, o = flat(reset[:]), flat(links[:]), flat(reach[:, d, :, :])
                if d:
                    a, b, o = a[:, ::-1], b[:, ::-1], o[:, ::-1]
                step(dve.tensor_tensor_scan(o, a, b, 0.0, ALU.add, ALU.min))
                step(dve.tensor_copy(whole[:, d, :, :], reach[:, d, :, leave:leave + 1].broadcast_to([SQ, SG, heads])))
            dve.wait_ge(taken, SG * heads)
            for d, links in enumerate((k.pen_prev, k.pen_next)):
                entry, leave = (0, P - 1) if d == 0 else (P - 1, 0)
                step(dve.tensor_copy(pen[:], links[:].unsqueeze(2).broadcast_to([SQ, SG, heads, P])))
                step(dve.memset(pen[:, :, :, entry:entry + 1], -BIG))
                a, b, o = flat4(pen[:]), flat4(v[:]), flat4(scan[d][:])
                if d:
                    a, b, o = a[:, ::-1], b[:, ::-1], o[:, ::-1]
                step(dve.tensor_tensor_scan(o, a, b, -BIG, ALU.add, ALU.max))
                step(dve.tensor_copy(edge[:, d, :, :], scan[d][:, :, :, leave:leave + 1].rearrange("q g h a -> q g (h a)")))
            dve.sem_inc(ends, 1)
            dve.wait_ge(lined, 1)
            step(dve.tensor_copy(line[:], lines[0:heads, :, 0:S]))
            step(dve.tensor_copy(lpen[:], lines2[0:heads, :, 0:S]))
            step(dve.memset(carry[:], -BIG))
            step(dve.tensor_tensor_scan(carry[:, 0, 1:S], lpen[:, 0, 0:S - 1], line[:, 0, 0:S - 1], -BIG,
                                        ALU.add, ALU.max))
            step(dve.tensor_tensor_scan(carry[:, 1, 0:S - 1][:, ::-1], lpen[:, 1, 1:S][:, ::-1],
                                        line[:, 1, 1:S][:, ::-1], -BIG, ALU.add, ALU.max))
            dve.sem_inc(carry_s, 1)
            dve.wait_ge(back, 1)
            step(dve.tensor_copy(carried[:].rearrange("q d g h -> q (d g h)"), turns[0:SQ, 0, 0:2 * SG * heads]))
            for d in range(2):
                for g in range(SG):
                    step(dve.tensor_tensor(pen[:, g, :, :], carried[:, d, g, :].unsqueeze(2).broadcast_to([SQ, heads, P]),
                                           reach[:, d, g, :].unsqueeze(1).broadcast_to([SQ, heads, P]), ALU.add))
                step(dve.tensor_tensor(flat4(scan[d][:]), flat4(scan[d][:]), flat4(pen[:]), ALU.max))
            step(dve.tensor_tensor(flat4(scan[0][:]), flat4(scan[0][:]), flat4(scan[1][:]), ALU.max))
            dve.sem_inc(final, 1)


def sum_by_destination(nc, k, name, table, index, weight=None, per_head=None):
    width = D + (H if per_head is not None else 0)
    IW = 8
    BLOCKS = S // IW
    with ExitStack() as c:
        c.enter_context(nc.cleanup_on_exit())
        sb = lambda n, s, d=F32: c.enter_context(nc.sbuf_tensor(name + n, s, d))
        sem = lambda n: nc.alloc_semaphore(name + n)
        idx = sb("idx", [P, 2, IW], I32)
        got = sb("got", [P, U, D])
        hot = sb("hot", [P, 8, P])
        part = sb("part", [P, 8, width]) if per_head is not None else None
        sums = c.enter_context(nc.psum_tensor(name + "sums", [P, 512], F32))
        arrived = [sem(f"arrived{n}") for n in range(U)]
        indexed, made, weighed, multiplied, full, copied = (
            sem("indexed"), sem("made"), sem("weighed"), sem("multiplied"), sem("full"), sem("copied"))
        block = c.enter_context(nc.Block())

        @block.gpsimd
        def _(pool):
            with pool.Fori(0, IT) as i:
                for u in range(U):
                    if u % IW == 0:
                        pool.wait_ge(indexed, i * (U // IW) + u // IW + 1)
                        pool.sem_inc(k.passed, 1)
                    pool.indirect_dma_start(got[:, u, :], None, table, bass.IndirectOffsetOnAxis(
                        ap=idx[:, u // IW, u % IW:u % IW + 1], axis=0)).then_inc(arrived[u], 16)

        @block.vector
        def _(dve):
            if per_head is not None:
                dve.sem_inc(weighed, U)
            with dve.Fori(0, IT) as i:
                for u in range(U):
                    j = i * U + u
                    if u % 4 == 0:
                        dve.wait_ge(multiplied, j + U - 4)
                    if weight is None:
                        ins = dve.tensor_scalar(hot[:, u % 8, :], k.iota[:], cols(k.dloc, j, 1), None, ALU.is_equal)
                    else:
                        ins = dve.tensor_scalar(hot[:, u % 8, :], k.iota[:], cols(k.dloc, j, 1), cols(weight, j, 1),
                                                ALU.is_equal, ALU.mult)
                    ins.then_inc(made, 1)
                    if per_head is not None:
                        w = per_head[:, bass.ds(j, 1), :].rearrange("p a h -> p (a h)")
                        dve.tensor_copy(part[:, u % 8, D:D + H], w).then_inc(made, 1)
                        dve.wait_ge(arrived[u], i * 16 + 16)
                        dve.tensor_tensor(part[:, u % 8, 0:D].rearrange("p (h f) -> p h f", h=H),
                                          got[:, u, :].rearrange("p (h f) -> p h f", h=H),
                                          w.unsqueeze(2).broadcast_to([P, H, HD]), ALU.mult).then_inc(weighed, 1)

        @block.tensor
        def _(pe):
            pe.sem_inc(multiplied, U)

            def zeros(start):
                return pe.matmul(sums[:, 0:width], k.zero_b[:, 0:P], k.zero_b[:, 0:width], start=start, stop=not start)

            def multiply(i, u):
                j = i * U + u
                if per_head is not None:
                    pe.wait_ge(made, 2 * j + 2)
                    pe.wait_ge(weighed, j + U + 1)
                    rows = part[:, u % 8, :]
                else:
                    pe.wait_ge(made, j + 1)
                    pe.wait_ge(arrived[u], i * 16 + 16)
                    rows = got[:, u, :]
                pe.matmul(sums[:, 0:width], hot[:, u % 8, :], rows, start=False, stop=False).then_inc(multiplied, 1)

            zeros(True)
            with pe.Fori(0, IT) as i:
                for g in range(U // 4):
                    turns = pe.value_load(k.group_turns_i[0:1, bass.ds(i * (U // 4) + g, 1)], min_val=0, max_val=4)
                    with pe.If(turns == 0):
                        for u in range(4 * g, 4 * g + 4):
                            multiply(i, u)
                    with pe.If(turns != 0):
                        for u in range(4 * g, 4 * g + 4):
                            j = i * U + u
                            first = pe.value_load(k.turns_i[0:1, bass.ds(j, 1)], min_val=0, max_val=1)
                            with pe.If(first != 0):
                                t = pe.value_load(k.slot_tile_i[0:1, bass.ds(j + 1, 1)], min_val=0, max_val=T - 1)
                                zeros(False).then_inc(full, 1)
                                pe.wait_ge(copied, t)
                                zeros(True)
                            multiply(i, u)
            zeros(False).then_inc(full, 1)

        @block.scalar
        def _(act):
            def indices(n, b):
                act.wait_ge(multiplied if per_head is None else weighed, n * IW + U - IW)
                act.sem_inc(k.passed, 1)
                act.copy(idx[:, b, :], cols(index, n * IW, IW)).then_inc(indexed, 1)

            def keep(t):
                act.wait_ge(full, t + 1)
                act.sem_inc(k.passed, 1)
                act.copy(k.acc[:, bass.ds(t, 1), 0:width].rearrange("p a f -> p (a f)"), sums[:, 0:width]).then_inc(copied, 1)

            def tiles(n):
                for g in range(IW // 4):
                    turns = act.value_load(k.group_turns_i[0:1, bass.ds(n * (IW // 4) + g, 1)], min_val=0, max_val=4)
                    with act.If(turns != 0):
                        for u in range(4 * g, 4 * g + 4):
                            first = act.value_load(k.turns_i[0:1, bass.ds(n * IW + u, 1)], min_val=0, max_val=1)
                            with act.If(first != 0):
                                keep(act.value_load(k.slot_tile_i[0:1, bass.ds(n * IW + u, 1)], min_val=0, max_val=T - 1))

            indices(0, 0)
            with act.Fori(0, BLOCKS // 2 - 1) as i:
                indices(2 * i + 1, 1)
                tiles(2 * i)
                indices(2 * i + 2, 0)
                tiles(2 * i + 1)
            indices(BLOCKS - 1, 1)
            tiles(BLOCKS - 2)
            tiles(BLOCKS - 1)
            keep(T - 1)
            act.wait_ge(copied, T)



def project(nc, k, name, sources, weights, width, steps, epilogue, stores=(), turned_weights=None):
    ns = len(sources)
    with ExitStack() as c:
        c.enter_context(nc.cleanup_on_exit())
        sb = lambda n, s, d=F32: c.enter_context(nc.sbuf_tensor(name + n, s, d))
        sem = lambda n: nc.alloc_semaphore(name + n)
        xs = sb("xs", [P, 2, ns, D])
        xt = sb("xt", [P, 2, ns * 2, P])
        flips = c.enter_context(nc.psum_tensor(name + "flips", [P, 2, 512], F32))
        nb = -(-width // 512)
        prods = c.enter_context(nc.psum_tensor(name + "prods", [P, 2, nb + (turned_weights is not None), 512], F32))
        staged, flipped, turned, multiplied, finished = (sem("staged"), sem("flipped"), sem("turned"),
                                                         sem("multiplied"), sem("finished"))
        vstep, stored = sem("vstep"), sem("stored")
        block = c.enter_context(nc.Block())

        @block.sync
        def _(sp):
            if stores:
                def store_all(t, b):
                    sp.wait_ge(finished, t + 3)
                    for src, dram in stores:
                        sp.dma_start(dram[bass.ds(t * P, P), :], src[:, bass.ds(t, 1), 0:D].rearrange(
                            "p a f -> p (a f)")).then_inc(stored, 16)
                over_tiles(sp, store_all)
                sp.wait_ge(stored, 16 * T * len(stores))

        @block.scalar
        def _(act):
            act.sem_inc(turned, 2)

            def stage(t, b):
                act.wait_ge(flipped, t + 1)
                act.sem_inc(k.passed, 1)
                for s, (src, column) in enumerate(sources):
                    if column is None:
                        ins = act.copy(xs[:, b, s, :], src[:, bass.ds(t, 1), 0:D].rearrange("p a f -> p (a f)"))
                    else:
                        ins = act.activation(xs[:, b, s, :], src[:, bass.ds(t, 1), 0:D].rearrange("p a f -> p (a f)"),
                                             ACT.Copy, scale=cols(column, t, 1))
                    ins.then_inc(staged, 1)

            def keep(t, b):
                act.wait_ge(flipped, t + 3)
                act.wait_ge(multiplied, t + 1)
                act.copy(xt[:, b, :, :].rearrange("p a q -> p (a q)"), flips[:, b, 0:ns * D]).then_inc(turned, 1)

            stage(0, 0)
            with act.Fori(0, T // 2) as i:
                stage(2 * i + 1, 1)
                keep(2 * i, 0)
                stage(2 * i + 2, 0)
                keep(2 * i + 1, 1)
            keep(T - 1, 0)

        @block.tensor
        def _(pe):
            pe.sem_inc(flipped, 2)
            pe.sem_inc(multiplied, 2)

            def flip(t, b):
                pe.wait_ge(turned, t + 1)
                pe.wait_ge(staged, (t + 1) * ns)
                for s in range(ns):
                    for h in range(2):
                        last = pe.transpose(flips[:, b, s * D + h * P:s * D + (h + 1) * P],
                                            xs[:, b, s, h * P:(h + 1) * P], k.ident[:])
                last.then_inc(flipped, 1)

            def multiply(t, b):
                pe.wait_ge(turned, t + 3)
                pe.wait_ge(finished, t + 1)
                for o in range(nb):
                    w = min(512, width - o * 512)
                    for s in range(ns * 2):
                        last = pe.matmul(prods[:, b, o, 0:w], xt[:, b, s, :], weights[:, s, o * 512:o * 512 + w],
                                         start=s == 0, stop=s == ns * 2 - 1)
                if turned_weights is not None:
                    for o in range(4):
                        for s in range(2):
                            last = pe.matmul(prods[:, b, nb, o * P:(o + 1) * P], turned_weights[:, s, o * P:(o + 1) * P],
                                             xt[:, b, s, :], start=s == 0, stop=s == 1)
                last.then_inc(multiplied, 1)

            flip(0, 0)
            with pe.Fori(0, T // 2) as i:
                flip(2 * i + 1, 1)
                multiply(2 * i, 0)
                flip(2 * i + 2, 0)
                multiply(2 * i + 1, 1)
            multiply(T - 1, 0)

        @block.vector
        def _(dve):
            dve.sem_inc(finished, 2)
            step = Order(dve, vstep)

            def work(t, b):
                dve.wait_ge(multiplied, t + 3)
                step.n = t * steps
                epilogue(dve, step, t, prods[:, b, :, :].rearrange("p a n -> p (a n)"))
                dve.sem_inc(finished, 1)
            over_tiles(dve, work)


def refine_root(dve, step, root, a, square):
    step(dve.reciprocal(root, root))
    step(dve.tensor_tensor(square, root, root, ALU.mult))
    step(dve.tensor_tensor(square, square, a, ALU.mult))
    step(dve.tensor_scalar(square, square, -0.5, 1.5, ALU.mult, ALU.add))
    step(dve.tensor_tensor(root, root, square, ALU.mult))


def normalize(nc, k, name, r, x, out=None, before=None):
    TOGETHER = 5
    with ExitStack() as c:
        c.enter_context(nc.cleanup_on_exit())
        sem = lambda n: nc.alloc_semaphore(name + n)
        given, square = (c.enter_context(nc.sbuf_tensor(name + n, [P, T], F32)) for n in ("given", "square"))
        six = c.enter_context(nc.sbuf_tensor(name + "six", [P, TOGETHER, 6], F32))
        two = c.enter_context(nc.sbuf_tensor(name + "two", [P, TOGETHER, 2], F32))
        vstep, rooted, stored, finished, safe = (sem("vstep"), sem("rooted"), sem("stored"), sem("finished"), sem("safe"))
        block = c.enter_context(nc.Block())

        @block.vector
        def _(dve):
            step = Order(dve, vstep)
            if before is not None:
                before(dve, step)
            base, each = step.n, 2 * TOGETHER + 1
            with dve.Fori(0, T // TOGETHER) as i:
                for m in range(TOGETHER):
                    dve.bn_stats(six[:, m, :], tile_of(r, i * TOGETHER + m)).then_inc(vstep, 1)
                dve.wait_ge(vstep, base + i * each + TOGETHER)
                dve.sem_inc(k.passed, 1)
                for m in range(TOGETHER):
                    dve.bn_aggr(two[:, m, :], six[:, m, :]).then_inc(vstep, 1)
                dve.wait_ge(vstep, base + i * each + 2 * TOGETHER)
                dve.tensor_copy(k.mv[:, bass.ds(i * TOGETHER, TOGETHER), :], two[:]).then_inc(vstep, 1)
                dve.wait_ge(vstep, base + i * each + each)
                dve.sem_inc(k.passed, 1)
            step.n = base + each * (T // TOGETHER)
            step(dve.tensor_scalar(given[:], k.mv[:, :, 1], LN_EPS, None, ALU.add))
            dve.sem_inc(safe, 1)
            dve.wait_ge(rooted, 1)
            refine_root(dve, step, k.rstd[:], given[:], square[:])

            def one(t, b):
                dve.tensor_scalar(tile_of(x, t), tile_of(r, t), k.mv[:, bass.ds(t, 1), 0:1].rearrange("p a f -> p (a f)"),
                                  cols(k.rstd, t, 1), ALU.subtract, ALU.mult).then_inc(finished, 1)
            over_tiles(dve, one)
            dve.wait_ge(finished, T)

        @block.scalar
        def _(act):
            act.wait_ge(safe, 1)
            act.activation(k.rstd[:], given[:], ACT.Sqrt).then_inc(rooted, 1)

        @block.sync
        def _(sp):
            if out is not None:
                with sp.Fori(0, T - 1) as t:
                    sp.wait_ge(finished, t + 1)
                    sp.dma_start(out[bass.ds(t * P, P), :], tile_of(x, t)).then_inc(stored, 16)
                sp.wait_ge(finished, T)
                sp.dma_start(out[(T - 1) * P:N, :], x[0:NLAST, T - 1, :]).then_inc(stored, 16)
                sp.wait_ge(stored, 16 * T)


def load(nc, name, pairs):
    with ExitStack() as c:
        c.enter_context(nc.cleanup_on_exit())
        loaded = nc.alloc_semaphore(name + "loaded")
        block = c.enter_context(nc.Block())

        @block.sync
        def _(sp):
            for to, src, *scattered in pairs:
                sp.dma_start(to, src, allow_slow_non_contiguous=bool(scattered)).then_inc(loaded, 16)
            sp.wait_ge(loaded, 16 * len(pairs))


def halves(w):
    return w.rearrange("(a p) n -> p a n", p=P)


def attention_weights(nc, k, name, value, other, best, heads):
    with ExitStack() as c:
        c.enter_context(nc.cleanup_on_exit())
        sem = lambda n: nc.alloc_semaphore(name + n)
        vstep, ready, done = sem("vstep"), sem("ready"), sem("done")
        block = c.enter_context(nc.Block())
        flat = lambda a: a.rearrange("p s h -> p (s h)")
        v, b = flat(value[:]), flat(best[:])

        @block.vector
        def _(dve):
            step = Order(dve, vstep)
            if other is not None:
                o = flat(other[:])
                for a in (v, b):
                    step(dve.tensor_tensor(a, a, o, ALU.add))
                    step(dve.scalar_tensor_tensor(a, a, 0.2, a, ALU.mult, ALU.max))
            step(dve.tensor_tensor(v, v, b, ALU.subtract))
            dve.sem_inc(ready, 1)

        @block.scalar
        def _(act):
            act.wait_ge(ready, 1)
            act.activation(v, v, ACT.Exp).then_inc(done, 1)
            act.wait_ge(done, 1)


def graph_layers(nc, x, src, dst, edge_type_16, edge_weight1, L0_gnn_W, L0_gnn_b, L1_gnn_W_lin, L1_gnn_b_lin,
                 L1_gnn_W_gat, L1_gnn_attn_l, L1_gnn_attn_r, L1_gnn_gat_bias, L2_gnn_Wq, L2_gnn_bq, L2_gnn_Wk,
                 L2_gnn_bk, L2_gnn_Wv, L2_gnn_bv, L2_gnn_Ws, L2_gnn_bs, L2_gnn_Wl, L2_gnn_bl, L2_gnn_Wr,
                 L2_gnn_gamma, L2_gnn_beta, L2_gnn_alpha_res, L3_gnn_weight, out, debug=None):
    k = Bag()
    dram = lambda n, s, d=F32: nc.dram_tensor(n, s, d).ap()
    k.ordered = [dram(f"ordered{n}", (E + SE,), I32) for n in range(4)]
    k.slots = [dram(f"slots{n}", (2 * SE + 2 * P,), I32) for n in range(4)]
    pairs_d, turned_d = dram("pairs_d", (NP, NP)), dram("turned_d", (NP, NP))
    feat_d = dram("feat_d", (NP, D))
    el_d = dram("el_d", (NP, H))
    query_d = dram("query_d", (P, 2, NP))
    rel_d = dram("rel_d", (R, NP, D))

    with ExitStack() as c:
        sb = lambda n, s, d=F32: c.enter_context(nc.sbuf_tensor(n, s, d))
        k.passed = nc.alloc_semaphore("passed")
        k.X = sb("X", [P, T, D])
        k.iota = sb("iota", [P, P])
        k.ident = sb("ident", [P, P])
        k.low = sb("low", [P, P])
        k.pcol = sb("pcol", [P, 1])
        k.ones = sb("ones", [P, P])
        k.zero = sb("zero", [P, D + H])
        k.starts = sb("starts", [1, 2 * T + 1], I32)
        k.slot_tile = sb("slot_tile", [P, S + 1])
        k.slot_tile_i = sb("slot_tile_i", [1, S + 1], I32)
        k.turns_i, k.group_turns_i = sb("turns_i", [1, S], I32), sb("group_turns_i", [1, S // 4], I32)
        k.deg_src, k.deg_dst = sb("deg_src", [P, T]), sb("deg_dst", [P, T])
        k.iota_b, k.zero_b = sb("iota_b", [P, P], BF16), sb("zero_b", [P, D + H], BF16)
        k.edge_pad = sb("edge_pad", [1, P], I32)
        k.src, k.dst, k.rel, k.weight, k.node, k.dloc = (
            sb(n, [P, S]) for n in ("src", "dst", "rel", "weight", "node", "dloc"))
        k.src_i, k.rel_i = sb("src_i", [P, S], I32), sb("rel_i", [P, S], I32)
        k.rows_dst, k.rows_w, k.pen_prev, k.pen_next = (
            sb(n, [SQ, SG, P]) for n in ("rows_dst", "rows_w", "pen_prev", "pen_next"))
        k.mv = sb("mv", [P, T, 2])
        k.rstd = sb("rstd", [P, T])
        col = sb("col", [P, T])

        with ExitStack() as l:
            k.slo, k.shi = (l.enter_context(nc.sbuf_tensor(n, [EP, EC], F32)) for n in ("slo", "shi"))
            prepare(nc, k, x, src, dst)
            order_edges(nc, k, [src, dst, edge_type_16, edge_weight1.rearrange("e a -> (e a)").bitcast(I32)], dst)
            fill_slots(nc, k)
        count_pairs(nc, k, pairs_d)

        with ExitStack() as l:
            sl = lambda n, s, d=F32: l.enter_context(nc.sbuf_tensor(n, s, d))
            w, b = sl("w0", [P, 2, D]), sl("b0", [P, D])
            load(nc, "l0", [(w[:], halves(L0_gnn_W)), (b[:], spread(L0_gnn_b))])
            inverse_root(nc, k, col)
            r = sl("r0", [P, T, D])
            scale_tiles(nc, r, k.X, col)
            if debug: debug(nc, 'y', r)
            agg = sl("agg0", [P, T, D])
            dense_product(nc, k, "d0", pairs_d, r, agg, col, turned_d)
            z = sl("z0", [P, D])

            def epilogue(dve, step, t, p):
                step(dve.tensor_tensor(z[:], p[:, 0:D], b[:], ALU.add))
                step(dve.scalar_tensor_tensor(z[:], z[:], 0.2, z[:], ALU.mult, ALU.max))
                step(dve.tensor_tensor(tile_of(r, t), tile_of(k.X, t), z[:], ALU.add))
            project(nc, k, "p0", [(agg, None)], w, D, 3, epilogue)
            normalize(nc, k, "n0", r, k.X)
            if debug: debug(nc, 'x1', k.X)

        with ExitStack() as l:
            sl = lambda n, s, d=F32: l.enter_context(nc.sbuf_tensor(n, s, d))
            h = sl("h1", [P, T, D])
            er = sl("er", [P, T, H])
            scores = sl("scores", [P, S, H])
            w, w2 = sl("w1", [P, 2, D]), sl("w1g", [P, 2, D])
            b, al, ar, gb = (sl(n, [P, D]) for n in ("b1", "al", "ar", "gb"))
            z = sl("z1", [P, D])
            load(nc, "l1", [(w[:], halves(L1_gnn_W_lin)), (w2[:], halves(L1_gnn_W_gat)), (b[:], spread(L1_gnn_b_lin)),
                            (al[:], spread(L1_gnn_attn_l.rearrange("h f -> (h f)"))),
                            (ar[:], spread(L1_gnn_attn_r.rearrange("h f -> (h f)"))),
                            (gb[:], spread(L1_gnn_gat_bias))])
            project(nc, k, "p1", [(k.X, None)], w, D, 1,
                    lambda dve, step, t, p: step(dve.tensor_tensor(tile_of(h, t), p[:, 0:D], b[:], ALU.add)))
            with ExitStack() as f:
                feat = f.enter_context(nc.sbuf_tensor("feat", [P, T, D], F32))
                el = f.enter_context(nc.sbuf_tensor("el", [P, T, H], F32))

                def epilogue(dve, step, t, p):
                    step(dve.tensor_copy(tile_of(feat, t), p[:, 0:D]))
                    step(dve.tensor_tensor(tile_of(h, t), tile_of(h, t), tile_of(k.X, t), ALU.add))
                    for a, to in ((al, el), (ar, er)):
                        step(dve.tensor_tensor(z[:], tile_of(feat, t), a[:], ALU.mult))
                        step(dve.tensor_reduce(tile_of(to, t), z[:].rearrange("p (h f) -> p h f", h=H), AX.X, ALU.add))
                project(nc, k, "p2", [(h, None)], w2, D, 6, epilogue, stores=[(feat, feat_d)])
                load(nc, "s2", [(el_d.rearrange("(t p) h -> p t h", p=P), el[:])])
            with ExitStack() as f:
                part = f.enter_context(nc.sbuf_tensor("er_edge", [P, S, H], F32))
                score_by_edge(nc, k, "a1", el_d, H, er, scores, part)
                best = f.enter_context(nc.sbuf_tensor("best", [P, S, H], F32))
                segment_maximum(nc, k, "m1", H, scores, best)
                attention_weights(nc, k, "w1", scores, part, best, H)
            with ExitStack() as f:
                k.acc = f.enter_context(nc.sbuf_tensor("acc1", [P, T, D + H], F32))
                sum_by_destination(nc, k, "e1", feat_d, k.src_i, per_head=scores)
                rs = f.enter_context(nc.sbuf_tensor("rs1", [P, T, H], F32))

                def before(dve, step):
                    step(dve.tensor_scalar(rs[:], k.acc[:, :, D:D + H], 1e-30, None, ALU.max))
                    step(dve.reciprocal(rs[:], rs[:]))
                    a = k.acc[:, :, 0:D]
                    for m in range(H):
                        dve.tensor_tensor(k.acc[:, :, m * HD:(m + 1) * HD], k.acc[:, :, m * HD:(m + 1) * HD],
                                          rs[:, :, m:m + 1].broadcast_to([P, T, HD]), ALU.mult).then_inc(step.sem, 1)
                    step.n = step.n + H
                    dve.wait_ge(step.sem, step.n)
                    step(dve.tensor_tensor(a, a, gb[:].unsqueeze(1).broadcast_to([P, T, D]), ALU.add))
                    step(dve.scalar_tensor_tensor(a, a, 0.01, a, ALU.mult, ALU.max))
                    step(dve.tensor_tensor(h[:], h[:], a, ALU.add))
                normalize(nc, k, "n1", h, k.X, before=before)
            if debug: debug(nc, 'x2', k.X)

        with ExitStack() as l:
            sl = lambda n, s, d=F32: l.enter_context(nc.sbuf_tensor(n, s, d))
            h = sl("h2", [P, T, D])
            with ExitStack() as f:
                sf = lambda n, s: f.enter_context(nc.sbuf_tensor(n, s, F32))
                key_t, value = sf("key_t", [P, 2, NP]), sf("value", [P, T, D + 1])
                with ExitStack() as g:
                    sg = lambda n, s: g.enter_context(nc.sbuf_tensor(n, s, F32))
                    query_t = sg("query_t", [P, 2, NP])
                    wqk, wvs = sg("wqk", [P, 2, 2 * D]), sg("wvs", [P, 2, 2 * D])
                    bqk, bvs = sg("bqk", [P, 4]), sg("bvs", [P, 2 * D])
                    by_half = lambda v: v.rearrange("(a p) -> p a", p=P)
                    load(nc, "l3", [(wqk[:, :, 0:D], halves(L2_gnn_Wq)), (wqk[:, :, D:2 * D], halves(L2_gnn_Wk)),
                                    (wvs[:, :, 0:D], halves(L2_gnn_Wv)), (wvs[:, :, D:2 * D], halves(L2_gnn_Ws)),
                                    (bqk[:, 0:2], by_half(L2_gnn_bq), 1), (bqk[:, 2:4], by_half(L2_gnn_bk), 1),
                                    (bvs[:, 0:D], spread(L2_gnn_bv)), (bvs[:, D:2 * D], spread(L2_gnn_bs))])

                    def epilogue(dve, step, t, p):
                        step(dve.tensor_tensor(value[:, bass.ds(t, 1), 0:D].rearrange("p a f -> p (a f)"), p[:, 0:D],
                                               bvs[:, 0:D], ALU.add))
                        step(dve.tensor_tensor(tile_of(h, t), p[:, D:2 * D], bvs[:, D:2 * D], ALU.add))
                        for o in range(4):
                            step(dve.tensor_scalar((query_t, key_t)[o // 2][:, o % 2, bass.ds(t * P, P)],
                                                   p[:, 512 + o * P:512 + (o + 1) * P], bqk[:, o:o + 1], None, ALU.add))
                    project(nc, k, "p3", [(k.X, None)], wvs, 2 * D, 6, epilogue, turned_weights=wqk)
                    load(nc, "s3", [(query_d, query_t[:])])
                dense_attention(nc, k, query_d, key_t, value, pairs_d, h)
            if debug: debug(nc, 'h0', h)
            z = sl("z2", [P, D])
            sage = [[sl(f"{n}{i}", [P, D]) for n in ("ga", "be", "bl")] for i in range(3)]
            wlr = [sl(f"wlr{i}", [P, 4, D]) for i in range(3)]
            alpha = sl("alpha", [P, 2])
            load(nc, "l2", [(alpha[:, 0:1], spread(L2_gnn_alpha_res))]
                 + [p for i in range(3) for p in (
                     (sage[i][0][:], spread(L2_gnn_gamma[i, :])), (sage[i][1][:], spread(L2_gnn_beta[i, :])),
                     (sage[i][2][:], spread(L2_gnn_bl[i, :])), (wlr[i][:, 0:2, :], halves(L2_gnn_Wl[i, :, :])),
                     (wlr[i][:, 2:4, :], halves(L2_gnn_Wr[i, :, :])))])
            k.acc = sl("acc2", [P, T, D])
            fold_scales(nc, alpha, sage)
            inverse_count(nc, k, col)
            for i in range(3):
                dense_product(nc, k, f"d{1 + i}", turned_d, h, k.acc, col)
                ga, be, _ = sage[i]

                def epilogue(dve, step, t, p, ga=ga, be=be, last=i == 2):
                    step(dve.tensor_tensor(z[:], p[:, 0:D], ga[:], ALU.mult))
                    step(dve.tensor_tensor(z[:], z[:], be[:], ALU.add))
                    step(dve.scalar_tensor_tensor(z[:], tile_of(h, t), alpha[:, 1:2], z[:], ALU.mult, ALU.add))
                    if last:
                        step(dve.scalar_tensor_tensor(tile_of(h, t), z[:], 0.0, tile_of(k.X, t), ALU.max, ALU.add))
                    else:
                        step(dve.tensor_scalar(tile_of(h, t), z[:], 0.0, None, ALU.max))
                project(nc, k, f"p{4 + i}", [(k.acc, None), (h, None)], wlr[i], D, 4, epilogue)
            normalize(nc, k, "n2", h, k.X)
            if debug: debug(nc, 'x3', k.X)

        with ExitStack() as l:
            sl = lambda n, s, d=F32: l.enter_context(nc.sbuf_tensor(n, s, d))
            with ExitStack() as f:
                w = f.enter_context(nc.sbuf_tensor("w3", [P, 2, R, D], F32))
                load(nc, "l4", [(w[:, a, :, :], L3_gnn_weight[:, a * P:(a + 1) * P, :].rearrange("r p n -> p r n"))
                                for a in range(2)])
                relation_tables(nc, k, w, rel_d)
            k.acc = sl("acc3", [P, T, D])
            sum_by_destination(nc, k, "e7", rel_d.rearrange("r n f -> (r n) f"), k.rel_i, weight=k.weight)

            normalize(nc, k, "n3", k.acc, k.X, out,
                      before=lambda dve, step: step(dve.tensor_tensor(k.acc[:], k.acc[:], k.X[:], ALU.add)))


def inverse_root(nc, k, col):
    with ExitStack() as c:
        c.enter_context(nc.cleanup_on_exit())
        vstep, rooted = nc.alloc_semaphore("r_v"), nc.alloc_semaphore("r_r")
        safe, given, square = (c.enter_context(nc.sbuf_tensor(n, [P, T], F32)) for n in ("safe", "given", "square"))
        block = c.enter_context(nc.Block())

        @block.vector
        def _(dve):
            step = Order(dve, vstep)
            step(dve.tensor_scalar(given[:], k.deg_src[:], 1.0, None, ALU.max))
            dve.wait_ge(rooted, 1)
            refine_root(dve, step, safe[:], given[:], square[:])
            step(dve.tensor_scalar(col[:], k.deg_src[:], 1.0, None, ALU.min))
            step(dve.tensor_tensor(col[:], col[:], safe[:], ALU.mult))

        @block.scalar
        def _(act):
            act.wait_ge(vstep, 1)
            act.activation(safe[:], given[:], ACT.Sqrt).then_inc(rooted, 1)


def inverse_count(nc, k, col):
    with ExitStack() as c:
        c.enter_context(nc.cleanup_on_exit())
        vstep = nc.alloc_semaphore("c_v")
        block = c.enter_context(nc.Block())

        @block.vector
        def _(dve):
            step = Order(dve, vstep)
            step(dve.tensor_scalar(col[:], k.deg_dst[:], 1.0, None, ALU.max))
            step(dve.reciprocal(col[:], col[:]))


def fold_scales(nc, alpha, sage):
    with ExitStack() as c:
        c.enter_context(nc.cleanup_on_exit())
        vstep, sig = nc.alloc_semaphore("f_v"), nc.alloc_semaphore("f_s")
        block = c.enter_context(nc.Block())

        @block.scalar
        def _(act):
            act.activation(alpha[:, 0:1], alpha[:, 0:1], ACT.Sigmoid).then_inc(sig, 1)

        @block.vector
        def _(dve):
            step = Order(dve, vstep)
            dve.wait_ge(sig, 1)
            step(dve.tensor_scalar(alpha[:, 1:2], alpha[:, 0:1], -1.0, 1.0, ALU.mult, ALU.add))
            for ga, be, bl in sage:
                step(dve.tensor_scalar(ga[:], ga[:], BN_SCALE, alpha[:, 0:1], ALU.mult, ALU.mult))
                step(dve.tensor_scalar(be[:], be[:], alpha[:, 0:1], None, ALU.mult))
                step(dve.tensor_tensor(bl[:], bl[:], ga[:], ALU.mult))
                step(dve.tensor_tensor(be[:], be[:], bl[:], ALU.add))


def scale_tiles(nc, to, x, col):
    with ExitStack() as c:
        c.enter_context(nc.cleanup_on_exit())
        done = nc.alloc_semaphore("sc_done")
        block = c.enter_context(nc.Block())

        @block.vector
        def _(dve):
            over_tiles(dve, lambda t, b: dve.tensor_scalar(tile_of(to, t), tile_of(x, t), cols(col, t, 1), None,
                                                           ALU.mult).then_inc(done, 1))
            dve.wait_ge(done, T)


def relation_tables(nc, k, w, rel_d):
    RP = R // 2
    with ExitStack() as c:
        c.enter_context(nc.cleanup_on_exit())
        sb = lambda n, s, d=F32: c.enter_context(nc.sbuf_tensor("q_" + n, s, d))
        sem = lambda n: nc.alloc_semaphore("q_" + n)
        xs = sb("xs", [P, 2, D])
        xt = sb("xt", [P, 2, 2, P])
        rows = sb("rows", [P, 2, R, D])
        flips = c.enter_context(nc.psum_tensor("q_flips", [P, 2, 512], F32))
        prods = c.enter_context(nc.psum_tensor("q_prods", [P, 4, 512], F32))
        staged, flipped, turned, multiplied, kept_a, kept_v = (
            sem("staged"), sem("flipped"), sem("turned"), sem("multiplied"), sem("kept_a"), sem("kept_v"))
        stored = [sem(f"stored{b}") for b in range(2)]
        block = c.enter_context(nc.Block())

        @block.sync
        def _(sp):
            def store(t, b):
                sp.wait_ge(kept_a, t * (RP // 2) + RP // 2 + 2)
                sp.wait_ge(kept_v, t * (RP // 2) + RP // 2 + 2)
                sp.dma_start(rel_d[:, bass.ds(t * P, P), :].rearrange("r p f -> p r f"), rows[:, b, :, :]).then_inc(stored[b], 16)
            over_tiles(sp, store)
            sp.wait_ge(stored[0], 16 * (T // 2 + 1))
            sp.wait_ge(stored[1], 16 * (T // 2))

        @block.tensor
        def _(pe):
            pe.sem_inc(flipped, 2)

            def tile(t, b):
                pe.wait_ge(staged, t + 1)
                pe.wait_ge(turned, t + 1)
                for h in range(2):
                    last = pe.transpose(flips[:, b, h * P:(h + 1) * P], xs[:, b, h * P:(h + 1) * P], k.ident[:])
                last.then_inc(flipped, 1)
                pe.wait_ge(turned, t + 3)
                for o in range(RP):
                    pe.wait_ge(kept_a if o % 2 == 0 else kept_v, t * (RP // 2) + o // 2 + 1)
                    for a in range(2):
                        last = pe.matmul(prods[:, o % 4, :], xt[:, b, a, :],
                                         w[:, a, 2 * o:2 * o + 2, :].rearrange("p r n -> p (r n)"),
                                         start=a == 0, stop=a == 1)
                    last.then_inc(multiplied, 1)
            over_tiles(pe, tile)

        @block.scalar
        def _(act):
            act.sem_inc(turned, 2)
            act.sem_inc(kept_a, 2)

            def stage(t, b):
                act.wait_ge(flipped, t + 1)
                act.sem_inc(k.passed, 1)
                act.copy(xs[:, b, :], tile_of(k.X, t)).then_inc(staged, 1)

            def tile(t, b):
                act.wait_ge(flipped, t + 3)
                act.copy(xt[:, b, :, :].rearrange("p a q -> p (a q)"), flips[:, b, 0:D]).then_inc(turned, 1)
                if reused(t):
                    act.wait_ge(stored[b], (t - b) * 8)
                for o in range(0, RP, 2):
                    act.wait_ge(multiplied, t * RP + o + 1)
                    act.copy(rows[:, b, 2 * o:2 * o + 2, :].rearrange("p r n -> p (r n)"),
                             prods[:, o % 4, :]).then_inc(kept_a, 1)
            stage(0, 0)
            stage(1, 1)
            tile(0, 0)
            stage(2, 0)
            tile(1, 1)
            with act.Fori(1, T // 2) as i:
                stage(2 * i + 1, 1)
                tile(2 * i, 0)
                stage(2 * i + 2, 0)
                tile(2 * i + 1, 1)
            tile(T - 1, 0)

        @block.vector
        def _(dve):
            dve.sem_inc(kept_v, 2)

            def tile(t, b):
                if reused(t):
                    dve.wait_ge(stored[b], (t - b) * 8)
                for o in range(1, RP, 2):
                    dve.wait_ge(multiplied, t * RP + o + 1)
                    dve.tensor_copy(rows[:, b, 2 * o:2 * o + 2, :].rearrange("p r n -> p (r n)"),
                                    prods[:, o % 4, :]).then_inc(kept_v, 1)
            over_tiles_after_two(dve, tile)


_INS = ['x', 'src', 'dst', 'edge_type_16', 'edge_weight1', 'L0_gnn_W', 'L0_gnn_b', 'L1_gnn_W_lin', 'L1_gnn_b_lin',
        'L1_gnn_W_gat', 'L1_gnn_attn_l', 'L1_gnn_attn_r', 'L1_gnn_gat_bias', 'L2_gnn_Wq', 'L2_gnn_bq', 'L2_gnn_Wk',
        'L2_gnn_bk', 'L2_gnn_Wv', 'L2_gnn_bv', 'L2_gnn_Ws', 'L2_gnn_bs', 'L2_gnn_Wl', 'L2_gnn_bl', 'L2_gnn_Wr',
        'L2_gnn_gamma', 'L2_gnn_beta', 'L2_gnn_alpha_res', 'L3_gnn_weight']


def kernel(**inputs):
    import concourse.bacc as _bacc
    from concourse.bass_utils import run_bass_kernel_spmd as _run

    nc = _bacc.Bacc("TRN2", target_bir_lowering=False, num_devices=1)
    arrays, args = {}, {}
    for name in _INS:
        a = np.ascontiguousarray(inputs[name])
        if a.ndim == 0:
            a = a.reshape(1)
        arrays[f"in_{name}"] = a
        args[name] = nc.dram_tensor(f"in_{name}", a.shape, mybir.dt.from_np(a.dtype), kind="ExternalInput").ap()
    out = nc.dram_tensor("out_0", (N, D), F32, kind="ExternalOutput").ap()
    graph_layers(nc, out=out, **args)
    r = _run(nc, [arrays], core_ids=[0])
    return r.results[0]["out_0"]
```
